# Optimizing a Trainium2 kernel written in Bass

```python
import numpy as np
import jax
import jax.numpy as jnp

def _softmax(x, axis=-1):
    return jax.nn.softmax(x, axis=axis)

def _gelu(x):
    return jax.nn.gelu(x, approximate=True)

def _silu(x):
    return jax.nn.silu(x)

def _sigmoid(x):
    return jax.nn.sigmoid(x)

def _layernorm(x, axis=-1, eps=1e-05):
    m = jnp.mean(x, axis=axis, keepdims=True)
    v = jnp.var(x, axis=axis, keepdims=True)
    return (x - m) / jnp.sqrt(v + eps)

def _scatter_add(tgt, idx, src, axis=0):
    return tgt.at[idx].add(src)

def _segment_sum(src, seg, n):
    return jax.ops.segment_sum(src, seg, n)
kernel_name = 'mk_seq_preln_d1_jaxref_r8_34bab7'

def setup_inputs(seed: int=0):
    np.random.seed(seed)
    _w = jnp.asarray

    def _L0_attn_setup():
        import jax, jax.numpy as jnp
        import numpy as np
        B, L, D, N = (8, 128, 128, 32)
        DT_MIN, DT_MAX = (0.001, 0.1)
        key = jax.random.key(seed)
        ks = jax.random.split(key, 12)
        s = 1.0 / np.sqrt(D)
        inp = {'x': jax.random.normal(ks[0], (B, L, D), jnp.float32), 'in_W': jax.random.uniform(ks[1], (D, D), jnp.float32, -s, s), 'in_b': jax.random.uniform(ks[2], (D,), jnp.float32, -s, s), 'log_dt': (np.log(DT_MIN) + jax.random.uniform(ks[3], (D,), jnp.float32) * (np.log(DT_MAX) - np.log(DT_MIN))).astype(jnp.float32), 'C': jax.random.normal(ks[4], (D, N, 2), jnp.float32), 'log_A_real': jnp.log(0.5 * jnp.ones((D, N), jnp.float32)), 'A_imag': jnp.tile((np.pi * jnp.arange(N, dtype=np.float32))[None, :], (D, 1)), 'D_skip': jax.random.normal(ks[5], (D,), jnp.float32), 'glu_W': jax.random.uniform(ks[6], (2 * D, D), jnp.float32, -s, s), 'glu_b': jax.random.uniform(ks[7], (2 * D,), jnp.float32, -s, s), 'out_W': jax.random.uniform(ks[8], (D, D), jnp.float32, -s, s), 'out_b': jax.random.uniform(ks[9], (D,), jnp.float32, -s, s)}
        return inp
    _L0_attn_in = _L0_attn_setup()

    def _L0_ffn_setup():
        import jax, jax.numpy as jnp
        import numpy as np
        D_MODEL = 128
        HIDDEN = 256
        E_ROUTED = 14
        E_SHARED = 2
        TOP_K = 2
        EPS = 1e-09
        RMS_EPS = 1.1920929e-07

        def _ffn(xn, rw, W1, W2):
            ms = jnp.mean(xn * xn, axis=-1, keepdims=True)
            h = xn * jax.lax.rsqrt(ms + RMS_EPS) * rw
            return jax.nn.silu(h @ W1) @ W2
        key = jax.random.key(seed)
        ks = jax.random.split(key, 9)
        B, T = (2, 128)
        x = jax.random.normal(ks[0], (B, T, D_MODEL), dtype=jnp.float32)
        router_w = jax.random.normal(ks[1], (D_MODEL, E_ROUTED), dtype=jnp.float32) * 0.006
        rms_w = jnp.ones((E_ROUTED, D_MODEL), dtype=jnp.float32)
        w1 = jax.random.normal(ks[2], (E_ROUTED, D_MODEL, HIDDEN), dtype=jnp.float32) * 0.02
        w2 = jax.random.normal(ks[3], (E_ROUTED, HIDDEN, D_MODEL), dtype=jnp.float32) * 0.02
        rms_w_s = jnp.ones((E_SHARED, D_MODEL), dtype=jnp.float32)
        w1_s = jax.random.normal(ks[4], (E_SHARED, D_MODEL, HIDDEN), dtype=jnp.float32) * 0.02
        w2_s = jax.random.normal(ks[5], (E_SHARED, HIDDEN, D_MODEL), dtype=jnp.float32) * 0.02
        return {'x': x, 'router_w': router_w, 'rms_w': rms_w, 'w1': w1, 'w2': w2, 'rms_w_s': rms_w_s, 'w1_s': w1_s, 'w2_s': w2_s}
    _L0_ffn_in = _L0_ffn_setup()
    _d = {'L0_attn_x': _L0_attn_in['x'], 'L0_attn_in_W': _L0_attn_in['in_W'], 'L0_attn_in_b': _L0_attn_in['in_b'], 'L0_attn_log_dt': _L0_attn_in['log_dt'], 'L0_attn_C': _L0_attn_in['C'], 'L0_attn_log_A_real': _L0_attn_in['log_A_real'], 'L0_attn_A_imag': _L0_attn_in['A_imag'], 'L0_attn_D_skip': _L0_attn_in['D_skip'], 'L0_attn_glu_W': _L0_attn_in['glu_W'], 'L0_attn_glu_b': _L0_attn_in['glu_b'], 'L0_attn_out_W': _L0_attn_in['out_W'], 'L0_attn_out_b': _L0_attn_in['out_b'], 'L0_ffn_router_w': _L0_ffn_in['router_w'], 'L0_ffn_rms_w': _L0_ffn_in['rms_w'], 'L0_ffn_w1': _L0_ffn_in['w1'], 'L0_ffn_w2': _L0_ffn_in['w2'], 'L0_ffn_rms_w_s': _L0_ffn_in['rms_w_s'], 'L0_ffn_w1_s': _L0_ffn_in['w1_s'], 'L0_ffn_w2_s': _L0_ffn_in['w2_s']}
    _x0 = _d['L0_attn_x']
    _d['L0_attn_x'] = jax.random.normal(jax.random.fold_in(jax.random.key(seed), 1), (2, 2048, 128), dtype=_x0.dtype)
    del _x0
    return _d

def reference(L0_attn_x, L0_attn_in_W, L0_attn_in_b, L0_attn_log_dt, L0_attn_C, L0_attn_log_A_real, L0_attn_A_imag, L0_attn_D_skip, L0_attn_glu_W, L0_attn_glu_b, L0_attn_out_W, L0_attn_out_b, L0_ffn_router_w, L0_ffn_rms_w, L0_ffn_w1, L0_ffn_w2, L0_ffn_rms_w_s, L0_ffn_w1_s, L0_ffn_w2_s):

    def _L0_attn_ref(x, in_W, in_b, log_dt, C, log_A_real, A_imag, D_skip, glu_W, glu_b, out_W, out_b):
        import jax, jax.numpy as jnp
        import numpy as np
        B, L, D, N = (8, 128, 128, 32)
        DT_MIN, DT_MAX = (0.001, 0.1)
        x_in = x @ in_W.T + in_b
        u = jnp.swapaxes(x_in, 1, 2)
        Lseq = u.shape[-1]
        dt = jnp.exp(log_dt)
        Cc = (C[..., 0] + 1j * C[..., 1]).astype(jnp.complex64)
        A = (-jnp.exp(log_A_real) + 1j * A_imag).astype(jnp.complex64)
        dtA = A * dt[:, None].astype(jnp.complex64)
        K = jnp.exp(dtA[:, :, None] * jnp.arange(Lseq, dtype=jnp.float32))
        Ceff = Cc * (jnp.exp(dtA) - 1.0) / A
        k = 2.0 * jnp.einsum('hn,hnl->hl', Ceff, K).real
        n = 2 * Lseq
        k_f = jnp.fft.rfft(k, n=n)
        u_f = jnp.fft.rfft(u, n=n)
        y = jnp.fft.irfft(u_f * k_f, n=n)[..., :Lseq]
        y = y + u * D_skip[:, None]
        y = jax.nn.gelu(y, approximate=False)
        z = jnp.einsum('oh,bhl->bol', glu_W, y) + glu_b[None, :, None]
        a, g = jnp.split(z, 2, axis=1)
        y = a * jax.nn.sigmoid(g)
        y = jnp.swapaxes(y, 1, 2)
        out = y @ out_W.T + out_b
        return out + x

    def _L0_ffn_ref(x, router_w, rms_w, w1, w2, rms_w_s, w1_s, w2_s):
        import jax, jax.numpy as jnp
        import numpy as np
        D_MODEL = 128
        HIDDEN = 256
        E_ROUTED = 14
        E_SHARED = 2
        TOP_K = 2
        EPS = 1e-09
        RMS_EPS = 1.1920929e-07

        def _ffn(xn, rw, W1, W2):
            ms = jnp.mean(xn * xn, axis=-1, keepdims=True)
            h = xn * jax.lax.rsqrt(ms + RMS_EPS) * rw
            return jax.nn.silu(h @ W1) @ W2
        B, T, D = x.shape
        N = B * T
        xf = x.reshape(N, D)
        gates = jax.nn.softmax(xf @ router_w, axis=-1)
        top_v, top_i = jax.lax.top_k(gates, TOP_K)
        masked = jnp.zeros_like(gates).at[jnp.arange(N)[:, None], top_i].set(top_v)
        masked = masked / (masked.sum(axis=-1, keepdims=True) + EPS)
        routed = jax.vmap(lambda rw_, W1_, W2_: _ffn(xf, rw_, W1_, W2_))(rms_w, w1, w2)
        routed_out = jnp.einsum('end,ne->nd', routed, masked)
        shared = jax.vmap(lambda rw_, W1_, W2_: _ffn(xf, rw_, W1_, W2_))(rms_w_s, w1_s, w2_s).sum(0)
        return (routed_out + shared).reshape(B, T, D)
    x = L0_attn_x
    x = x + _L0_attn_ref(_layernorm(x, axis=-1), L0_attn_in_W, L0_attn_in_b, L0_attn_log_dt, L0_attn_C, L0_attn_log_A_real, L0_attn_A_imag, L0_attn_D_skip, L0_attn_glu_W, L0_attn_glu_b, L0_attn_out_W, L0_attn_out_b)
    x = x + _L0_ffn_ref(_layernorm(x, axis=-1), L0_ffn_router_w, L0_ffn_rms_w, L0_ffn_w1, L0_ffn_w2, L0_ffn_rms_w_s, L0_ffn_w1_s, L0_ffn_w2_s)
    return x

_drawn_inputs = setup_inputs


def setup_inputs(seed=0):
    import zlib

    import numpy as np

    out = dict(_drawn_inputs(seed))
    spreads = {'L0_attn_log_A_real': (-0.6931471824645996, 0.6),
     'L0_ffn_rms_w': (1.0, 0.6),
     'L0_ffn_rms_w_s': (1.0, 0.6)}
    factors = {'L0_attn_in_b': 5.597,
     'L0_attn_glu_b': 6.946,
     'L0_ffn_router_w': 4.445,
     'L0_ffn_w1': 4.149,
     'L0_ffn_w2': 4.143}
    for name, (base, spread) in spreads.items():
        noise = np.random.default_rng([zlib.crc32(name.encode()), seed]).standard_normal(out[name].shape)
        drawn = base * np.exp(spread * noise) if base else spread * noise
        out[name] = jnp.asarray(drawn.astype(out[name].dtype))
    for name, factor in factors.items():
        out[name] = (out[name] * factor).astype(out[name].dtype)
    return out
```

```python
from contextlib import ExitStack

import numpy as np

import concourse.bass as bass
from concourse import mybir

F32 = mybir.dt.float32
U32 = mybir.dt.uint32
ALU = mybir.AluOpType
ACT = mybir.ActivationFunctionType
AX = mybir.AxisListType

P = 128
LN_EPS = 1e-5
RMS_EPS = 1.1920929e-07
PI = float(np.pi)
MAGIC = 12582912.0
LOG2E = float(np.log2(np.e))
LN2_HI = 0.693359375
LN2_LO = float(np.log(2.0) - 0.693359375)
TWO_PI = 6.2831850
FACT = [1.0, 1.0, 2.0, 6.0, 24.0, 120.0, 720.0, 5040.0, 40320.0, 362880.0]


def build_kernel(nc, x, in_w, in_b, log_dt, c_par, log_a, a_imag, d_skip, glu_w, glu_b,
                 out_w, out_b, router_w, rms_w, w1, w2, rms_ws, w1s, w2s, out):
    B, L, D = x.shape
    N = a_imag.shape[1]
    NT = B * L // P
    NC = L // P
    NPAIR = D // 2
    NG, HG = 4, D // 4
    PG = HG // 2
    NX = D // 4
    E, ES, HID = w1.shape[0], w1s.shape[0], w1.shape[2]
    EA, HC = E + ES, HID // P
    TOKENS = B * L
    ROUTES = 2 * TOKENS
    STEP = 6
    NBLK = -(-(ROUTES // P + E - 1) // STEP) * STEP
    AHEAD = 3
    NROW = (NBLK + AHEAD) * P
    ROW = D + 2
    NOWHERE = 1 << 20
    CH = NT // 4
    assert (B, L, D, N) == (2, 2048, 128, 32) and (E, ES, HID) == (14, 2, 256)

    ctx = ExitStack()
    with ctx:
        def sb(name, shape, dt=F32):
            return ctx.enter_context(nc.sbuf_tensor(name, shape, dt))

        def sem(name):
            return ctx.enter_context(nc.semaphore(name))

        bank = [ctx.enter_context(nc.psum_tensor(f"bank{i}", [P, 512], F32)) for i in range(8)]

        x_sb = sb("x_sb", [P, NT, D])
        xn = sb("xn", [P, NT, D])
        xnT = sb("xnT", [P, 2, 512])
        u = sb("u", [P, D, NT])
        v1 = sb("v1", [P, D, 2, N])
        v2 = sb("v2", [P, NPAIR, P])
        area = sb("area", [P, 13312])
        abb = area[:, 0:4096].rearrange("p (z h c) -> p z h c", z=2, h=HG)
        mag = area[:, 4096:8192].rearrange("p (g m) -> p g m", g=NG)
        trig = area[:, 8192:12288].rearrange("p (z r m) -> p z r m", z=2, r=2)
        rnd = area[:, 12288:13312]
        s_bd = area[:, 8192:12288].rearrange("p (q e c) -> p q e c", q=NPAIR, e=2)
        st = sb("st", [P, 2, NX, NT])
        v1_flat = v1[:].rearrange("p h r n -> p (h r n)")
        xn_flat = xn[:].rearrange("p i d -> p (i d)")
        hank = [h_.rearrange("p (h t) -> p h t", h=HG)
                for h_ in (area[:, 0:4096], area[:, 4096:8192], v1_flat[:, 4096:8192], xn_flat)]
        yq = area[:, 0:4096]
        mul1 = v1_flat[:, 0:2048].rearrange("p (r x t) -> p r x t", r=2, x=NX)
        mul2 = v1_flat[:, 2048:4096].rearrange("p (r x t) -> p r x t", r=2, x=NX)
        y_sb = xn
        w1_sb = v1_flat[:, 4096:8192].rearrange("p (e m) -> p e m", e=EA)
        w2_sb = v1_flat[:, 0:4096].rearrange("p (e c d) -> p e c d", e=EA, c=HC)
        v2_flat = v2[:].rearrange("p q s -> p (q s)")
        h0T = v2_flat[:, 0:4096]
        yT = v2_flat[:, 4096:5120].rearrange("p (z m) -> p z m", z=2)
        aT = v2_flat[:, 5120:6144].rearrange("p (z m) -> p z m", z=2)
        sg = v2_flat[:, 6144:7168].rearrange("p (z m) -> p z m", z=2)
        hx = area[:, 0:NT * 2 * ROW].rearrange("p (i k c) -> p i k c", i=NT, k=2)
        ysh = xn[:].rearrange("p i d -> p (i d)").rearrange("p (z e m) -> p z e m", z=2, e=ES * HC)
        u_flat = u[:].rearrange("p h c -> p (h c)")
        rt = [u_flat[:, 448 * i:448 * i + 448] for i in range(9)]
        xs = v2_flat[:, 4096:4096 + STEP * ROW].rearrange("p (z c) -> p z c", z=STEP)
        xsT = v2_flat[:, 5120:5504].rearrange("p (z c) -> p z c", z=3)
        w1c = v2_flat[:, 5504:6272].rearrange("p (z c) -> p z c", z=3)
        act_sb = v2_flat[:, 6272:7040].rearrange("p (z c) -> p z c", z=3)
        yb = v2_flat[:, 7040:7808].rearrange("p (z c) -> p z c", z=STEP)
        yl = area[:, 0:8192].rearrange("p (i m) -> p i m", i=NT)

        ident = sb("ident", [P, P])
        exch = sb("exch", [P, P])
        srow = sb("srow", [P, 1])
        halfpi = sb("halfpi", [P, 1])
        mhalf = sb("mhalf", [P, NT])
        inb_bc = sb("inb_bc", [P, D])
        outb_bc = sb("outb_bc", [P, D])
        glub = sb("glub", [P, 2])
        dskip = sb("dskip", [HG, NG])
        wnat = v2[:, NPAIR - 4:NPAIR, :]
        wT = sb("wT", [P, 4, P])

        p33 = sb("p33", [P, N + 1])
        z33 = sb("z33", [P, N + 1])
        r33 = sb("r33", [P, N + 1])
        q33 = sb("q33", [P, N + 1])
        e33 = sb("e33", [P, N + 1])
        aim = sb("aim", [P, N])
        cpar = sb("cpar", [P, N, 2])
        ab = sb("ab", [P, 2, N])
        fr = sb("fr", [P, 2, N])
        frq = sb("frq", [P, 2, N])
        sn = sb("sn", [P, 2, N])
        cs128 = sb("cs128", [P, N])
        sh = sb("sh", [P, N])
        mag128 = sb("mag128", [P, N])
        em = sb("em", [P, N])
        ey = sb("ey", [P, N])
        inv = sb("inv", [P, N])
        den = sb("den", [P, N])
        t = [sb(f"t{i}", [P, N]) for i in range(8)]
        q1 = sb("q1", [P, 4, N])
        q2 = sb("q2", [P, 2, N])
        lw = sb("lw", [P, 6, NX])
        cbig = st[:].rearrange("p r x c -> p (r x c)").rearrange("p (g m) -> p g m", g=NG)
        ksb = sb("ksb", [HG, NG, 256])
        stats = sb("stats", [P, NT, 6])
        mv = sb("mv", [P, NT, 2])
        ve = sb("ve", [P, NT])
        rs0 = sb("rs0", [P, NT])
        rs1 = sb("rs1", [P, NT])
        rstd = sb("rstd", [P, NT])

        upper = sb("upper", [P, P])
        ones = sb("ones", [P, P])
        rank_w = sb("rank_w", [P, 448])
        first = sb("first", [P, 448])
        blk = sb("blk", [P, NBLK + 4])
        xinit = sb("xinit", [P, ROW])
        rw = sb("rw", [P, E])
        rmsn = sb("rmsn", [EA, P])
        rmsT = sb("rmsT", [P, EA])
        ybi = sb("ybi", [P, STEP])
        col = [sb(f"col{i}", [P, NT]) for i in range(8)]
        e14 = [sb(f"e14_{i}", [P, E]) for i in range(4)]
        pos = sb("pos", [P, 2, NT], U32)
        etab = sb("etab", [P, NBLK + 4], U32)

        xs_dram = nc.dram_tensor("xs_dram", [NROW, ROW], F32, kind="Internal")
        y_dram = nc.dram_tensor("y_dram", [ROUTES, D], F32, kind="Internal")
        ab_dram = nc.dram_tensor("ab_dram", [D, 2 * N], F32, kind="Internal")
        kp_dram = nc.dram_tensor("kp_dram", [D, 256], F32, kind="Internal")

        par_in = sem("par_in")
        x_in = [sem(f"x_in{g}") for g in range(4)]
        w_in = sem("w_in")
        b_in = sem("b_in")
        const_ready = sem("const_ready")
        pool_step = sem("pool_step")
        dve_step = sem("dve_step")
        act_step = sem("act_step")
        ab_ready = sem("ab_ready")
        ab_out = sem("ab_out")
        abb_in = [sem(f"abb_in{z}") for z in range(2)]
        abb_used = sem("abb_used")
        turns_ready = sem("turns_ready")
        psin_ready = sem("psin_ready")
        em_ready = sem("em_ready")
        var_ready = sem("var_ready")
        rs_ready = sem("rs_ready")
        xn_ready = sem("xn_ready")
        wT_ps = sem("wT_ps")
        wT_ready = sem("wT_ready")
        xnT_ps = sem("xnT_ps")
        xnT_ready = sem("xnT_ready")
        u_ps = sem("u_ps")
        u_ready = sem("u_ready")
        r0_ready = sem("r0_ready")
        mag_ready = sem("mag_ready")
        arg_ready = sem("arg_ready")
        trig_ready = sem("trig_ready")
        trig_used = sem("trig_used")
        v1_ready = sem("v1_ready")
        v2_ps = sem("v2_ps")
        v2_act = sem("v2_act")
        v2_dve = sem("v2_dve")
        q_ready = sem("q_ready")
        q_ps = sem("q_ps")
        lw_act = sem("lw_act")
        cbig_ready = sem("cbig_ready")
        cbig_zero = sem("cbig_zero")
        k_ps = sem("k_ps")
        k_ready = sem("k_ready")
        kp_out = sem("kp_out")
        hank_in = [sem(f"hank_in{g}") for g in range(NG)]
        t0_ps = sem("t0_ps")
        b_ps = sem("b_ps")
        b_act = sem("b_act")
        b_dve = sem("b_dve")
        sbd_zero = sem("sbd_zero")
        mul_ready = sem("mul_ready")
        sbd_act = sem("sbd_act")
        sbd_dve = sem("sbd_dve")
        y_ps = sem("y_ps")
        yq_ready = sem("yq_ready")
        yq_ps = sem("yq_ps")
        y_dve = sem("y_dve")
        y_ready = sem("y_ready")
        xinit_ready = sem("xinit_ready")
        xs_cleared = sem("xs_cleared")
        ew_in = sem("ew_in")
        ew2_in = sem("ew2_in")
        rms_in = sem("rms_in")
        rms_ps = sem("rms_ps")
        w1_ready = sem("w1_ready")
        yT_ps = sem("yT_ps")
        yT_ready = sem("yT_ready")
        ag_ps = sem("ag_ps")
        sg_ready = sem("sg_ready")
        aT_ready = sem("aT_ready")
        o_ps = sem("o_ps")
        x2_ready = sem("x2_ready")
        q2_ready = sem("q2_ready")
        scale_ready = sem("scale_ready")
        h0_ready = sem("h0_ready")
        ids_ready = sem("ids_ready")
        hx_ready = sem("hx_ready")
        hT_ps = sem("hT_ps")
        hT_ready = sem("hT_ready")
        r_ps = sem("r_ps")
        rstd_ready = sem("rstd_ready")
        lg_ready = sem("lg_ready")
        ex_ready = sem("ex_ready")
        m_ready = sem("m_ready")
        rank_ps = sem("rank_ps")
        gate_ready = sem("gate_ready")
        pos_ready = sem("pos_ready")
        etab_ready = sem("etab_ready")
        sh_ps = sem("sh_ps")
        sh_ready = sem("sh_ready")
        so_ps = sem("so_ps")
        so_added = sem("so_added")
        rows_out = sem("rows_out")
        xs_in = [sem(f"xs_in{z}") for z in range(STEP)]
        pool_turn = sem("pool_turn")
        xt_ps = sem("xt_ps")
        xt_ready = sem("xt_ready")
        w1c_ready = sem("w1c_ready")
        hid_ps = sem("hid_ps")
        act_ready = sem("act_ready")
        yb_ps = sem("yb_ps")
        yb_ready = sem("yb_ready")
        yb_out = [sem(f"yb_out{z}") for z in range(STEP)]
        y_in = [sem(f"y_in{g}") for g in range(4)]
        sum_ready = sem("sum_ready")
        out_done = sem("out_done")

        x_tok = x.rearrange("b (c p) d -> p (b c) d", p=P)

        def evict_v2_by_act(i):
            return i % 2 == 0

        def y_tiles(i):
            return y_sb[:, :, 16 * i:16 * i + 16].rearrange("p c (x k) -> p c x k", k=4)

        block = ctx.enter_context(nc.Block())

        @block.sync
        def _(sp):
            sp.dma_start(p33[:, 0:1], log_dt.rearrange("(h o) -> h o", o=1)).then_inc(par_in, 16)
            sp.dma_start(p33[:, 1:N + 1], log_a).then_inc(par_in, 16)
            sp.dma_start(aim[:], a_imag).then_inc(par_in, 16)
            sp.dma_start(cpar[:], c_par).then_inc(par_in, 16)
            for g in range(4):
                sp.dma_start(x_sb[:, 8 * g:8 * g + 8, :], x_tok[:, 8 * g:8 * g + 8, :]).then_inc(x_in[g], 16)
            sp.wait_ge(ab_ready, 1)
            sp.dma_start(ab_dram.ap(), ab[:].rearrange("p a n -> p (a n)")).then_inc(ab_out, 16)
            sp.wait_ge(ab_out, 16)
            for g in range(NG):
                if g >= 2:
                    sp.wait_ge(abb_used, g - 1)
                    sp.wait_ge(mag_ready, g - 1)
                src = bass.AP(ab_dram, g * HG * 2 * N, [[0, P], [1, HG * 2 * N]])
                sp.dma_start(abb[:, g % 2].rearrange("p h c -> p (h c)"), src).then_inc(abb_in[g % 2], 16)
            for g in range(NG):
                sp.wait_ge(k_ready, g + 1)
                sp.dma_start(kp_dram.ap()[g * HG:(g + 1) * HG, :], ksb[:, g, :]).then_inc(kp_out, 16)
            for g in range(NG):
                sp.wait_ge(kp_out, 16 * NG)
                if g == 0:
                    sp.wait_ge(mag_ready, NG)
                    sp.wait_ge(abb_used, NG)
                    sp.wait_ge(v1_ready, NG)
                if g == 2:
                    sp.wait_ge(b_ps, 8)
                if g == 3:
                    sp.wait_ge(r0_ready, 4)
                    sp.wait_ge(xnT_ps, 8)
                src = bass.AP(kp_dram, g * HG * 256, [[1, P], [256, HG], [1, P]])
                sp.dma_start(hank[g], src).then_inc(hank_in[g], 16)
            xs_rows = xs_dram.ap().rearrange("(b p) c -> p b c", p=P)
            sp.wait_ge(rows_out, 16 * 2 * NT)
            for z in range(STEP):
                if z == 0:
                    sp.wait_ge(h0_ready, CH)
                    sp.wait_ge(hT_ready, CH)
                    sp.wait_ge(o_ps, CH)
                    sp.wait_ge(ag_ps, CH)
                sp.dma_start(xs[:, z, :], xs_rows[:, z, :]).then_inc(xs_in[z], 16)
            with sp.Fori(0, NBLK // STEP - 1) as it:
                for z in range(STEP):
                    sp.wait_ge(yb_ready, it * STEP + (z + 1 + 2))
                    sp.dma_start(xs[:, z, :], xs_rows[:, bass.ds(it * STEP + (STEP + z), 1), :]
                                 .rearrange("p b c -> p (b c)")).then_inc(xs_in[z], 16)
            for z in range(AHEAD):
                sp.wait_ge(yb_ready, NBLK - STEP + z + 1 + 2)
                sp.dma_start(xs[:, z, :], xs_rows[:, NBLK + z, :]).then_inc(xs_in[z], 16)
            y_tok = y_dram.ap().rearrange("(i p k) d -> p i (k d)", p=P, k=2)
            for z in range(STEP):
                sp.wait_ge(yb_out[z], 16 * (NBLK // STEP))
            for g in range(4):
                rows = slice(8 * g, 8 * g + 8)
                sp.dma_start(yl[:, rows], y_tok[:, rows]).then_inc(y_in[g], 16)
            out_tok = out.rearrange("b (c p) d -> p (b c) d", p=P)
            for g in range(4):
                rows = slice(8 * g, 8 * g + 8)
                sp.wait_ge(sum_ready, g + 1)
                sp.dma_start(out_tok[:, rows], x_sb[:, rows]).then_inc(out_done, 16)
            for z in range(AHEAD):
                sp.wait_ge(xs_in[z], 16 * (NBLK // STEP + 1))
            sp.wait_ge(out_done, 64)

        @block.gpsimd
        def _(pool):
            g_ = nc.gpsimd
            steps = [0]

            def link(ins):
                steps[0] += 1
                ins.then_inc(pool_step, 1)
                pool.wait_ge(pool_step, steps[0])

            link(g_.memset(ident[:], 0.0))
            link(g_.affine_select(out=ident[:], in_=ident[:], compare_op=ALU.not_equal, fill=1.0,
                                  base=0, pattern=[[-1, P]], channel_multiplier=1))
            link(g_.memset(exch[:], 0.0))
            link(g_.affine_select(out=exch[:], in_=exch[:], compare_op=ALU.not_equal, fill=1.0,
                                  base=-(P - 1), pattern=[[1, P]], channel_multiplier=1))
            link(g_.iota(srow[:], pattern=[[0, 1]], base=0, channel_multiplier=1,
                         allow_small_or_imprecise_dtypes=True))
            g_.memset(halfpi[:], PI / 2)
            link(g_.memset(mhalf[:], -0.5))
            link(g_.memset(xinit[:], 0.0))
            g_.memset(xinit[:, D:D + 1].bitcast(U32), NOWHERE).then_inc(xinit_ready, 1)
            g_.memset(cbig[:], 0.0).then_inc(cbig_zero, 1)
            g_.memset(ksb[:], 0.0).then_inc(const_ready, 1)

            def power(g):
                pool.wait_ge(var_ready, g + 1)
                g_.tensor_tensor(rs0[:, 8 * g:8 * g + 8], ve[:, 8 * g:8 * g + 8], mhalf[:, 8 * g:8 * g + 8],
                                 ALU.pow).then_inc(rs_ready, 1)

            power(0)
            power(1)
            power(2)
            power(3)
            tt, ts = g_.tensor_tensor, g_.tensor_scalar
            pool.wait_ge(em_ready, 1)
            pool.wait_ge(psin_ready, 1)
            tS, cb, lr, li, er, gr, gi, tmp = t
            ar, ai = e33[:, 1:N + 1], aim[:]
            cr, ci = cpar[:, :, 0], cpar[:, :, 1]
            link(tt(sh[:], sh[:], sh[:], ALU.mult))
            ts(cb[:], sh[:], -2.0, 1.0, ALU.mult, ALU.add)
            link(ts(tS[:], sh[:], 2.0, None, ALU.mult))
            tt(er[:], em[:], cb[:], ALU.mult)
            tt(li[:], em[:], sn[:, 0, :], ALU.mult)
            link(tt(lr[:], em[:], cb[:], ALU.mult))
            tt(er[:], er[:], tS[:], ALU.subtract)
            tt(lr[:], lr[:], cb[:], ALU.add)
            link(tt(li[:], li[:], sn[:, 0, :], ALU.add))
            tt(gr[:], li[:], ai, ALU.mult)
            link(tt(tmp[:], er[:], ar, ALU.mult))
            link(tt(gr[:], gr[:], tmp[:], ALU.subtract))
            tt(gi[:], li[:], ar, ALU.mult)
            link(tt(tmp[:], er[:], ai, ALU.mult))
            link(tt(gi[:], gi[:], tmp[:], ALU.add))
            tt(gr[:], gr[:], inv[:], ALU.mult)
            link(tt(gi[:], gi[:], inv[:], ALU.mult))
            tt(er[:], gr[:], cr, ALU.mult)
            tt(tS[:], gi[:], ci, ALU.mult)
            tt(cb[:], gr[:], ci, ALU.mult)
            link(tt(tmp[:], gi[:], cr, ALU.mult))
            tt(er[:], er[:], tS[:], ALU.add)
            link(tt(cb[:], cb[:], tmp[:], ALU.subtract))
            ts(q2[:, 0, :], er[:], 2.0, None, ALU.mult)
            link(ts(q2[:, 1, :], cb[:], -2.0, None, ALU.mult))
            tt(er[:], q2[:, 0, :], lr[:], ALU.mult)
            tt(tS[:], q2[:, 1, :], li[:], ALU.mult)
            tt(cb[:], q2[:, 0, :], li[:], ALU.mult)
            link(tt(tmp[:], q2[:, 1, :], lr[:], ALU.mult))
            tt(q1[:, 2, :], er[:], tS[:], ALU.add)
            tt(q1[:, 3, :], cb[:], tmp[:], ALU.subtract)
            tt(q1[:, 0, :], mag128[:], cs128[:], ALU.mult)
            link(tt(q1[:, 1, :], mag128[:], sn[:, 1, :], ALU.mult))
            g_.engine_nop().then_inc(q_ready, 1)
            link(g_.memset(ones[:], 1.0))
            link(g_.affine_select(out=upper[:], in_=ones[:], compare_op=ALU.is_gt, fill=0.0,
                                  base=0, pattern=[[1, P]], channel_multiplier=-1))
            g_.iota(rank_w[:], pattern=[[0, NT], [-1, E]], base=E, channel_multiplier=0,
                    allow_small_or_imprecise_dtypes=True)
            g_.iota(blk[:], pattern=[[1, NBLK + 4]], base=0, channel_multiplier=0,
                    allow_small_or_imprecise_dtypes=True)
            link(g_.memset(first[:], 1.0))
            link(g_.memset(first[:].rearrange("p (e i) -> p e i", e=E)[:, :, 0:1], 0.0))
            for g in range(NG):
                pool.wait_ge(mag_ready, g + 1)
                pool.wait_ge(trig_ready, g + 1)
                dst = v1[:, g * HG:(g + 1) * HG]
                for r in range(2):
                    last = g_.tensor_tensor(dst[:, :, r, :], mag[:, g].rearrange("p (h n) -> p h n", h=HG),
                                            trig[:, g % 2, r].rearrange("p (h n) -> p h n", h=HG), ALU.mult)
                last.then_inc(v1_ready, 1)
            for g in range(4):
                rows = slice(8 * g, 8 * g + 8)
                pool.wait_ge(xn_ready, g + 1)
                link(g_.tensor_tensor(x_sb[:, rows], x_sb[:, rows], xn[:, rows], ALU.add))
                g_.tensor_tensor(x_sb[:, rows], x_sb[:, rows], outb_bc[:].unsqueeze(1).broadcast_to([P, 8, D]),
                                 ALU.add).then_inc(r0_ready, 1)
            pool.wait_ge(v1_ready, NG)
            g_.memset(area[:, 8192:12288], 0.0).then_inc(sbd_zero, 1)

            pool.wait_ge(yq_ps, 8)
            ids = hx[:, :, :, D:D + 1].bitcast(U32).rearrange("p i k o -> p i (k o)")
            g_.iota(ids, pattern=[[2 * P, NT], [1, 2]], base=0, channel_multiplier=2).then_inc(ids_ready, 1)

            def root(dst, src, tmp1, tmp2, w):
                link(tt(tmp1, src, mhalf[:, 0:w], ALU.pow))
                link(tt(tmp2, tmp1, tmp1, ALU.mult))
                link(tt(tmp2, tmp2, src, ALU.mult))
                link(ts(tmp2, tmp2, -0.5, 1.5, ALU.mult, ALU.add))
                return tt(dst, tmp1, tmp2, ALU.mult)

            for c in range(CH + 1):
                if c < CH:
                    k = slice(4 * c, 4 * c + 4)
                    pool.wait_ge(q2_ready, c + 1)
                    root(rs1[:, k], ve[:, k], rs0[:, k], col[0][:, k], 4).then_inc(scale_ready, 1)
                if c >= 1:
                    k = slice(4 * c - 4, 4 * c)
                    pool.wait_ge(h0_ready, c)
                    g_.tensor_copy(hx[:, k, 1, 0:D], hx[:, k, 0, 0:D]).then_inc(hx_ready, 1)
            link(ts(col[1][:], mv[:, :, 1], LN_EPS, None, ALU.add))
            link(root(rstd[:], col[1][:], rs0[:], col[0][:], NT))
            link(tt(rstd[:], rstd[:], ve[:], ALU.mult))
            tt(rstd[:], rstd[:], rs1[:], ALU.mult).then_inc(rstd_ready, 1)

            pool.wait_ge(gate_ready, 1)
            pool.wait_ge(pos_ready, 1)
            pool.wait_ge(ids_ready, 1)
            pool.wait_ge(xs_cleared, 16)
            for i in range(NT):
                for k in range(2):
                    pool.indirect_dma_start(out=xs_dram.ap(), out_offset=bass.IndirectOffsetOnAxis(ap=pos[:, k, i:i + 1], axis=0),
                                            in_=hx[:, i, k, :], in_offset=None, bounds_check=NROW - 1,
                                            oob_is_err=False).then_inc(rows_out, 16)
            last_row = pool.to_reg(ROUTES - 1)
            with pool.Fori(0, NBLK // STEP) as it:
                for z in range(STEP):
                    pool.wait_ge(yb_ready, it * STEP + (z + 1 + 2))
                    g_.sem_inc(pool_turn, 1)
                    pool.indirect_dma_start(out=y_dram.ap(), out_offset=bass.IndirectOffsetOnAxis(ap=ybi[:, z:z + 1].bitcast(U32), axis=0),
                                            in_=yb[:, z, :], in_offset=None, bounds_check=last_row,
                                            oob_is_err=False).then_inc(yb_out[z], 16)

        @block.vector
        def _(dve):
            v = nc.vector
            steps = [0]

            def link(ins):
                steps[0] += 1
                ins.then_inc(dve_step, 1)
                dve.wait_ge(dve_step, steps[0])

            dve.wait_ge(par_in, 64)
            link(v.tensor_scalar(p33[:], p33[:], -87.0, 88.0, ALU.max, ALU.min))
            link(v.tensor_scalar(z33[:], p33[:], LOG2E, MAGIC + 127.0, ALU.mult, ALU.add))
            link(v.tensor_scalar(q33[:], z33[:], -(MAGIC + 127.0), None, ALU.add))
            link(v.scalar_tensor_tensor(out=r33[:], in0=q33[:], scalar=-LN2_HI, in1=p33[:], op0=ALU.mult, op1=ALU.add))
            link(v.scalar_tensor_tensor(out=r33[:], in0=q33[:], scalar=-LN2_LO, in1=r33[:], op0=ALU.mult, op1=ALU.add))
            link(v.tensor_scalar(q33[:], r33[:], 1.0 / FACT[7], None, ALU.mult))
            for k in (6, 5, 4, 3, 2, 1):
                link(v.scalar_tensor_tensor(out=q33[:], in0=q33[:], scalar=1.0 / FACT[k], in1=r33[:],
                                            op0=ALU.add, op1=ALU.mult))
            link(v.tensor_scalar(z33[:].bitcast(U32), z33[:].bitcast(U32), 23, None, ALU.logical_shift_left))
            link(v.scalar_tensor_tensor(out=e33[:], in0=q33[:], scalar=1.0, in1=z33[:], op0=ALU.add, op1=ALU.mult))
            v.tensor_scalar(ab[:, 0, :], e33[:, 1:N + 1], e33[:, 0:1], -1.0, ALU.mult, ALU.mult)
            link(v.tensor_scalar(ab[:, 1, :], aim[:], e33[:, 0:1], 1.0 / (2 * PI), ALU.mult, ALU.mult))
            v.engine_nop().then_inc(ab_ready, 1)
            v.tensor_copy(fr[:, 0, :], ab[:, 1, :])
            link(v.tensor_scalar(fr[:, 1, :], ab[:, 1, :], float(P), None, ALU.mult))
            link(v.tensor_scalar(frq[:], fr[:], MAGIC, None, ALU.add))
            link(v.tensor_scalar(frq[:], frq[:], -MAGIC, None, ALU.add))
            link(v.tensor_tensor(fr[:], fr[:], frq[:], ALU.subtract))
            v.tensor_scalar(frq[:].bitcast(U32), fr[:].bitcast(U32), 0x7FFFFFFF, None, ALU.bitwise_and).then_inc(turns_ready, 1)
            link(v.tensor_scalar(ey[:], ab[:, 0, :], -24.0, 1.0 / 32, ALU.max, ALU.mult))
            link(v.tensor_scalar(em[:], ey[:], 1.0 / FACT[9], None, ALU.mult))
            for k in (8, 7, 6, 5, 4, 3, 2, 1):
                link(v.scalar_tensor_tensor(out=em[:], in0=em[:], scalar=1.0 / FACT[k], in1=ey[:],
                                            op0=ALU.add, op1=ALU.mult))
            for _ in range(5):
                link(v.scalar_tensor_tensor(out=em[:], in0=em[:], scalar=2.0, in1=em[:], op0=ALU.add, op1=ALU.mult))
            v.tensor_tensor(den[:], e33[:, 1:N + 1], e33[:, 1:N + 1], ALU.mult)
            link(v.tensor_tensor(inv[:], aim[:], aim[:], ALU.mult))
            link(v.tensor_tensor(den[:], den[:], inv[:], ALU.add))
            v.reciprocal(inv[:], den[:]).then_inc(em_ready, 1)

            def ln_stats(g):
                dve.wait_ge(x_in[g], 16)
                for i in range(8 * g, 8 * g + 8):
                    last = v.bn_stats(stats[:, i, :], x_sb[:, i, :])
                link(last)
                for i in range(8 * g, 8 * g + 8):
                    last = v.bn_aggr(mv[:, i, :], stats[:, i, :])
                link(last)
                v.tensor_scalar(ve[:, 8 * g:8 * g + 8], mv[:, 8 * g:8 * g + 8, 1], LN_EPS, None,
                                ALU.add).then_inc(var_ready, 1)

            def ln_norm(g):
                c = slice(8 * g, 8 * g + 8)
                dve.wait_ge(rs_ready, g + 1)
                link(v.tensor_tensor(rs1[:, c], rs0[:, c], rs0[:, c], ALU.mult))
                link(v.tensor_tensor(rs1[:, c], rs1[:, c], ve[:, c], ALU.mult))
                link(v.tensor_scalar(rs1[:, c], rs1[:, c], -0.5, 1.5, ALU.mult, ALU.add))
                link(v.tensor_tensor(rstd[:, c], rs1[:, c], rs0[:, c], ALU.mult))
                for i in range(8 * g, 8 * g + 8):
                    last = v.tensor_scalar(xn[:, i, :], x_sb[:, i, :], mv[:, i, 0:1], rstd[:, i:i + 1],
                                           ALU.subtract, ALU.mult)
                last.then_inc(xn_ready, 1)

            def table_args(g):
                dve.wait_ge(abb_in[g % 2], 16 * (g // 2 + 1))
                if g >= 2:
                    dve.wait_ge(v1_ready, g - 1)
                f = abb[:, g % 2, :, N:2 * N]
                rv = rnd.rearrange("p (h n) -> p h n", h=HG)
                arg = trig[:, g % 2, 1].rearrange("p (h n) -> p h n", h=HG)
                link(v.tensor_scalar(rv, f, srow[:, 0:1], MAGIC, ALU.mult, ALU.add))
                link(v.tensor_scalar(rnd, rnd, -MAGIC, None, ALU.add))
                ins = v.scalar_tensor_tensor(out=arg, in0=f, scalar=srow[:, 0:1], in1=rv,
                                             op0=ALU.mult, op1=ALU.subtract)
                link(ins)
                v.tensor_scalar(trig[:, g % 2, 0].bitcast(U32), trig[:, g % 2, 1].bitcast(U32), 0x7FFFFFFF, None,
                                ALU.bitwise_and).then_inc(arg_ready, 1)
                v.engine_nop().then_inc(abb_used, 1)

            def evict_u(i):
                dve.wait_ge(u_ps, i + 1)
                src = bank[2 + i % 2][:].rearrange("p (c h) -> p h c", c=4)
                v.tensor_tensor(u[:, :, 4 * i:4 * i + 4], src, inb_bc[:].unsqueeze(2).broadcast_to([P, D, 4]),
                                ALU.add).then_inc(u_ready, 1)

            def evict_v2(i):
                if not evict_v2_by_act(i):
                    dve.wait_ge(v2_ps, i + 1)
                    v.tensor_copy(v2[:, 4 * i:4 * i + 4, :], bank[4 + i % 4][:]
                                  .rearrange("p (q s) -> p q s", q=4)).then_inc(v2_dve, 1)

            dve.wait_ge(const_ready, 1)
            ln_stats(0)
            ln_stats(1)
            ln_norm(0)
            ln_stats(2)
            table_args(0)
            ln_norm(1)
            ln_stats(3)
            table_args(1)
            ln_norm(2)
            ln_norm(3)
            dve.wait_ge(b_in, 64)
            for i in range(4):
                evict_u(i)
            table_args(2)
            for i in range(4, 8):
                evict_u(i)
            table_args(3)
            dve.wait_ge(q_ps, 1)
            dve.wait_ge(cbig_zero, 1)
            for e in range(2):
                dst = cbig[64 * e:64 * e + 64].rearrange("p g m -> p (g m)")
                for g in range(NG):
                    lo = 512 * g + e
                    last = v.tensor_copy(dst[:, lo:lo + 34 * 15 + 1:34], bank[3][0:64, HG * g + e:HG * (g + 1):2])
            last.then_inc(cbig_ready, 1)
            dve.wait_ge(lw_act, 1)
            link(v.tensor_scalar(lw[:, 2:6:2, :], lw[:, 3:6:2, :], -1.0, None, ALU.mult))
            for g in range(NG):
                for i in range(4 * g, 4 * g + 4):
                    evict_v2(i)
                if g >= 1:
                    evict_k = g - 1
                    dve.wait_ge(k_ps, evict_k + 1)
                    link(v.tensor_copy(ksb[:, evict_k, 127:255], bank[1 + evict_k % 2][0:HG, 0:P]))
                    v.tensor_tensor(ksb[:, evict_k, 127:128], ksb[:, evict_k, 127:128], dskip[:, evict_k:evict_k + 1],
                                    ALU.add).then_inc(k_ready, 1)
            g = NG - 1
            dve.wait_ge(k_ps, NG)
            link(v.tensor_copy(ksb[:, g, 127:255], bank[1 + g % 2][0:HG, 0:P]))
            v.tensor_tensor(ksb[:, g, 127:128], ksb[:, g, 127:128], dskip[:, g:g + 1], ALU.add).then_inc(k_ready, 1)

            for half in range(2):
                dve.wait_ge(b_ps, 4 * half + 4)
                for m in range(2):
                    k = 2 * m + 1
                    for r in range(2):
                        for q in range(4):
                            src = bank[4 * half + q][64 + 32 * r:96 + 32 * r].rearrange(
                                "p (j m e c) -> p j m e c", j=4, m=2, e=2)[:, :, m, 1, :]
                            last = v.tensor_copy(st[32 * k:32 * k + 32, r, 16 * half + 4 * q:16 * half + 4 * q + 4, :], src)
                last.then_inc(b_dve, 1)
            link(v.engine_nop())
            dve.wait_ge(b_act, 2)
            sv = st[:].rearrange("p r x (b j) -> p r x b j", b=B)
            lr_b = lw[:, 0, :].unsqueeze(1).unsqueeze(3).broadcast_to([P, 2, NX, B])
            li_b = lw[:, 2:4, :].unsqueeze(3).broadcast_to([P, 2, NX, B])
            m1 = mul1[:, :, :, 0:B]
            m2 = mul2[:, :, :, 0:B]
            dve.wait_ge(v2_ps, 16)
            for j in range(1, NC - 1):
                for r in range(2):
                    v.tensor_tensor(m1[:, r], lr_b[:, r], sv[:, r, :, :, j - 1], ALU.mult)
                    last = v.tensor_tensor(m2[:, r], li_b[:, r], sv[:, 1 - r, :, :, j - 1], ALU.mult)
                link(last)
                link(v.tensor_tensor(m1, m1, m2, ALU.add))
                link(v.tensor_tensor(sv[:, :, :, :, j], sv[:, :, :, :, j], m1, ALU.add))
            for r in range(2):
                v.tensor_tensor(mul1[:, r], lw[:, 1, :].unsqueeze(2).broadcast_to([P, NX, NT]), st[:, r], ALU.mult)
                last = v.tensor_tensor(mul2[:, r], lw[:, 4 + r, :].unsqueeze(2).broadcast_to([P, NX, NT]), st[:, 1 - r], ALU.mult)
            link(last)
            v.tensor_tensor(mul1[:, 0], mul1[:, 0], mul2[:, 0], ALU.add)
            link(v.scalar_tensor_tensor(out=mul1[:, 1], in0=mul1[:, 1], scalar=-1.0, in1=mul2[:, 1],
                                        op0=ALU.mult, op1=ALU.subtract))
            v.engine_nop().then_inc(mul_ready, 1)
            dve.wait_ge(sbd_zero, 1)
            for m in range(2):
                k = 2 * m + 1
                for r in range(2):
                    for b in range(B):
                        dst = s_bd[64 + 32 * r:96 + 32 * r, m::2, 1, NC * b + 1:NC * b + NC]
                        src = mul1[32 * k:32 * k + 32, r, :, NC * b:NC * b + NC - 1]
                        last = v.tensor_copy(dst, src)
            last.then_inc(sbd_dve, 1)


            for i in range(1, 8, 2):
                dve.wait_ge(yq_ps, i + 1)
                v.tensor_copy(y_tiles(i), bank[i][:].rearrange("p (x k c) -> p c x k", x=4, k=4)).then_inc(y_dve, 1)

            dve.wait_ge(rms_ps, 1)
            link(v.tensor_copy(rmsT[:], bank[0][:, 0:EA]))
            dve.wait_ge(ew_in, 32)
            for e in range(EA):
                last = v.tensor_scalar(w1_sb[:, e, :], w1_sb[:, e, :], rmsT[:, e:e + 1], None, ALU.mult)
            last.then_inc(w1_ready, 1)

            def glu(c):
                dve.wait_ge(sg_ready, c + 1)
                if c >= 2:
                    dve.wait_ge(o_ps, c - 1)
                v.scalar_tensor_tensor(out=aT[:, c % 2], in0=bank[2][:], scalar=glub[:, 0:1], in1=sg[:, c % 2],
                                       op0=ALU.add, op1=ALU.mult).then_inc(aT_ready, 1)

            def residual(c):
                rows = x_sb[:, 4 * c:4 * c + 4]
                dve.wait_ge(o_ps, c + 1)
                ins = v.tensor_tensor(rows, bank[4][:].rearrange("p (i d) -> p i d", i=4), rows, ALU.add)
                link(ins)
                v.engine_nop().then_inc(x2_ready, 1)
                for i in range(4 * c, 4 * c + 4):
                    last = v.bn_stats(stats[:, i, :], x_sb[:, i, :])
                link(last)
                for i in range(4 * c, 4 * c + 4):
                    last = v.bn_aggr(mv[:, i, :], stats[:, i, :])
                link(last)
                v.tensor_scalar(ve[:, 4 * c:4 * c + 4], mv[:, 4 * c:4 * c + 4, 1], 1.0 + RMS_EPS, RMS_EPS * LN_EPS,
                                ALU.mult, ALU.add).then_inc(q2_ready, 1)

            def normalise(c):
                dve.wait_ge(scale_ready, c + 1)
                for i in range(4 * c, 4 * c + 4):
                    last = v.tensor_scalar(hx[:, i, 0, 0:D], x_sb[:, i, :], mv[:, i, 0:1], rs1[:, i:i + 1],
                                           ALU.subtract, ALU.mult)
                last.then_inc(h0_ready, 1)

            dve.wait_ge(yq_ps, 8)
            for i in range(CH + 2):
                if i < CH:
                    glu(i)
                if 0 <= i - 1 < CH:
                    residual(i - 1)
                if 0 <= i - 2 < CH:
                    normalise(i - 2)

            def te(a):
                return a.rearrange("p (i e) -> p i e", e=E)

            def tb(a):
                return a.unsqueeze(2).broadcast_to([P, NT, E])

            lg, gt, oh1, oh2, sc, p2, cntT, incl, slot = rt
            mx, z1, m1_, m2_, r1, gs, g1, g2_ = [c_[:] for c_ in col]
            dve.wait_ge(r_ps, 1)
            dve.wait_ge(rstd_ready, 1)
            link(v.tensor_tensor(te(lg), te(bank[6][:, 0:448]), tb(rstd[:]), ALU.mult))
            link(v.tensor_reduce(mx, te(lg), AX.X, ALU.max))
            v.tensor_tensor(te(lg), te(lg), tb(mx), ALU.subtract).then_inc(lg_ready, 1)
            dve.wait_ge(ex_ready, 1)
            link(v.tensor_reduce(z1, te(gt), AX.X, ALU.add))
            link(v.reciprocal(z1, z1))
            link(v.tensor_tensor(te(gt), te(gt), tb(z1), ALU.mult))
            link(v.tensor_reduce(m1_, te(gt), AX.X, ALU.max))
            link(v.tensor_tensor(te(sc), te(gt), tb(m1_), ALU.is_equal))
            link(v.tensor_tensor(sc, sc, rank_w[:], ALU.mult))
            link(v.tensor_reduce(r1, te(sc), AX.X, ALU.max))
            link(v.tensor_tensor(te(oh1), te(sc), tb(r1), ALU.is_equal))
            link(v.scalar_tensor_tensor(out=p2, in0=oh1, scalar=-2.0, in1=gt, op0=ALU.mult, op1=ALU.add))
            link(v.tensor_reduce(m2_, te(p2), AX.X, ALU.max))
            link(v.tensor_tensor(te(sc), te(p2), tb(m2_), ALU.is_equal))
            link(v.tensor_tensor(sc, sc, rank_w[:], ALU.mult))
            link(v.tensor_reduce(r1, te(sc), AX.X, ALU.max))
            link(v.tensor_tensor(te(oh2), te(sc), tb(r1), ALU.is_equal))
            v.tensor_tensor(p2, oh1, oh2, ALU.add).then_inc(m_ready, 1)
            link(v.scalar_tensor_tensor(out=gs, in0=m1_, scalar=1e-9, in1=m2_, op0=ALU.add, op1=ALU.add))
            link(v.reciprocal(gs, gs))
            dve.wait_ge(hx_ready, CH)
            v.tensor_tensor(hx[:, :, 0, D + 1], m1_, gs, ALU.mult)
            v.tensor_tensor(hx[:, :, 1, D + 1], m2_, gs, ALU.mult).then_inc(gate_ready, 1)

            def add_shared(c):
                dve.wait_ge(so_ps, c + 1)
                rows = x_sb[:, 4 * c:4 * c + 4]
                v.tensor_tensor(rows, bank[4 + c % 2][:].rearrange("p (i d) -> p i d", i=4), rows,
                                ALU.add).then_inc(so_added, 1)

            dve.wait_ge(rank_ps, 1)
            ei = "p (e i) -> p e i"
            link(v.tensor_copy(cntT.rearrange(ei, e=E), te(bank[6][:, 0:448]).rearrange("p i e -> p e i")))
            link(v.tensor_tensor_scan(incl, first[:], cntT, 0.0, ALU.mult, ALU.add))
            nb, cnb, eb, tot = [x_[:] for x_ in e14]
            link(v.tensor_scalar(nb, incl.rearrange(ei, e=E)[:, :, NT - 1], 1.0 / P, (P - 1) / P - 0.5 + 1.0 / (2 * P), ALU.mult, ALU.add))
            link(v.tensor_scalar(nb, nb, MAGIC, None, ALU.add))
            link(v.tensor_scalar(nb, nb, -MAGIC, None, ALU.add))
            link(v.tensor_tensor_scan(cnb, ones[:, 0:E], nb, 0.0, ALU.mult, ALU.add))
            link(v.tensor_tensor(eb, cnb, nb, ALU.subtract))
            link(v.tensor_scalar(eb, eb, float(P), None, ALU.mult))
            link(v.tensor_tensor(incl, incl, cntT, ALU.subtract))
            link(v.tensor_tensor(incl.rearrange(ei, e=E), incl.rearrange(ei, e=E), eb.unsqueeze(2).broadcast_to([P, E, NT]), ALU.add))
            link(v.tensor_tensor(te(slot), te(bank[7][:, 0:448]), incl.rearrange(ei, e=E).rearrange("p e i -> p i e"), ALU.add))
            link(v.tensor_tensor(oh1, oh1, slot, ALU.mult))
            link(v.tensor_tensor(oh2, oh2, slot, ALU.mult))
            v.tensor_reduce(mx, te(oh1), AX.X, ALU.add)
            link(v.tensor_reduce(z1, te(oh2), AX.X, ALU.add))
            v.tensor_copy(pos[:, 0, :], mx)
            v.tensor_copy(pos[:, 1, :], z1).then_inc(pos_ready, 1)
            lb = NBLK + 4
            cmp_ = sg.rearrange("p z m -> p (z m)")[0:1, 0:lb * (E - 1)] if lb * (E - 1) <= 1024 else \
                v2_flat[0:1, 5120:5120 + lb * (E - 1)]
            dve.wait_ge(hT_ready, CH)
            link(v.tensor_tensor(cmp_.rearrange("p (b e) -> p b e", e=E - 1), cnb[0:1, 0:E - 1].unsqueeze(1).broadcast_to([1, lb, E - 1]),
                                 blk[0:1, :].unsqueeze(2).broadcast_to([1, lb, E - 1]), ALU.is_le))
            link(v.tensor_reduce(rt[4][0:1, 0:lb], cmp_.rearrange("p (b e) -> p b e", e=E - 1), AX.X, ALU.add))
            link(v.tensor_scalar(etab[0:1, :], rt[4][0:1, 0:lb], float(HID), None, ALU.mult))
            v.engine_nop().then_inc(etab_ready, 1)
            for c in range(CH):
                add_shared(c)

            dve.wait_ge(o_ps, CH)
            v.engine_nop().then_inc(yb_ready, 2)

            def fetch_w1(at, z):
                r = dve.value_load(etab[0:1, bass.ds(at, 1)], min_val=0, max_val=(E - 1) * HID)
                v.tensor_copy(w1c[:, z % 3], w1_sb.rearrange("p e m -> p (e m)")[:, bass.ds(r, HID)]).then_inc(w1c_ready, 1)

            for z in range(3):
                fetch_w1(z, z)

            def finish_block(n, z):
                dve.wait_ge(yb_ps, n + 4)
                v.tensor_copy(ybi[:, z:z + 1].bitcast(U32), xs[:, z, D:D + 1].bitcast(U32))
                v.tensor_scalar(yb[:, z], bank[4 + z % 2][:, 0:D], xs[:, z, D + 1:D + 2], None,
                                ALU.mult).then_inc(yb_ready, 1)
                dve.wait_ge(hid_ps, n + 5)
                fetch_w1(n + 4, z + 1)

            dve.wait_ge(hid_ps, 4)
            fetch_w1(3, 3)
            for z in range(STEP):
                finish_block(z, z)
            with dve.Fori(1, NBLK // STEP) as it:
                for z in range(STEP):
                    dve.wait_ge(yb_out[z], it * 16)
                    finish_block(it * STEP + z, z)
            for g in range(4):
                rows = slice(8 * g, 8 * g + 8)
                dve.wait_ge(y_in[g], 16)
                link(v.tensor_tensor(x_sb[:, rows], x_sb[:, rows], yl[:, rows, 0:D], ALU.add))
                v.tensor_tensor(x_sb[:, rows], x_sb[:, rows], yl[:, rows, D:2 * D], ALU.add).then_inc(sum_ready, 1)

        @block.scalar
        def _(act):
            a = nc.scalar
            steps = [0]

            def link(ins):
                steps[0] += 1
                ins.then_inc(act_step, 1)
                act.wait_ge(act_step, steps[0])

            act.dma_start(wnat[:, 0, :], in_w).then_inc(w_in, 16)
            act.dma_start(wnat[:, 1:3, :], glu_w.rearrange("(c p) h -> p c h", p=P)).then_inc(w_in, 16)
            act.dma_start(wnat[:, 3, :], out_w).then_inc(w_in, 16)
            act.dma_start(inb_bc[:], in_b.partition_broadcast(P)).then_inc(b_in, 16)
            act.dma_start(outb_bc[:], out_b.partition_broadcast(P)).then_inc(b_in, 16)
            act.dma_start(glub[:], glu_b.rearrange("(c p) -> p c", p=P), allow_slow_non_contiguous=True).then_inc(b_in, 16)
            act.dma_start(rmsn[0:E, :], rms_w).then_inc(rms_in, 16)
            act.dma_start(rmsn[E:EA, :], rms_ws).then_inc(rms_in, 16)
            act.dma_start(rw[:], router_w).then_inc(rms_in, 16)
            act.wait_ge(xinit_ready, 1)
            act.dma_start(xs_dram.ap().rearrange("(b p) c -> p b c", p=P),
                          xinit[:].unsqueeze(1).broadcast_to([P, NROW // P, ROW])).then_inc(xs_cleared, 16)
            act.dma_start(dskip[:], d_skip.rearrange("(g p) -> p g", p=HG), allow_slow_non_contiguous=True).then_inc(b_in, 16)

            def evict_xnT(i):
                act.wait_ge(xnT_ps, i + 1)
                if i >= 2:
                    act.wait_ge(u_ps, i - 1)
                a.copy(xnT[:, i % 2, :], bank[i % 2][:]).then_inc(xnT_ready, 1)

            act.wait_ge(const_ready, 1)
            act.wait_ge(ab_ready, 1)
            a.activation(mag128[:], ab[:, 0, :], ACT.Exp, scale=float(P))
            act.wait_ge(wT_ps, 1)
            a.copy(wT[:].rearrange("p c m -> p (c m)"), bank[4][:]).then_inc(wT_ready, 1)

            def magnitude(g):
                act.wait_ge(abb_in[g % 2], 16 * (g // 2 + 1))
                a.activation(mag[:, g].rearrange("p (h n) -> p h n", h=HG), abb[:, g % 2, :, 0:N], ACT.Exp,
                             scale=srow[:, 0:1]).then_inc(mag_ready, 1)

            for i in range(2):
                evict_xnT(i)
            magnitude(0)
            for i in range(2, 4):
                evict_xnT(i)
            magnitude(1)
            magnitude(2)
            magnitude(3)
            act.wait_ge(turns_ready, 1)
            a.activation(sn[:], fr[:], ACT.Sin, scale=TWO_PI)
            a.activation(cs128[:], frq[:, 1, :], ACT.Sin, scale=-TWO_PI, bias=halfpi[:])
            a.activation(sh[:], fr[:, 0, :], ACT.Sin, scale=TWO_PI / 2).then_inc(psin_ready, 1)

            def sines(g):
                act.wait_ge(arg_ready, g + 1)
                a.activation(trig[:, g % 2, 1], trig[:, g % 2, 1], ACT.Sin, scale=TWO_PI)
                a.activation(trig[:, g % 2, 0], trig[:, g % 2, 0], ACT.Sin, scale=-TWO_PI,
                             bias=halfpi[:]).then_inc(trig_ready, 1)

            sines(0)
            sines(1)
            for i in range(4, 8):
                evict_xnT(i)
            sines(2)
            sines(3)
            act.wait_ge(q_ps, 1)
            for k in range(4):
                for q, to in enumerate((0, 3, 1, 5)):
                    last = a.copy(lw[32 * k:32 * k + 32, to, :], bank[0][32 * q:32 * q + 32, k:P:4])
            last.then_inc(lw_act, 1)
            for i in range(16):
                if evict_v2_by_act(i):
                    act.wait_ge(v2_ps, i + 1)
                    a.copy(v2[:, 4 * i:4 * i + 4, :], bank[4 + i % 4][:]
                           .rearrange("p (q s) -> p q s", q=4)).then_inc(v2_act, 1)
            for half in range(2):
                act.wait_ge(b_ps, 4 * half + 4)
                for m in range(2):
                    k = 2 * m
                    for r in range(2):
                        for q in range(4):
                            src = bank[4 * half + q][32 * r:32 + 32 * r].rearrange(
                                "p (j m e c) -> p j m e c", j=4, m=2, e=2)[:, :, m, 0, :]
                            last = a.copy(st[32 * k:32 * k + 32, r, 16 * half + 4 * q:16 * half + 4 * q + 4, :], src)
                last.then_inc(b_act, 1)
            act.wait_ge(mul_ready, 1)
            act.wait_ge(sbd_zero, 1)
            for m in range(2):
                k = 2 * m
                for r in range(2):
                    for b in range(B):
                        dst = s_bd[32 * r:32 + 32 * r, m::2, 0, NC * b + 1:NC * b + NC]
                        src = mul1[32 * k:32 * k + 32, r, :, NC * b:NC * b + NC - 1]
                        last = a.copy(dst, src)
            last.then_inc(sbd_act, 1)
            act.wait_ge(t0_ps, 3)
            act.dma_start(w1_sb[:, 0:E], w1.rearrange("e p m -> p e m")).then_inc(ew_in, 16)
            act.dma_start(w1_sb[:, E:EA], w1s.rearrange("e p m -> p e m")).then_inc(ew_in, 16)
            act.wait_ge(sbd_dve, 1)
            act.wait_ge(sbd_act, 1)
            for c in range(HC):
                act.dma_start(w2_sb[:, 0:E, c], w2.rearrange("e (c p) d -> c p e d", c=HC)[c]).then_inc(ew2_in, 16)
                act.dma_start(w2_sb[:, E:EA, c], w2s.rearrange("e (c p) d -> c p e d", c=HC)[c]).then_inc(ew2_in, 16)
            act.wait_ge(t0_ps, 4)
            for i in range(8):
                act.wait_ge(y_ps, i + 1)
                a.activation(yq[:, 512 * i:512 * i + 512], bank[i][:], ACT.Gelu).then_inc(yq_ready, 1)
            for i in range(0, 8, 2):
                act.wait_ge(yq_ps, i + 1)
                a.copy(y_tiles(i), bank[i][:].rearrange("p (x k c) -> p c x k", x=4, k=4)).then_inc(y_ready, 1)


            def copy_yT(c):
                act.wait_ge(yT_ps, c + 1)
                if c >= 2:
                    act.wait_ge(ag_ps, c - 1)
                a.copy(yT[:, c % 2], bank[c % 2][:]).then_inc(yT_ready, 1)

            def gate_glu(c):
                act.wait_ge(ag_ps, c + 1)
                if c >= 2:
                    act.wait_ge(aT_ready, c - 1)
                a.activation(sg[:, c % 2], bank[3][:], ACT.Sigmoid, bias=glub[:, 1:2]).then_inc(sg_ready, 1)

            copy_yT(0)
            for i in range(CH + 3):
                if i < CH:
                    gate_glu(i)
                if i + 1 < CH:
                    copy_yT(i + 1)
                if 0 <= i - 3 < CH:
                    c = i - 3
                    act.wait_ge(hT_ps, c + 1)
                    a.copy(h0T[:, 512 * c:512 * c + 512], bank[5][:]).then_inc(hT_ready, 1)
            act.wait_ge(lg_ready, 1)
            a.activation(rt[1], rt[0], ACT.Exp).then_inc(ex_ready, 1)
            for c in range(CH):
                for e in range(ES * HC):
                    act.wait_ge(sh_ps, 4 * c + e + 1)
                    if c >= 2 and e == 0:
                        act.wait_ge(so_ps, c - 1)
                    a.activation(ysh[:, c % 2, e], bank[e][:], ACT.Silu).then_inc(sh_ready, 1)
            a.nop().then_inc(xt_ready, 2)
            a.nop().then_inc(act_ready, 2)

            def copy_xsT(n, z):
                act.wait_ge(xt_ps, n + 1)
                act.wait_ge(hid_ps, n + 1)
                a.copy(xsT[:, z % 3], bank[z % 2][:, 0:P]).then_inc(xt_ready, 1)

            def silu(n, z):
                act.wait_ge(hid_ps, n + 4)
                act.wait_ge(yb_ps, n + 1)
                a.activation(act_sb[:, z % 3], bank[2 + z % 2][:, 0:HID], ACT.Silu).then_inc(act_ready, 1)

            copy_xsT(0, 0)
            copy_xsT(1, 1)
            copy_xsT(2, 2)
            silu(0, 0)
            silu(1, 1)
            with act.Fori(0, NBLK // STEP) as it:
                for z in range(STEP):
                    copy_xsT(it * STEP + (z + 3), z + 3)
                    silu(it * STEP + (z + 2), z + 2)

        @block.tensor
        def _(pe):
            mm, tr = nc.tensor.matmul, nc.tensor.transpose
            pe.wait_ge(const_ready, 1)
            pe.wait_ge(w_in, 48)
            for c in range(4):
                last = tr(bank[4][:, P * c:P * c + P], wnat[:, c, :], ident[:])
            last.then_inc(wT_ps, 1)

            def turn_xn(i):
                if i % 2 == 0:
                    pe.wait_ge(xn_ready, i // 2 + 1)
                if i >= 2:
                    pe.wait_ge(xnT_ready, i - 1)
                for c in range(4):
                    last = mm(bank[i % 2][:, P * c:P * c + P], xn[:, 4 * i + c, :], exch[:], start=True, stop=True)
                last.then_inc(xnT_ps, 1)

            def project_in(i):
                pe.wait_ge(xnT_ready, i + 1)
                if i == 0:
                    pe.wait_ge(wT_ready, 1)
                if i >= 2:
                    pe.wait_ge(u_ready, i - 1)
                for c in range(4):
                    last = mm(bank[2 + i % 2][:, P * c:P * c + P], xnT[:, i % 2, P * c:P * c + P], wT[:, 0, :],
                              start=True, stop=True)
                last.then_inc(u_ps, 1)

            turn_xn(0)
            for i in range(8):
                if i + 1 < 8:
                    turn_xn(i + 1)
                project_in(i)
            pe.wait_ge(q_ready, 1)
            pe.wait_ge(xnT_ready, 8)
            pe.wait_ge(u_ready, 8)
            tr(bank[0][:, 0:P], q1[:].rearrange("p q n -> p (q n)"), ident[:])
            tr(bank[3][0:64, 0:P], q2[:].rearrange("p q n -> p (q n)"), ident[:]).then_inc(q_ps, 1)

            for g in range(NG):
                pe.wait_ge(v1_ready, g + 1)
                for i in range(4 * g, 4 * g + 4):
                    if i >= 4:
                        pe.wait_ge(v2_act if evict_v2_by_act(i - 4) else v2_dve, (i - 4) // 2 + 1)
                    else:
                        pe.wait_ge(wT_ready, 1)
                    for q in range(4):
                        p = 4 * i + q
                        last = tr(bank[4 + i % 4][:, P * q:P * q + P], v1[:, 2 * p:2 * p + 2].rearrange("p h r n -> p (h r n)"), ident[:])
                    last.then_inc(v2_ps, 1)
                if g == 0:
                    pe.wait_ge(cbig_ready, 1)
                if g >= 2:
                    pe.wait_ge(k_ready, g - 1)
                pe.wait_ge(v2_act, 2 * g + 2)
                pe.wait_ge(v2_dve, 2 * g + 2)
                for j in range(PG):
                    last = mm(bank[1 + g % 2][0:HG, 0:P], cbig[:, g, 32 * j:32 * j + 32], v2[:, PG * g + j, :],
                              start=(j == 0), stop=(j == PG - 1))
                last.then_inc(k_ps, 1)

            pe.wait_ge(u_ready, 8)
            pe.wait_ge(lw_act, 1)
            pe.wait_ge(k_ready, NG)
            for i in range(8):
                for q in range(8):
                    p = 8 * i + q
                    last = mm(bank[i][:, 64 * q:64 * q + 64], v1[:, 2 * p:2 * p + 2].rearrange("p h r n -> p (h r n)"),
                              u[:, 2 * p:2 * p + 2, :].rearrange("p h c -> p (h c)"), start=True, stop=True)
                last.then_inc(b_ps, 1)

            pe.wait_ge(b_act, 2)
            pe.wait_ge(b_dve, 2)
            for g in range(NG):
                pe.wait_ge(hank_in[g], 16)
                for q in range(HG):
                    h = HG * g + q
                    k, x_ = h % 4, h // 4
                    last = mm(bank[x_ // 4][32 * k:32 * k + 32, P * (x_ % 4):P * (x_ % 4) + P], u[:, h, :], hank[g][:, q, :],
                              start=(x_ % 4 == 0), stop=False, skip_group_check=True)
                last.then_inc(t0_ps, 1)
            pe.wait_ge(sbd_act, 1)
            pe.wait_ge(sbd_dve, 1)
            for p in range(NPAIR):
                m, x_ = p % 2, p // 2
                last = mm(bank[x_ // 4][64 * m:64 * m + 64, P * (x_ % 4):P * (x_ % 4) + P],
                          s_bd[:, p].rearrange("p e c -> p (e c)"), v2[:, p, :],
                          start=False, stop=(x_ % 4 == 3), skip_group_check=True)
                if p % 8 == 7:
                    last.then_inc(y_ps, 1)
            for i in range(8):
                pe.wait_ge(yq_ready, i + 1)
                for q in range(4):
                    last = tr(bank[i][:, P * q:P * q + P], yq[:, 512 * i + P * q:512 * i + P * q + P], ident[:])
                last.then_inc(yq_ps, 1)

            pe.wait_ge(rms_in, 48)
            pe.wait_ge(y_ready, 4)
            pe.wait_ge(y_dve, 4)
            tr(bank[0][:, 0:EA], rmsn[:], ident[0:EA, 0:EA]).then_inc(rms_ps, 1)

            def turn_y(c):
                if c >= 2:
                    pe.wait_ge(yT_ready, c - 1)
                if c == 0:
                    pe.wait_ge(w1_ready, 1)
                for q in range(4):
                    last = tr(bank[c % 2][:, P * q:P * q + P], y_sb[:, 4 * c + q, :], ident[:])
                last.then_inc(yT_ps, 1)

            def glu_products(c):
                pe.wait_ge(yT_ready, c + 1)
                pe.wait_ge(aT_ready, c) if c else None
                mm(bank[2][:], wT[:, 1, :], yT[:, c % 2], start=True, stop=True)
                mm(bank[3][:], wT[:, 2, :], yT[:, c % 2], start=True, stop=True).then_inc(ag_ps, 1)

            def project_out(c):
                pe.wait_ge(aT_ready, c + 1)
                if c:
                    pe.wait_ge(x2_ready, c)
                for q in range(4):
                    last = mm(bank[4][:, P * q:P * q + P], aT[:, c % 2, P * q:P * q + P], wT[:, 3, :], start=True, stop=True)
                last.then_inc(o_ps, 1)

            def turn_h0(c):
                pe.wait_ge(h0_ready, c + 1)
                if c:
                    pe.wait_ge(hT_ready, c)
                for q in range(4):
                    last = tr(bank[5][:, P * q:P * q + P], hx[:, 4 * c + q, 0, 0:D], ident[:])
                last.then_inc(hT_ps, 1)

            def route(c):
                pe.wait_ge(hT_ready, c + 1)
                for i in range(4 * c, 4 * c + 4):
                    last = mm(bank[6][:, E * i:E * i + E], h0T[:, P * i:P * i + P], rw[:], start=True, stop=True)
                if c == CH - 1:
                    last.then_inc(r_ps, 1)

            turn_y(0)
            for i in range(CH + 4):
                if i < CH:
                    glu_products(i)
                if i + 1 < CH:
                    turn_y(i + 1)
                if 0 <= i - 1 < CH:
                    project_out(i - 1)
                if 0 <= i - 3 < CH:
                    turn_h0(i - 3)
                if 0 <= i - 4 < CH:
                    route(i - 4)

            def shared_in(c):
                for e in range(ES * HC):
                    if c:
                        pe.wait_ge(sh_ready, 4 * c - 4 + e + 1)
                    mm(bank[e][:], w1_sb[:, E + e // HC, P * (e % HC):P * (e % HC) + P], h0T[:, 512 * c:512 * c + 512],
                       start=True, stop=True).then_inc(sh_ps, 1)

            def shared_out(c):
                pe.wait_ge(sh_ready, 4 * c + 4)
                if c == 0:
                    pe.wait_ge(ew2_in, 16 * 2 * HC)
                    pe.wait_ge(x2_ready, CH)
                if c >= 2:
                    pe.wait_ge(so_added, c - 1)
                for q in range(4):
                    for e in range(ES * HC):
                        last = mm(bank[4 + c % 2][:, P * q:P * q + P], ysh[:, c % 2, e, P * q:P * q + P],
                                  w2_sb[:, E + e // HC, e % HC, :], start=(e == 0), stop=(e == ES * HC - 1))
                last.then_inc(so_ps, 1)

            shared_in(0)
            shared_in(1)
            shared_out(0)
            pe.wait_ge(m_ready, 1)
            mm(bank[6][:, 0:448], ones[:], rt[5], start=True, stop=True)
            mm(bank[7][:, 0:448], upper[:], rt[5], start=True, stop=True).then_inc(rank_ps, 1)
            for c in range(1, CH):
                if c + 1 < CH:
                    shared_in(c + 1)
                shared_out(c)

            pe.nop().then_inc(hid_ps, 3)
            pe.nop().then_inc(yb_ps, 3)
            pe.wait_ge(sh_ready, 4 * CH)
            pe.wait_ge(so_added, CH)
            pe.wait_ge(etab_ready, 1)

            def turn_rows(n, it, z):
                pe.wait_ge(xs_in[z % STEP], it * 16 + 16)
                pe.wait_ge(xt_ready, n + 1)
                tr(bank[z % 2][:, 0:P], xs[:, z % STEP, 0:D], ident[:]).then_inc(xt_ps, 1)

            def first_matrix(n, z):
                pe.wait_ge(xt_ready, n + 3)
                pe.wait_ge(w1c_ready, n + 1)
                pe.wait_ge(act_ready, n + 1)
                for c in range(HC):
                    last = mm(bank[2 + z % 2][:, P * c:P * c + P], w1c[:, z % 3, P * c:P * c + P], xsT[:, z % 3],
                              start=True, stop=True)
                last.then_inc(hid_ps, 1)

            def second_matrix(n, z):
                r = pe.value_load(etab[0:1, bass.ds(n, 1)], min_val=0, max_val=(E - 1) * HID)
                pe.wait_ge(act_ready, n + 3)
                pe.wait_ge(yb_ready, n + 1)
                w2_flat = w2_sb.rearrange("p e c d -> p (e c d)")
                for c in range(HC):
                    last = mm(bank[4 + z % 2][:, 0:D], act_sb[:, z % 3, P * c:P * c + P], w2_flat[:, bass.ds(r + P * c, D)],
                              start=(c == 0), stop=(c == HC - 1))
                last.then_inc(yb_ps, 1)

            turn_rows(0, 0, 0)
            turn_rows(1, 0, 1)
            turn_rows(2, 0, 2)
            first_matrix(0, 0)
            first_matrix(1, 1)
            with pe.Fori(0, NBLK // STEP) as it:
                for z in range(STEP):
                    turn_rows(it * STEP + (z + 3), it + (z + 3) // STEP, z + 3)
                    first_matrix(it * STEP + (z + 2), z + 2)
                    second_matrix(it * STEP + z, z)


_INS = ['L0_attn_x', 'L0_attn_in_W', 'L0_attn_in_b', 'L0_attn_log_dt', 'L0_attn_C', 'L0_attn_log_A_real',
        'L0_attn_A_imag', 'L0_attn_D_skip', 'L0_attn_glu_W', 'L0_attn_glu_b', 'L0_attn_out_W', 'L0_attn_out_b',
        'L0_ffn_router_w', 'L0_ffn_rms_w', 'L0_ffn_w1', 'L0_ffn_w2', 'L0_ffn_rms_w_s', 'L0_ffn_w1_s', 'L0_ffn_w2_s']


def kernel(**inputs):
    import concourse.bacc as bacc
    from concourse.bass_utils import run_bass_kernel_spmd

    nc = bacc.Bacc("TRN2", target_bir_lowering=False, num_devices=1)
    arrays, args = {}, []
    for name in _INS:
        a = np.ascontiguousarray(inputs[name])
        arrays[f"in_{name}"] = a
        args.append(nc.dram_tensor(f"in_{name}", a.shape, mybir.dt.from_np(a.dtype), kind="ExternalInput").ap())
    out = nc.dram_tensor("out_x", (2, 2048, 128), F32, kind="ExternalOutput").ap()
    build_kernel(nc, *args, out)
    r = run_bass_kernel_spmd(nc, [arrays], core_ids=[0])
    return r.results[0]["out_x"]
```

```python
from contextlib import ExitStack

import numpy as np

import concourse.bass as bass
from concourse import mybir

F32 = mybir.dt.float32
U32 = mybir.dt.uint32
ALU = mybir.AluOpType
ACT = mybir.ActivationFunctionType
AX = mybir.AxisListType

P = 128
LN_EPS = 1e-5
RMS_EPS = 1.1920929e-07
PI = float(np.pi)
MAGIC = 12582912.0
LOG2E = float(np.log2(np.e))
LN2_HI = 0.693359375
LN2_LO = float(np.log(2.0) - 0.693359375)
TWO_PI = 6.2831850
FACT = [1.0, 1.0, 2.0, 6.0, 24.0, 120.0, 720.0, 5040.0, 40320.0, 362880.0]


def build_kernel(nc, x, in_w, in_b, log_dt, c_par, log_a, a_imag, d_skip, glu_w, glu_b,
                 out_w, out_b, router_w, rms_w, w1, w2, rms_ws, w1s, w2s, out):
    B, L, D = x.shape
    N = a_imag.shape[1]
    NT = B * L // P
    NC = L // P
    NPAIR = D // 2
    NG, HG = 4, D // 4
    PG = HG // 2
    NX = D // 4
    E, ES, HID = w1.shape[0], w1s.shape[0], w1.shape[2]
    EA, HC = E + ES, HID // P
    TOKENS = B * L
    ROUTES = 2 * TOKENS
    STEP = 6
    NBLK = -(-(ROUTES // P + E - 1) // STEP) * STEP
    UNROLL = 2 * STEP
    LOOPS = (NBLK - STEP) // UNROLL
    LOADS = NBLK - STEP + UNROLL
    NROW = LOADS * P
    ROW = D + 2
    NOWHERE = 1 << 20
    CH = NT // 4
    assert (NBLK - STEP) % UNROLL == 0 and (B, L, D, N) == (2, 2048, 128, 32) and (E, ES, HID) == (14, 2, 256)

    ctx = ExitStack()
    with ctx:
        def sb(name, shape, dt=F32):
            return ctx.enter_context(nc.sbuf_tensor(name, shape, dt))

        def sem(name):
            return ctx.enter_context(nc.semaphore(name))

        bank = [ctx.enter_context(nc.psum_tensor(f"bank{i}", [P, 512], F32)) for i in range(8)]

        x_sb = sb("x_sb", [P, NT, D])
        xn = sb("xn", [P, NT, D])
        xnT = sb("xnT", [P, 2, 512])
        u = sb("u", [P, D, NT])
        v1 = sb("v1", [P, D, 2, N])
        v2 = sb("v2", [P, NPAIR, P])
        area = sb("area", [P, 13312])
        v2_flat = v2[:].rearrange("p q s -> p (q s)")
        abb = [a_.rearrange("p (h c) -> p h c", h=HG) for a_ in
               (area[:, 0:2048], area[:, 2048:4096], v2_flat[:, 3584:5632], v2_flat[:, 5632:7680])]
        mag = area[:, 4096:8192].rearrange("p (g m) -> p g m", g=NG)
        trig = area[:, 8192:12288].rearrange("p (z r m) -> p z r m", z=2, r=2)
        rnd = area[:, 12288:13312]
        s_bd = area[:, 8192:12288].rearrange("p (q e c) -> p q e c", q=NPAIR, e=2)
        st = sb("st", [P, 2, NX, NT])
        v1_flat = v1[:].rearrange("p h r n -> p (h r n)")
        xn_flat = xn[:].rearrange("p i d -> p (i d)")
        hank = [h_.rearrange("p (h t) -> p h t", h=HG)
                for h_ in (area[:, 0:4096], area[:, 4096:8192], v1_flat[:, 4096:8192], xn_flat)]
        yq = area[:, 0:4096]
        mul1 = v1_flat[:, 0:2048].rearrange("p (r x t) -> p r x t", r=2, x=NX)
        mul2 = v1_flat[:, 2048:4096].rearrange("p (r x t) -> p r x t", r=2, x=NX)
        y_sb = xn
        w1_sb = v1_flat[:, 4096:8192].rearrange("p (e m) -> p e m", e=EA)
        w2_sb = v1_flat[:, 0:4096].rearrange("p (e c d) -> p e c d", e=EA, c=HC)
        h0T = v2_flat[:, 0:4096]
        yT = v2_flat[:, 4096:5120].rearrange("p (z m) -> p z m", z=2)
        aT = v2_flat[:, 5120:6144].rearrange("p (z m) -> p z m", z=2)
        sg = v2_flat[:, 6144:7168].rearrange("p (z m) -> p z m", z=2)
        hx = area[:, 0:NT * 2 * ROW].rearrange("p (i k c) -> p i k c", i=NT, k=2)
        ysh = xn[:].rearrange("p i d -> p (i d)").rearrange("p (z e m) -> p z e m", z=2, e=ES * HC)
        u_flat = u[:].rearrange("p h c -> p (h c)")
        rt = [u_flat[:, 448 * i:448 * i + 448] for i in range(9)]
        xs = area[:, NT * 2 * ROW:NT * 2 * ROW + UNROLL * ROW].rearrange("p (z c) -> p z c", z=UNROLL)
        xsT = v2_flat[:, 0:384].rearrange("p (z c) -> p z c", z=3)
        act_sb = v2_flat[:, 384:1152].rearrange("p (z c) -> p z c", z=3)
        yb = v2_flat[:, 1152:1152 + STEP * D].rearrange("p (z c) -> p z c", z=STEP)
        wc = v2_flat[:, 5120:8192].rearrange("p (z w c) -> p z w c", z=STEP, w=2)
        yl = area[:, 0:8192].rearrange("p (i m) -> p i m", i=NT)

        ident = sb("ident", [P, P])
        exch = sb("exch", [P, P])
        srow = sb("srow", [P, 1])
        halfpi = sb("halfpi", [P, 1])
        mhalf = sb("mhalf", [P, NT])
        inb_bc = sb("inb_bc", [P, D])
        outb_bc = sb("outb_bc", [P, D])
        glub = sb("glub", [P, 2])
        dskip = sb("dskip", [HG, NG])
        wnat = v2[:, NPAIR - 4:NPAIR, :]
        wT = sb("wT", [P, 4, P])

        p33 = sb("p33", [P, N + 1])
        z33 = sb("z33", [P, N + 1])
        r33 = sb("r33", [P, N + 1])
        q33 = sb("q33", [P, N + 1])
        e33 = sb("e33", [P, N + 1])
        aim = sb("aim", [P, N])
        cpar = sb("cpar", [P, N, 2])
        ab = sb("ab", [P, 2, N])
        fr = sb("fr", [P, 2, N])
        frq = sb("frq", [P, 2, N])
        sn = sb("sn", [P, 2, N])
        cs128 = sb("cs128", [P, N])
        sh = sb("sh", [P, N])
        mag128 = sb("mag128", [P, N])
        em = sb("em", [P, N])
        ey = sb("ey", [P, N])
        inv = sb("inv", [P, N])
        den = sb("den", [P, N])
        t = [sb(f"t{i}", [P, N]) for i in range(8)]
        q1 = sb("q1", [P, 4, N])
        q2 = sb("q2", [P, 2, N])
        lw = sb("lw", [P, 6, NX])
        cbig = st[:].rearrange("p r x c -> p (r x c)").rearrange("p (g m) -> p g m", g=NG)
        ksb = sb("ksb", [HG, NG, 256])
        stats = sb("stats", [P, NT, 6])
        mv = sb("mv", [P, NT, 2])
        ve = sb("ve", [P, NT])
        rs0 = sb("rs0", [P, NT])
        rs1 = sb("rs1", [P, NT])
        rstd = sb("rstd", [P, NT])

        upper = sb("upper", [P, P])
        ones = sb("ones", [P, P])
        rank_w = sb("rank_w", [P, 448])
        first = sb("first", [P, 448])
        blk = sb("blk", [P, NBLK + STEP])
        xinit = sb("xinit", [P, ROW])
        rw = sb("rw", [P, E])
        rmsn = sb("rmsn", [EA, P])
        rmsT = sb("rmsT", [P, EA])
        ybi = sb("ybi", [P, STEP])
        col = [sb(f"col{i}", [P, NT]) for i in range(8)]
        e14 = [sb(f"e14_{i}", [P, E]) for i in range(4)]
        pos = sb("pos", [P, 2, NT], U32)
        etab = sb("etab", [P, NBLK + STEP], U32)

        xs_dram = nc.dram_tensor("xs_dram", [NROW, ROW], F32, kind="Internal")
        y_dram = nc.dram_tensor("y_dram", [ROUTES, D], F32, kind="Internal")
        ab_dram = nc.dram_tensor("ab_dram", [D, 2 * N], F32, kind="Internal")
        kp_dram = nc.dram_tensor("kp_dram", [D, 256], F32, kind="Internal")

        par_in = sem("par_in")
        x_in = [sem(f"x_in{g}") for g in range(4)]
        w_in = sem("w_in")
        b_in = sem("b_in")
        const_ready = sem("const_ready")
        pool_step = sem("pool_step")
        dve_step = sem("dve_step")
        act_step = sem("act_step")
        ab_ready = sem("ab_ready")
        ab_out = sem("ab_out")
        abb_in = [sem(f"abb_in{g}") for g in range(NG)]
        abb_used = sem("abb_used")
        turns_ready = sem("turns_ready")
        psin_ready = sem("psin_ready")
        em_ready = sem("em_ready")
        var_ready = sem("var_ready")
        rs_ready = sem("rs_ready")
        xn_ready = sem("xn_ready")
        wT_ps = sem("wT_ps")
        wT_ready = sem("wT_ready")
        xnT_ps = sem("xnT_ps")
        xnT_ready = sem("xnT_ready")
        u_ps = sem("u_ps")
        u_ready = sem("u_ready")
        r0_ready = sem("r0_ready")
        mag_ready = sem("mag_ready")
        arg_ready = sem("arg_ready")
        trig_ready = sem("trig_ready")
        trig_used = sem("trig_used")
        v1_dve = sem("v1_dve")
        v1_pool = sem("v1_pool")
        v2_ps = sem("v2_ps")
        v2_act = sem("v2_act")
        v2_dve = sem("v2_dve")
        q_ready = sem("q_ready")
        q_ps = sem("q_ps")
        lw_act = sem("lw_act")
        cbig_ready = sem("cbig_ready")
        cbig_zero = sem("cbig_zero")
        k_ps = sem("k_ps")
        k_ready = sem("k_ready")
        kp_out = [sem(f"kp_out{g}") for g in range(NG)]
        hank_in = [sem(f"hank_in{g}") for g in range(NG)]
        t0_ps = sem("t0_ps")
        b_ps = sem("b_ps")
        b_act = sem("b_act")
        b_dve = sem("b_dve")
        sbd_zero = sem("sbd_zero")
        mul_ready = sem("mul_ready")
        sbd_act = sem("sbd_act")
        sbd_dve = sem("sbd_dve")
        y_ps = sem("y_ps")
        yq_ready = sem("yq_ready")
        yq_ps = sem("yq_ps")
        y_dve = sem("y_dve")
        y_ready = sem("y_ready")
        xinit_ready = sem("xinit_ready")
        xs_cleared = sem("xs_cleared")
        ew_in = sem("ew_in")
        ew2_in = sem("ew2_in")
        rms_in = sem("rms_in")
        rms_ps = sem("rms_ps")
        w1_ready = sem("w1_ready")
        yT_ps = sem("yT_ps")
        yT_ready = sem("yT_ready")
        ag_ps = sem("ag_ps")
        sg_ready = sem("sg_ready")
        aT_ready = sem("aT_ready")
        o_ps = sem("o_ps")
        x2_ready = sem("x2_ready")
        q2_ready = sem("q2_ready")
        scale_ready = sem("scale_ready")
        h0_ready = sem("h0_ready")
        ids_ready = sem("ids_ready")
        hx_ready = sem("hx_ready")
        hT_ps = sem("hT_ps")
        hT_ready = sem("hT_ready")
        r_ps = sem("r_ps")
        rstd_ready = sem("rstd_ready")
        lg_ready = sem("lg_ready")
        ex_ready = sem("ex_ready")
        m_ready = sem("m_ready")
        rank_ps = sem("rank_ps")
        gate_ready = sem("gate_ready")
        pos_ready = sem("pos_ready")
        sh_ps = sem("sh_ps")
        sh_ready = sem("sh_ready")
        so_ps = sem("so_ps")
        so_added = sem("so_added")
        rows_out = sem("rows_out")
        xs_in = [sem(f"xs_in{z}") for z in range(UNROLL)]
        pool_turn = sem("pool_turn")
        xt_ps = sem("xt_ps")
        xt_ready = sem("xt_ready")
        wc_ready = sem("wc_ready")
        hid_ps = sem("hid_ps")
        act_ready = sem("act_ready")
        yb_ps = sem("yb_ps")
        yb_ready = sem("yb_ready")
        yb_out = [sem(f"yb_out{z}") for z in range(STEP)]
        y_in = [sem(f"y_in{g}") for g in range(4)]
        sum_ready = sem("sum_ready")
        out_done = sem("out_done")

        x_tok = x.rearrange("b (c p) d -> p (b c) d", p=P)

        def evict_v2_by_act(i):
            return i % 2 == 0

        def table_product(engine, g, r):
            return engine.tensor_tensor(v1[:, g * HG:(g + 1) * HG, r], mag[:, g].rearrange("p (h n) -> p h n", h=HG),
                                        trig[:, g % 2, r].rearrange("p (h n) -> p h n", h=HG), ALU.mult)

        def y_tiles(i):
            return y_sb[:, :, 16 * i:16 * i + 16].rearrange("p c (x k) -> p c x k", k=4)

        block = ctx.enter_context(nc.Block())

        @block.sync
        def _(sp):
            sp.dma_start(p33[:, 0:1], log_dt.rearrange("(h o) -> h o", o=1)).then_inc(par_in, 16)
            sp.dma_start(p33[:, 1:N + 1], log_a).then_inc(par_in, 16)
            sp.dma_start(aim[:], a_imag).then_inc(par_in, 16)
            sp.dma_start(cpar[:], c_par).then_inc(par_in, 16)
            for g in range(4):
                sp.dma_start(x_sb[:, 8 * g:8 * g + 8, :], x_tok[:, 8 * g:8 * g + 8, :]).then_inc(x_in[g], 16)
            sp.wait_ge(ab_ready, 1)
            sp.dma_start(ab_dram.ap(), ab[:].rearrange("p a n -> p (a n)")).then_inc(ab_out, 16)
            sp.wait_ge(ab_out, 16)
            for g in range(NG):
                src = bass.AP(ab_dram, g * HG * 2 * N, [[0, P], [1, HG * 2 * N]])
                sp.dma_start(abb[g].rearrange("p h c -> p (h c)"), src).then_inc(abb_in[g], 16)
            for g in range(NG):
                sp.wait_ge(k_ready, g + 1)
                sp.dma_start(kp_dram.ap()[g * HG:(g + 1) * HG, :], ksb[:, g, :]).then_inc(kp_out[g], 16)
                sp.wait_ge(kp_out[g], 16)
                if g < 2:
                    sp.wait_ge(mag_ready, NG)
                    sp.wait_ge(abb_used, NG)
                    sp.wait_ge(v1_dve, NG)
                    sp.wait_ge(v1_pool, NG)
                if g == 2:
                    sp.wait_ge(b_ps, 8)
                if g == 3:
                    sp.wait_ge(r0_ready, 4)
                    sp.wait_ge(xnT_ps, 8)
                src = bass.AP(kp_dram, g * HG * 256, [[1, P], [256, HG], [1, P]])
                sp.dma_start(hank[g], src).then_inc(hank_in[g], 16)
            sp.wait_ge(xinit_ready, 1)
            sp.dma_start(xs_dram.ap().rearrange("(b p) c -> p b c", p=P),
                         xinit[:].unsqueeze(1).broadcast_to([P, NROW // P, ROW])).then_inc(xs_cleared, 16)
            xs_rows = xs_dram.ap().rearrange("(b p) c -> p b c", p=P)
            sp.wait_ge(rows_out, 16 * 2 * NT)
            for z in range(UNROLL):
                sp.dma_start(xs[:, z, :], xs_rows[:, z, :]).then_inc(xs_in[z], 16)
            with sp.Fori(0, LOOPS) as it:
                for z in range(UNROLL):
                    sp.wait_ge(yb_ready, it * UNROLL + (z + 1 + 2))
                    sp.dma_start(xs[:, z, :], xs_rows[:, bass.ds(it * UNROLL + (UNROLL + z), 1), :]
                                 .rearrange("p b c -> p (b c)")).then_inc(xs_in[z], 16)
            y_tok = y_dram.ap().rearrange("(i p k) d -> p i (k d)", p=P, k=2)
            for z in range(STEP):
                sp.wait_ge(yb_out[z], 16 * (NBLK // STEP))
            for g in range(4):
                rows = slice(8 * g, 8 * g + 8)
                sp.dma_start(yl[:, rows], y_tok[:, rows]).then_inc(y_in[g], 16)
            out_tok = out.rearrange("b (c p) d -> p (b c) d", p=P)
            for g in range(4):
                rows = slice(8 * g, 8 * g + 8)
                sp.wait_ge(sum_ready, g + 1)
                sp.dma_start(out_tok[:, rows], x_sb[:, rows]).then_inc(out_done, 16)
            for z in range(UNROLL):
                sp.wait_ge(xs_in[z], 16 * (LOADS // UNROLL))
            sp.wait_ge(out_done, 64)

        @block.gpsimd
        def _(pool):
            g_ = nc.gpsimd
            steps = [0]

            def link(ins):
                steps[0] += 1
                ins.then_inc(pool_step, 1)
                pool.wait_ge(pool_step, steps[0])

            link(g_.memset(ident[:], 0.0))
            link(g_.affine_select(out=ident[:], in_=ident[:], compare_op=ALU.not_equal, fill=1.0,
                                  base=0, pattern=[[-1, P]], channel_multiplier=1))
            link(g_.memset(exch[:], 0.0))
            link(g_.affine_select(out=exch[:], in_=exch[:], compare_op=ALU.not_equal, fill=1.0,
                                  base=-(P - 1), pattern=[[1, P]], channel_multiplier=1))
            link(g_.iota(srow[:], pattern=[[0, 1]], base=0, channel_multiplier=1,
                         allow_small_or_imprecise_dtypes=True))
            g_.memset(halfpi[:], PI / 2)
            link(g_.memset(mhalf[:], -0.5))
            link(g_.memset(xinit[:], 0.0))
            g_.memset(xinit[:, D:D + 1].bitcast(U32), NOWHERE).then_inc(xinit_ready, 1)
            g_.memset(cbig[:], 0.0).then_inc(cbig_zero, 1)
            g_.memset(ksb[:], 0.0).then_inc(const_ready, 1)

            def power(g):
                pool.wait_ge(var_ready, g + 1)
                g_.tensor_tensor(rs0[:, 8 * g:8 * g + 8], ve[:, 8 * g:8 * g + 8], mhalf[:, 8 * g:8 * g + 8],
                                 ALU.pow).then_inc(rs_ready, 1)

            tt, ts = g_.tensor_tensor, g_.tensor_scalar
            pool.wait_ge(em_ready, 1)
            pool.wait_ge(psin_ready, 1)
            tS, cb, lr, li, er, gr, gi, tmp = t
            ar, ai = e33[:, 1:N + 1], aim[:]
            cr, ci = cpar[:, :, 0], cpar[:, :, 1]
            link(tt(sh[:], sh[:], sh[:], ALU.mult))
            ts(cb[:], sh[:], -2.0, 1.0, ALU.mult, ALU.add)
            link(ts(tS[:], sh[:], 2.0, None, ALU.mult))
            tt(er[:], em[:], cb[:], ALU.mult)
            tt(li[:], em[:], sn[:, 0, :], ALU.mult)
            link(tt(lr[:], em[:], cb[:], ALU.mult))
            tt(er[:], er[:], tS[:], ALU.subtract)
            tt(lr[:], lr[:], cb[:], ALU.add)
            link(tt(li[:], li[:], sn[:, 0, :], ALU.add))
            tt(gr[:], li[:], ai, ALU.mult)
            link(tt(tmp[:], er[:], ar, ALU.mult))
            link(tt(gr[:], gr[:], tmp[:], ALU.subtract))
            tt(gi[:], li[:], ar, ALU.mult)
            link(tt(tmp[:], er[:], ai, ALU.mult))
            link(tt(gi[:], gi[:], tmp[:], ALU.add))
            tt(gr[:], gr[:], inv[:], ALU.mult)
            link(tt(gi[:], gi[:], inv[:], ALU.mult))
            tt(er[:], gr[:], cr, ALU.mult)
            tt(tS[:], gi[:], ci, ALU.mult)
            tt(cb[:], gr[:], ci, ALU.mult)
            link(tt(tmp[:], gi[:], cr, ALU.mult))
            tt(er[:], er[:], tS[:], ALU.add)
            link(tt(cb[:], cb[:], tmp[:], ALU.subtract))
            ts(q2[:, 0, :], er[:], 2.0, None, ALU.mult)
            link(ts(q2[:, 1, :], cb[:], -2.0, None, ALU.mult))
            tt(er[:], q2[:, 0, :], lr[:], ALU.mult)
            tt(tS[:], q2[:, 1, :], li[:], ALU.mult)
            tt(cb[:], q2[:, 0, :], li[:], ALU.mult)
            link(tt(tmp[:], q2[:, 1, :], lr[:], ALU.mult))
            tt(q1[:, 2, :], er[:], tS[:], ALU.add)
            tt(q1[:, 3, :], cb[:], tmp[:], ALU.subtract)
            tt(q1[:, 0, :], mag128[:], cs128[:], ALU.mult)
            link(tt(q1[:, 1, :], mag128[:], sn[:, 1, :], ALU.mult))
            g_.engine_nop().then_inc(q_ready, 1)
            power(0)
            for g in range(NG):
                pool.wait_ge(mag_ready, g + 1)
                pool.wait_ge(trig_ready, g + 1)
                table_product(g_, g, 1).then_inc(v1_pool, 1)
            power(1)
            power(2)
            power(3)
            link(g_.memset(ones[:], 1.0))
            link(g_.affine_select(out=upper[:], in_=ones[:], compare_op=ALU.is_gt, fill=0.0,
                                  base=0, pattern=[[1, P]], channel_multiplier=-1))
            g_.iota(rank_w[:], pattern=[[0, NT], [-1, E]], base=E, channel_multiplier=0,
                    allow_small_or_imprecise_dtypes=True)
            g_.iota(blk[:], pattern=[[1, NBLK + STEP]], base=0, channel_multiplier=0,
                    allow_small_or_imprecise_dtypes=True)
            link(g_.memset(first[:], 1.0))
            link(g_.memset(first[:].rearrange("p (e i) -> p e i", e=E)[:, :, 0:1], 0.0))
            for g in range(4):
                rows = slice(8 * g, 8 * g + 8)
                pool.wait_ge(xn_ready, g + 1)
                link(g_.tensor_tensor(x_sb[:, rows], x_sb[:, rows], xn[:, rows], ALU.add))
                g_.tensor_tensor(x_sb[:, rows], x_sb[:, rows], outb_bc[:].unsqueeze(1).broadcast_to([P, 8, D]),
                                 ALU.add).then_inc(r0_ready, 1)
            pool.wait_ge(v1_dve, NG)
            pool.wait_ge(v1_pool, NG)
            g_.memset(area[:, 8192:12288], 0.0).then_inc(sbd_zero, 1)

            pool.wait_ge(yq_ps, 8)
            ids = hx[:, :, :, D:D + 1].bitcast(U32).rearrange("p i k o -> p i (k o)")
            g_.iota(ids, pattern=[[2 * P, NT], [1, 2]], base=0, channel_multiplier=2).then_inc(ids_ready, 1)

            def root(dst, src, tmp1, tmp2, w):
                link(tt(tmp1, src, mhalf[:, 0:w], ALU.pow))
                link(tt(tmp2, tmp1, tmp1, ALU.mult))
                link(tt(tmp2, tmp2, src, ALU.mult))
                link(ts(tmp2, tmp2, -0.5, 1.5, ALU.mult, ALU.add))
                return tt(dst, tmp1, tmp2, ALU.mult)

            for c in range(CH + 1):
                if c < CH:
                    k = slice(4 * c, 4 * c + 4)
                    pool.wait_ge(q2_ready, c + 1)
                    root(rs1[:, k], ve[:, k], rs0[:, k], col[0][:, k], 4).then_inc(scale_ready, 1)
                if c >= 1:
                    k = slice(4 * c - 4, 4 * c)
                    pool.wait_ge(h0_ready, c)
                    g_.tensor_copy(hx[:, k, 1, 0:D], hx[:, k, 0, 0:D]).then_inc(hx_ready, 1)
            link(ts(col[1][:], mv[:, :, 1], LN_EPS, None, ALU.add))
            link(root(rstd[:], col[1][:], rs0[:], col[0][:], NT))
            link(tt(rstd[:], rstd[:], ve[:], ALU.mult))
            tt(rstd[:], rstd[:], rs1[:], ALU.mult).then_inc(rstd_ready, 1)

            pool.wait_ge(gate_ready, 1)
            pool.wait_ge(pos_ready, 1)
            pool.wait_ge(ids_ready, 1)
            pool.wait_ge(xs_cleared, 16)
            for i in range(NT):
                for k in range(2):
                    pool.indirect_dma_start(out=xs_dram.ap(), out_offset=bass.IndirectOffsetOnAxis(ap=pos[:, k, i:i + 1], axis=0),
                                            in_=hx[:, i, k, :], in_offset=None, bounds_check=NROW - 1,
                                            oob_is_err=False).then_inc(rows_out, 16)
            last_row = pool.to_reg(ROUTES - 1)
            def send_block(z):
                pool.indirect_dma_start(out=y_dram.ap(), out_offset=bass.IndirectOffsetOnAxis(ap=ybi[:, z:z + 1].bitcast(U32), axis=0),
                                        in_=yb[:, z, :], in_offset=None, bounds_check=last_row,
                                        oob_is_err=False).then_inc(yb_out[z], 16)

            for z in range(STEP):
                pool.wait_ge(yb_ready, z + 1 + 2)
                send_block(z)
            with pool.Fori(0, LOOPS) as it:
                for z in range(UNROLL):
                    pool.wait_ge(yb_ready, it * UNROLL + (STEP + z + 1 + 2))
                    g_.sem_inc(pool_turn, 1)
                    send_block(z % STEP)

        @block.vector
        def _(dve):
            v = nc.vector
            steps = [0]

            def link(ins):
                steps[0] += 1
                ins.then_inc(dve_step, 1)
                dve.wait_ge(dve_step, steps[0])

            dve.wait_ge(par_in, 64)
            link(v.tensor_scalar(p33[:], p33[:], -87.0, 88.0, ALU.max, ALU.min))
            link(v.tensor_scalar(z33[:], p33[:], LOG2E, MAGIC + 127.0, ALU.mult, ALU.add))
            link(v.tensor_scalar(q33[:], z33[:], -(MAGIC + 127.0), None, ALU.add))
            link(v.scalar_tensor_tensor(out=r33[:], in0=q33[:], scalar=-LN2_HI, in1=p33[:], op0=ALU.mult, op1=ALU.add))
            link(v.scalar_tensor_tensor(out=r33[:], in0=q33[:], scalar=-LN2_LO, in1=r33[:], op0=ALU.mult, op1=ALU.add))
            link(v.tensor_scalar(q33[:], r33[:], 1.0 / FACT[7], None, ALU.mult))
            for k in (6, 5, 4, 3, 2, 1):
                link(v.scalar_tensor_tensor(out=q33[:], in0=q33[:], scalar=1.0 / FACT[k], in1=r33[:],
                                            op0=ALU.add, op1=ALU.mult))
            link(v.tensor_scalar(z33[:].bitcast(U32), z33[:].bitcast(U32), 23, None, ALU.logical_shift_left))
            link(v.scalar_tensor_tensor(out=e33[:], in0=q33[:], scalar=1.0, in1=z33[:], op0=ALU.add, op1=ALU.mult))
            v.tensor_scalar(ab[:, 0, :], e33[:, 1:N + 1], e33[:, 0:1], -1.0, ALU.mult, ALU.mult)
            link(v.tensor_scalar(ab[:, 1, :], aim[:], e33[:, 0:1], 1.0 / (2 * PI), ALU.mult, ALU.mult))
            v.engine_nop().then_inc(ab_ready, 1)
            v.tensor_copy(fr[:, 0, :], ab[:, 1, :])
            link(v.tensor_scalar(fr[:, 1, :], ab[:, 1, :], float(P), None, ALU.mult))
            link(v.tensor_scalar(frq[:], fr[:], MAGIC, None, ALU.add))
            link(v.tensor_scalar(frq[:], frq[:], -MAGIC, None, ALU.add))
            link(v.tensor_tensor(fr[:], fr[:], frq[:], ALU.subtract))
            v.tensor_scalar(frq[:].bitcast(U32), fr[:].bitcast(U32), 0x7FFFFFFF, None, ALU.bitwise_and).then_inc(turns_ready, 1)
            link(v.tensor_scalar(ey[:], ab[:, 0, :], -24.0, 1.0 / 32, ALU.max, ALU.mult))
            link(v.tensor_scalar(em[:], ey[:], 1.0 / FACT[9], None, ALU.mult))
            for k in (8, 7, 6, 5, 4, 3, 2, 1):
                link(v.scalar_tensor_tensor(out=em[:], in0=em[:], scalar=1.0 / FACT[k], in1=ey[:],
                                            op0=ALU.add, op1=ALU.mult))
            for _ in range(5):
                link(v.scalar_tensor_tensor(out=em[:], in0=em[:], scalar=2.0, in1=em[:], op0=ALU.add, op1=ALU.mult))
            v.tensor_tensor(den[:], e33[:, 1:N + 1], e33[:, 1:N + 1], ALU.mult)
            link(v.tensor_tensor(inv[:], aim[:], aim[:], ALU.mult))
            link(v.tensor_tensor(den[:], den[:], inv[:], ALU.add))
            v.reciprocal(inv[:], den[:]).then_inc(em_ready, 1)

            def ln_stats(g):
                dve.wait_ge(x_in[g], 16)
                for i in range(8 * g, 8 * g + 8):
                    last = v.bn_stats(stats[:, i, :], x_sb[:, i, :])
                link(last)
                for i in range(8 * g, 8 * g + 8):
                    last = v.bn_aggr(mv[:, i, :], stats[:, i, :])
                link(last)
                v.tensor_scalar(ve[:, 8 * g:8 * g + 8], mv[:, 8 * g:8 * g + 8, 1], LN_EPS, None,
                                ALU.add).then_inc(var_ready, 1)

            def ln_norm(g):
                c = slice(8 * g, 8 * g + 8)
                dve.wait_ge(rs_ready, g + 1)
                link(v.tensor_tensor(rs1[:, c], rs0[:, c], rs0[:, c], ALU.mult))
                link(v.tensor_tensor(rs1[:, c], rs1[:, c], ve[:, c], ALU.mult))
                link(v.tensor_scalar(rs1[:, c], rs1[:, c], -0.5, 1.5, ALU.mult, ALU.add))
                link(v.tensor_tensor(rstd[:, c], rs1[:, c], rs0[:, c], ALU.mult))
                for i in range(8 * g, 8 * g + 8):
                    last = v.tensor_scalar(xn[:, i, :], x_sb[:, i, :], mv[:, i, 0:1], rstd[:, i:i + 1],
                                           ALU.subtract, ALU.mult)
                last.then_inc(xn_ready, 1)

            def table_args(g):
                dve.wait_ge(abb_in[g], 16)
                if g >= 2:
                    dve.wait_ge(v1_pool, g - 1)
                    dve.wait_ge(v1_dve, g - 1)
                f = abb[g][:, :, N:2 * N]
                rv = rnd.rearrange("p (h n) -> p h n", h=HG)
                arg = trig[:, g % 2, 1].rearrange("p (h n) -> p h n", h=HG)
                link(v.tensor_scalar(rv, f, srow[:, 0:1], MAGIC, ALU.mult, ALU.add))
                link(v.tensor_scalar(rnd, rnd, -MAGIC, None, ALU.add))
                ins = v.scalar_tensor_tensor(out=arg, in0=f, scalar=srow[:, 0:1], in1=rv,
                                             op0=ALU.mult, op1=ALU.subtract)
                link(ins)
                v.tensor_scalar(trig[:, g % 2, 0].bitcast(U32), trig[:, g % 2, 1].bitcast(U32), 0x7FFFFFFF, None,
                                ALU.bitwise_and).then_inc(arg_ready, 1)
                v.engine_nop().then_inc(abb_used, 1)

            def evict_u(i):
                dve.wait_ge(u_ps, i + 1)
                src = bank[2 + i % 2][:].rearrange("p (c h) -> p h c", c=4)
                v.tensor_tensor(u[:, :, 4 * i:4 * i + 4], src, inb_bc[:].unsqueeze(2).broadcast_to([P, D, 4]),
                                ALU.add).then_inc(u_ready, 1)

            def evict_v2(i):
                if not evict_v2_by_act(i):
                    dve.wait_ge(v2_ps, i + 1)
                    v.tensor_copy(v2[:, 4 * i:4 * i + 4, :], bank[4 + i % 4][:]
                                  .rearrange("p (q s) -> p q s", q=4)).then_inc(v2_dve, 1)

            def real_half(g):
                dve.wait_ge(mag_ready, g + 1)
                dve.wait_ge(trig_ready, g + 1)
                table_product(v, g, 0).then_inc(v1_dve, 1)

            def evict_k(g):
                dve.wait_ge(k_ps, g + 1)
                link(v.tensor_copy(ksb[:, g, 127:255], bank[1 + g % 2][0:HG, 0:P]))
                v.tensor_tensor(ksb[:, g, 127:128], ksb[:, g, 127:128], dskip[:, g:g + 1], ALU.add).then_inc(k_ready, 1)

            dve.wait_ge(const_ready, 1)
            ln_stats(0)
            table_args(0)
            table_args(1)
            real_half(0)
            ln_norm(0)
            table_args(2)
            real_half(1)
            table_args(3)
            dve.wait_ge(q_ps, 1)
            dve.wait_ge(cbig_zero, 1)
            for e in range(2):
                dst = cbig[64 * e:64 * e + 64].rearrange("p g m -> p (g m)")
                for g in range(NG):
                    lo = 512 * g + e
                    last = v.tensor_copy(dst[:, lo:lo + 34 * 15 + 1:34], bank[3][0:64, HG * g + e:HG * (g + 1):2])
            last.then_inc(cbig_ready, 1)
            for i in range(0, 4):
                evict_v2(i)
            real_half(2)
            ln_stats(1)
            real_half(3)
            dve.wait_ge(lw_act, 1)
            link(v.tensor_scalar(lw[:, 2:6:2, :], lw[:, 3:6:2, :], -1.0, None, ALU.mult))
            dve.wait_ge(mag_ready, NG)
            for i in range(4, 8):
                evict_v2(i)
            ln_stats(2)
            for i in range(8, 12):
                evict_v2(i)
            dve.wait_ge(b_in, 64)
            evict_k(0)
            ln_stats(3)
            for i in range(12, 16):
                evict_v2(i)
            evict_k(1)
            ln_norm(1)
            evict_u(0)
            evict_u(1)
            evict_k(2)
            ln_norm(2)
            evict_k(3)
            ln_norm(3)
            for i in range(2, 8):
                evict_u(i)

            for half in range(2):
                dve.wait_ge(b_ps, 4 * half + 4)
                for m in range(2):
                    k = 2 * m + 1
                    for r in range(2):
                        for q in range(4):
                            src = bank[4 * half + q][64 + 32 * r:96 + 32 * r].rearrange(
                                "p (j m e c) -> p j m e c", j=4, m=2, e=2)[:, :, m, 1, :]
                            last = v.tensor_copy(st[32 * k:32 * k + 32, r, 16 * half + 4 * q:16 * half + 4 * q + 4, :], src)
                last.then_inc(b_dve, 1)
            link(v.engine_nop())
            dve.wait_ge(b_act, 2)
            sv = st[:].rearrange("p r x (b j) -> p r x b j", b=B)
            m1, m2 = [rnd[:, 128 * i:128 * i + 128].rearrange("p (r x b) -> p r x b", r=2, x=NX) for i in range(2)]
            lr_b = lw[:, 0, :].unsqueeze(1).unsqueeze(3).broadcast_to([P, 2, NX, B])
            li_b = lw[:, 2:4, :].unsqueeze(3).broadcast_to([P, 2, NX, B])
            dve.wait_ge(v2_ps, 16)
            for j in range(1, NC - 1):
                v.tensor_tensor(m1, lr_b, sv[:, :, :, :, j - 1], ALU.mult)
                link(v.tensor_tensor(m2, li_b, sv[:, ::-1, :, :, j - 1], ALU.mult))
                link(v.tensor_tensor(m1, m1, m2, ALU.add))
                link(v.tensor_tensor(sv[:, :, :, :, j], sv[:, :, :, :, j], m1, ALU.add))
            for r in range(2):
                v.tensor_tensor(mul1[:, r], lw[:, 1, :].unsqueeze(2).broadcast_to([P, NX, NT]), st[:, r], ALU.mult)
                last = v.tensor_tensor(mul2[:, r], lw[:, 4 + r, :].unsqueeze(2).broadcast_to([P, NX, NT]), st[:, 1 - r], ALU.mult)
            link(last)
            v.tensor_tensor(mul1[:, 0], mul1[:, 0], mul2[:, 0], ALU.add)
            link(v.scalar_tensor_tensor(out=mul1[:, 1], in0=mul1[:, 1], scalar=-1.0, in1=mul2[:, 1],
                                        op0=ALU.mult, op1=ALU.subtract))
            v.engine_nop().then_inc(mul_ready, 1)
            dve.wait_ge(sbd_zero, 1)
            for m in range(2):
                k = 2 * m + 1
                for r in range(2):
                    for b in range(B):
                        dst = s_bd[64 + 32 * r:96 + 32 * r, m::2, 1, NC * b + 1:NC * b + NC]
                        src = mul1[32 * k:32 * k + 32, r, :, NC * b:NC * b + NC - 1]
                        last = v.tensor_copy(dst, src)
            last.then_inc(sbd_dve, 1)


            for i in range(1, 8, 2):
                dve.wait_ge(yq_ps, i + 1)
                v.tensor_copy(y_tiles(i), bank[i][:].rearrange("p (x k c) -> p c x k", x=4, k=4)).then_inc(y_dve, 1)

            dve.wait_ge(rms_ps, 1)
            link(v.tensor_copy(rmsT[:], bank[0][:, 0:EA]))
            dve.wait_ge(ew_in, 32)
            for e in range(EA):
                last = v.tensor_scalar(w1_sb[:, e, :], w1_sb[:, e, :], rmsT[:, e:e + 1], None, ALU.mult)
            last.then_inc(w1_ready, 1)

            def glu(c):
                dve.wait_ge(sg_ready, c + 1)
                if c >= 2:
                    dve.wait_ge(o_ps, c - 1)
                v.scalar_tensor_tensor(out=aT[:, c % 2], in0=bank[2][:], scalar=glub[:, 0:1], in1=sg[:, c % 2],
                                       op0=ALU.add, op1=ALU.mult).then_inc(aT_ready, 1)

            def residual(c):
                rows = x_sb[:, 4 * c:4 * c + 4]
                dve.wait_ge(o_ps, c + 1)
                ins = v.tensor_tensor(rows, bank[4][:].rearrange("p (i d) -> p i d", i=4), rows, ALU.add)
                link(ins)
                v.engine_nop().then_inc(x2_ready, 1)
                for i in range(4 * c, 4 * c + 4):
                    last = v.bn_stats(stats[:, i, :], x_sb[:, i, :])
                link(last)
                for i in range(4 * c, 4 * c + 4):
                    last = v.bn_aggr(mv[:, i, :], stats[:, i, :])
                link(last)
                v.tensor_scalar(ve[:, 4 * c:4 * c + 4], mv[:, 4 * c:4 * c + 4, 1], 1.0 + RMS_EPS, RMS_EPS * LN_EPS,
                                ALU.mult, ALU.add).then_inc(q2_ready, 1)

            def normalise(c):
                dve.wait_ge(scale_ready, c + 1)
                for i in range(4 * c, 4 * c + 4):
                    last = v.tensor_scalar(hx[:, i, 0, 0:D], x_sb[:, i, :], mv[:, i, 0:1], rs1[:, i:i + 1],
                                           ALU.subtract, ALU.mult)
                last.then_inc(h0_ready, 1)

            dve.wait_ge(yq_ps, 8)
            for i in range(CH + 2):
                if i < CH:
                    glu(i)
                if 0 <= i - 1 < CH:
                    residual(i - 1)
                if 0 <= i - 2 < CH:
                    normalise(i - 2)

            def te(a):
                return a.rearrange("p (i e) -> p i e", e=E)

            def tb(a):
                return a.unsqueeze(2).broadcast_to([P, NT, E])

            lg, gt, oh1, oh2, sc, p2, cntT, incl, slot = rt
            mx, z1, m1_, m2_, r1, gs, g1, g2_ = [c_[:] for c_ in col]
            dve.wait_ge(r_ps, 1)
            dve.wait_ge(rstd_ready, 1)
            link(v.tensor_tensor(te(lg), te(bank[6][:, 0:448]), tb(rstd[:]), ALU.mult))
            link(v.tensor_reduce(mx, te(lg), AX.X, ALU.max))
            v.tensor_tensor(te(lg), te(lg), tb(mx), ALU.subtract).then_inc(lg_ready, 1)
            dve.wait_ge(ex_ready, 1)
            link(v.tensor_reduce(z1, te(gt), AX.X, ALU.add))
            link(v.reciprocal(z1, z1))
            link(v.tensor_tensor(te(gt), te(gt), tb(z1), ALU.mult))
            link(v.tensor_reduce(m1_, te(gt), AX.X, ALU.max))
            link(v.tensor_tensor(te(sc), te(gt), tb(m1_), ALU.is_equal))
            link(v.tensor_tensor(sc, sc, rank_w[:], ALU.mult))
            link(v.tensor_reduce(r1, te(sc), AX.X, ALU.max))
            link(v.tensor_tensor(te(oh1), te(sc), tb(r1), ALU.is_equal))
            link(v.scalar_tensor_tensor(out=p2, in0=oh1, scalar=-2.0, in1=gt, op0=ALU.mult, op1=ALU.add))
            link(v.tensor_reduce(m2_, te(p2), AX.X, ALU.max))
            link(v.tensor_tensor(te(sc), te(p2), tb(m2_), ALU.is_equal))
            link(v.tensor_tensor(sc, sc, rank_w[:], ALU.mult))
            link(v.tensor_reduce(r1, te(sc), AX.X, ALU.max))
            link(v.tensor_tensor(te(oh2), te(sc), tb(r1), ALU.is_equal))
            v.tensor_tensor(p2, oh1, oh2, ALU.add).then_inc(m_ready, 1)
            link(v.scalar_tensor_tensor(out=gs, in0=m1_, scalar=1e-9, in1=m2_, op0=ALU.add, op1=ALU.add))
            link(v.reciprocal(gs, gs))
            dve.wait_ge(hx_ready, CH)
            v.tensor_tensor(hx[:, :, 0, D + 1], m1_, gs, ALU.mult)
            v.tensor_tensor(hx[:, :, 1, D + 1], m2_, gs, ALU.mult).then_inc(gate_ready, 1)

            def add_shared(c):
                dve.wait_ge(so_ps, c + 1)
                rows = x_sb[:, 4 * c:4 * c + 4]
                v.tensor_tensor(rows, bank[4 + c % 2][:].rearrange("p (i d) -> p i d", i=4), rows,
                                ALU.add).then_inc(so_added, 1)

            dve.wait_ge(rank_ps, 1)
            ei = "p (e i) -> p e i"
            link(v.tensor_copy(cntT.rearrange(ei, e=E), te(bank[6][:, 0:448]).rearrange("p i e -> p e i")))
            link(v.tensor_tensor_scan(incl, first[:], cntT, 0.0, ALU.mult, ALU.add))
            nb, cnb, eb, tot = [x_[:] for x_ in e14]
            link(v.tensor_scalar(nb, incl.rearrange(ei, e=E)[:, :, NT - 1], 1.0 / P, (P - 1) / P - 0.5 + 1.0 / (2 * P), ALU.mult, ALU.add))
            link(v.tensor_scalar(nb, nb, MAGIC, None, ALU.add))
            link(v.tensor_scalar(nb, nb, -MAGIC, None, ALU.add))
            link(v.tensor_tensor_scan(cnb, ones[:, 0:E], nb, 0.0, ALU.mult, ALU.add))
            link(v.tensor_tensor(eb, cnb, nb, ALU.subtract))
            link(v.tensor_scalar(eb, eb, float(P), None, ALU.mult))
            link(v.tensor_tensor(incl, incl, cntT, ALU.subtract))
            link(v.tensor_tensor(incl.rearrange(ei, e=E), incl.rearrange(ei, e=E), eb.unsqueeze(2).broadcast_to([P, E, NT]), ALU.add))
            link(v.tensor_tensor(te(slot), te(bank[7][:, 0:448]), incl.rearrange(ei, e=E).rearrange("p e i -> p i e"), ALU.add))
            link(v.tensor_tensor(oh1, oh1, slot, ALU.mult))
            link(v.tensor_tensor(oh2, oh2, slot, ALU.mult))
            v.tensor_reduce(mx, te(oh1), AX.X, ALU.add)
            link(v.tensor_reduce(z1, te(oh2), AX.X, ALU.add))
            v.tensor_copy(pos[:, 0, :], mx)
            v.tensor_copy(pos[:, 1, :], z1).then_inc(pos_ready, 1)
            lb = NBLK + STEP
            cmp_ = sg.rearrange("p z m -> p (z m)")[0:1, 0:lb * (E - 1)] if lb * (E - 1) <= 1024 else \
                v2_flat[0:1, 5120:5120 + lb * (E - 1)]
            dve.wait_ge(hT_ready, CH)
            link(v.tensor_tensor(cmp_.rearrange("p (b e) -> p b e", e=E - 1), cnb[0:1, 0:E - 1].unsqueeze(1).broadcast_to([1, lb, E - 1]),
                                 blk[0:1, :].unsqueeze(2).broadcast_to([1, lb, E - 1]), ALU.is_le))
            link(v.tensor_reduce(rt[4][0:1, 0:lb], cmp_.rearrange("p (b e) -> p b e", e=E - 1), AX.X, ALU.add))
            link(v.tensor_scalar(etab[0:1, :], rt[4][0:1, 0:lb], float(HID), None, ALU.mult))
            for c in range(CH):
                add_shared(c)

            dve.wait_ge(o_ps, CH)
            v.engine_nop().then_inc(yb_ready, 2)

            def fetch_weights(at, z):
                r = dve.value_load(etab[0:1, bass.ds(at, 1)], min_val=0, max_val=(E - 1) * HID)
                v.tensor_copy(wc[:, z % STEP], v1_flat.rearrange("p (w m) -> p w m", w=2)[:, :, bass.ds(r, HID)]).then_inc(wc_ready, 1)

            dve.wait_ge(ew2_in, 16 * 2 * HC)
            for z in range(STEP - 1):
                fetch_weights(z, z)

            def finish_block(n, z):
                row = z % UNROLL
                z = z % STEP
                dve.wait_ge(yb_ps, n + 4)
                v.tensor_copy(ybi[:, z:z + 1].bitcast(U32), xs[:, row, D:D + 1].bitcast(U32))
                v.tensor_scalar(yb[:, z], bank[4 + z % 2][:, 0:D], xs[:, row, D + 1:D + 2], None,
                                ALU.mult).then_inc(yb_ready, 1)
                fetch_weights(n + STEP - 1, z + STEP - 1)

            for z in range(STEP):
                finish_block(z, z)
            with dve.Fori(0, LOOPS) as it:
                for z in range(UNROLL):
                    dve.wait_ge(yb_out[z % STEP], it * (16 * UNROLL // STEP) + 16 * (1 + z // STEP))
                    finish_block(it * UNROLL + (STEP + z), STEP + z)
            for g in range(4):
                rows = slice(8 * g, 8 * g + 8)
                dve.wait_ge(y_in[g], 16)
                link(v.tensor_tensor(x_sb[:, rows], x_sb[:, rows], yl[:, rows, 0:D], ALU.add))
                v.tensor_tensor(x_sb[:, rows], x_sb[:, rows], yl[:, rows, D:2 * D], ALU.add).then_inc(sum_ready, 1)

        @block.scalar
        def _(act):
            a = nc.scalar
            steps = [0]

            def link(ins):
                steps[0] += 1
                ins.then_inc(act_step, 1)
                act.wait_ge(act_step, steps[0])

            act.dma_start(wnat[:, 0, :], in_w).then_inc(w_in, 16)
            act.dma_start(wnat[:, 1:3, :], glu_w.rearrange("(c p) h -> p c h", p=P)).then_inc(w_in, 16)
            act.dma_start(wnat[:, 3, :], out_w).then_inc(w_in, 16)
            act.dma_start(inb_bc[:], in_b.partition_broadcast(P)).then_inc(b_in, 16)
            act.dma_start(outb_bc[:], out_b.partition_broadcast(P)).then_inc(b_in, 16)
            act.dma_start(glub[:], glu_b.rearrange("(c p) -> p c", p=P), allow_slow_non_contiguous=True).then_inc(b_in, 16)
            act.dma_start(rmsn[0:E, :], rms_w).then_inc(rms_in, 16)
            act.dma_start(rmsn[E:EA, :], rms_ws).then_inc(rms_in, 16)
            act.dma_start(rw[:], router_w).then_inc(rms_in, 16)
            act.dma_start(dskip[:], d_skip.rearrange("(g p) -> p g", p=HG), allow_slow_non_contiguous=True).then_inc(b_in, 16)

            def evict_xnT(i):
                act.wait_ge(xnT_ps, i + 1)
                if i >= 2:
                    act.wait_ge(u_ps, i - 1)
                a.copy(xnT[:, i % 2, :], bank[i % 2][:]).then_inc(xnT_ready, 1)

            act.wait_ge(const_ready, 1)
            act.wait_ge(ab_ready, 1)
            a.activation(mag128[:], ab[:, 0, :], ACT.Exp, scale=float(P))
            act.wait_ge(wT_ps, 1)
            a.copy(wT[:].rearrange("p c m -> p (c m)"), bank[4][:]).then_inc(wT_ready, 1)

            def magnitude(g):
                act.wait_ge(abb_in[g], 16)
                a.activation(mag[:, g].rearrange("p (h n) -> p h n", h=HG), abb[g][:, :, 0:N], ACT.Exp,
                             scale=srow[:, 0:1]).then_inc(mag_ready, 1)

            def sines(g):
                act.wait_ge(arg_ready, g + 1)
                a.activation(trig[:, g % 2, 1], trig[:, g % 2, 1], ACT.Sin, scale=TWO_PI)
                a.activation(trig[:, g % 2, 0], trig[:, g % 2, 0], ACT.Sin, scale=-TWO_PI,
                             bias=halfpi[:]).then_inc(trig_ready, 1)

            act.wait_ge(turns_ready, 1)
            a.activation(sn[:], fr[:], ACT.Sin, scale=TWO_PI)
            a.activation(cs128[:], frq[:, 1, :], ACT.Sin, scale=-TWO_PI, bias=halfpi[:])
            a.activation(sh[:], fr[:, 0, :], ACT.Sin, scale=TWO_PI / 2).then_inc(psin_ready, 1)
            magnitude(0)
            magnitude(1)
            sines(0)
            sines(1)
            magnitude(2)
            magnitude(3)
            sines(2)
            sines(3)
            act.wait_ge(q_ps, 1)
            for k in range(4):
                for q, to in enumerate((0, 3, 1, 5)):
                    last = a.copy(lw[32 * k:32 * k + 32, to, :], bank[0][32 * q:32 * q + 32, k:P:4])
            last.then_inc(lw_act, 1)
            act.wait_ge(abb_used, NG)
            for i in range(16):
                if evict_v2_by_act(i):
                    act.wait_ge(v2_ps, i + 1)
                    a.copy(v2[:, 4 * i:4 * i + 4, :], bank[4 + i % 4][:]
                           .rearrange("p (q s) -> p q s", q=4)).then_inc(v2_act, 1)
            for i in range(8):
                evict_xnT(i)
            for half in range(2):
                act.wait_ge(b_ps, 4 * half + 4)
                for m in range(2):
                    k = 2 * m
                    for r in range(2):
                        for q in range(4):
                            src = bank[4 * half + q][32 * r:32 + 32 * r].rearrange(
                                "p (j m e c) -> p j m e c", j=4, m=2, e=2)[:, :, m, 0, :]
                            last = a.copy(st[32 * k:32 * k + 32, r, 16 * half + 4 * q:16 * half + 4 * q + 4, :], src)
                last.then_inc(b_act, 1)
            act.wait_ge(mul_ready, 1)
            act.wait_ge(sbd_zero, 1)
            for m in range(2):
                k = 2 * m
                for r in range(2):
                    for b in range(B):
                        dst = s_bd[32 * r:32 + 32 * r, m::2, 0, NC * b + 1:NC * b + NC]
                        src = mul1[32 * k:32 * k + 32, r, :, NC * b:NC * b + NC - 1]
                        last = a.copy(dst, src)
            last.then_inc(sbd_act, 1)
            act.wait_ge(t0_ps, 3)
            act.dma_start(w1_sb[:, 0:E], w1.rearrange("e p m -> p e m")).then_inc(ew_in, 16)
            act.dma_start(w1_sb[:, E:EA], w1s.rearrange("e p m -> p e m")).then_inc(ew_in, 16)
            act.wait_ge(sbd_dve, 1)
            act.wait_ge(sbd_act, 1)
            for c in range(HC):
                act.dma_start(w2_sb[:, 0:E, c], w2.rearrange("e (c p) d -> c p e d", c=HC)[c]).then_inc(ew2_in, 16)
                act.dma_start(w2_sb[:, E:EA, c], w2s.rearrange("e (c p) d -> c p e d", c=HC)[c]).then_inc(ew2_in, 16)
            act.wait_ge(t0_ps, 4)
            for i in range(8):
                act.wait_ge(y_ps, i + 1)
                a.activation(yq[:, 512 * i:512 * i + 512], bank[i][:], ACT.Gelu).then_inc(yq_ready, 1)
            for i in range(0, 8, 2):
                act.wait_ge(yq_ps, i + 1)
                a.copy(y_tiles(i), bank[i][:].rearrange("p (x k c) -> p c x k", x=4, k=4)).then_inc(y_ready, 1)


            def copy_yT(c):
                act.wait_ge(yT_ps, c + 1)
                if c >= 2:
                    act.wait_ge(ag_ps, c - 1)
                a.copy(yT[:, c % 2], bank[c % 2][:]).then_inc(yT_ready, 1)

            def gate_glu(c):
                act.wait_ge(ag_ps, c + 1)
                if c >= 2:
                    act.wait_ge(aT_ready, c - 1)
                a.activation(sg[:, c % 2], bank[3][:], ACT.Sigmoid, bias=glub[:, 1:2]).then_inc(sg_ready, 1)

            copy_yT(0)
            for i in range(CH + 3):
                if i < CH:
                    gate_glu(i)
                if i + 1 < CH:
                    copy_yT(i + 1)
                if 0 <= i - 3 < CH:
                    c = i - 3
                    act.wait_ge(hT_ps, c + 1)
                    a.copy(h0T[:, 512 * c:512 * c + 512], bank[5][:]).then_inc(hT_ready, 1)
            act.wait_ge(lg_ready, 1)
            a.activation(rt[1], rt[0], ACT.Exp).then_inc(ex_ready, 1)
            for c in range(CH):
                for e in range(ES * HC):
                    act.wait_ge(sh_ps, 4 * c + e + 1)
                    if c >= 2 and e == 0:
                        act.wait_ge(so_ps, c - 1)
                    a.activation(ysh[:, c % 2, e], bank[e][:], ACT.Silu).then_inc(sh_ready, 1)
            a.nop().then_inc(xt_ready, 2)
            a.nop().then_inc(act_ready, 2)

            def copy_xsT(n, z):
                act.wait_ge(xt_ps, n + 1)
                act.wait_ge(hid_ps, n + 1)
                a.copy(xsT[:, z % 3], bank[z % 2][:, 0:P]).then_inc(xt_ready, 1)

            def silu(n, z):
                act.wait_ge(hid_ps, n + 4)
                act.wait_ge(yb_ps, n + 1)
                a.activation(act_sb[:, z % 3], bank[2 + z % 2][:, 0:HID], ACT.Silu).then_inc(act_ready, 1)

            copy_xsT(0, 0)
            copy_xsT(1, 1)
            copy_xsT(2, 2)
            silu(0, 0)
            silu(1, 1)
            for z in range(STEP):
                copy_xsT(z + 3, z + 3)
                silu(z + 2, z + 2)
            with act.Fori(0, LOOPS) as it:
                for z in range(UNROLL):
                    copy_xsT(it * UNROLL + (STEP + z + 3), z + 3)
                    silu(it * UNROLL + (STEP + z + 2), z + 2)

        @block.tensor
        def _(pe):
            mm, tr = nc.tensor.matmul, nc.tensor.transpose
            pe.wait_ge(const_ready, 1)
            pe.wait_ge(w_in, 48)
            for c in range(4):
                last = tr(bank[4][:, P * c:P * c + P], wnat[:, c, :], ident[:])
            last.then_inc(wT_ps, 1)

            def turn_xn(i):
                if i % 2 == 0:
                    pe.wait_ge(xn_ready, i // 2 + 1)
                if i >= 2:
                    pe.wait_ge(xnT_ready, i - 1)
                for c in range(4):
                    last = mm(bank[i % 2][:, P * c:P * c + P], xn[:, 4 * i + c, :], exch[:], start=True, stop=True)
                last.then_inc(xnT_ps, 1)

            def project_in(i):
                pe.wait_ge(xnT_ready, i + 1)
                if i == 0:
                    pe.wait_ge(wT_ready, 1)
                if i >= 2:
                    pe.wait_ge(u_ready, i - 1)
                for c in range(4):
                    last = mm(bank[2 + i % 2][:, P * c:P * c + P], xnT[:, i % 2, P * c:P * c + P], wT[:, 0, :],
                              start=True, stop=True)
                last.then_inc(u_ps, 1)

            pe.wait_ge(q_ready, 1)
            tr(bank[0][:, 0:P], q1[:].rearrange("p q n -> p (q n)"), ident[:])
            tr(bank[3][0:64, 0:P], q2[:].rearrange("p q n -> p (q n)"), ident[:]).then_inc(q_ps, 1)

            def turn_tables(g):
                pe.wait_ge(v1_dve, g + 1)
                pe.wait_ge(v1_pool, g + 1)
                for i in range(4 * g, 4 * g + 4):
                    if i >= 4:
                        pe.wait_ge(v2_act if evict_v2_by_act(i - 4) else v2_dve, (i - 4) // 2 + 1)
                    else:
                        pe.wait_ge(wT_ready, 1)
                    for q in range(4):
                        p = 4 * i + q
                        last = tr(bank[4 + i % 4][:, P * q:P * q + P], v1[:, 2 * p:2 * p + 2].rearrange("p h r n -> p (h r n)"), ident[:])
                    last.then_inc(v2_ps, 1)

            def impulse(g):
                if g == 0:
                    pe.wait_ge(cbig_ready, 1)
                if g >= 2:
                    pe.wait_ge(k_ready, g - 1)
                pe.wait_ge(v2_act, 2 * g + 2)
                pe.wait_ge(v2_dve, 2 * g + 2)
                for j in range(PG):
                    last = mm(bank[1 + g % 2][0:HG, 0:P], cbig[:, g, 32 * j:32 * j + 32], v2[:, PG * g + j, :],
                              start=(j == 0), stop=(j == PG - 1))
                last.then_inc(k_ps, 1)

            turn_tables(0)
            turn_tables(1)
            impulse(0)
            turn_tables(2)
            impulse(1)
            turn_tables(3)
            pe.wait_ge(lw_act, 1)
            pe.wait_ge(cbig_ready, 1)
            pe.wait_ge(k_ready, 2)
            turn_xn(0)
            turn_xn(1)
            project_in(0)
            project_in(1)
            pe.wait_ge(u_ready, 2)
            impulse(2)
            impulse(3)
            pe.wait_ge(k_ready, NG)
            turn_xn(2)
            for i in range(2, 8):
                if i < 7:
                    turn_xn(i + 1)
                project_in(i)

            pe.wait_ge(u_ready, 8)
            pe.wait_ge(lw_act, 1)
            pe.wait_ge(k_ready, NG)
            for i in range(8):
                for q in range(8):
                    p = 8 * i + q
                    last = mm(bank[i][:, 64 * q:64 * q + 64], v1[:, 2 * p:2 * p + 2].rearrange("p h r n -> p (h r n)"),
                              u[:, 2 * p:2 * p + 2, :].rearrange("p h c -> p (h c)"), start=True, stop=True)
                last.then_inc(b_ps, 1)

            pe.wait_ge(b_act, 2)
            pe.wait_ge(b_dve, 2)
            for g in range(NG):
                pe.wait_ge(hank_in[g], 16)
                for q in range(HG):
                    h = HG * g + q
                    k, x_ = h % 4, h // 4
                    last = mm(bank[x_ // 4][32 * k:32 * k + 32, P * (x_ % 4):P * (x_ % 4) + P], u[:, h, :], hank[g][:, q, :],
                              start=(x_ % 4 == 0), stop=False, skip_group_check=True)
                last.then_inc(t0_ps, 1)
            pe.wait_ge(sbd_act, 1)
            pe.wait_ge(sbd_dve, 1)
            for p in range(NPAIR):
                m, x_ = p % 2, p // 2
                last = mm(bank[x_ // 4][64 * m:64 * m + 64, P * (x_ % 4):P * (x_ % 4) + P],
                          s_bd[:, p].rearrange("p e c -> p (e c)"), v2[:, p, :],
                          start=False, stop=(x_ % 4 == 3), skip_group_check=True)
                if p % 8 == 7:
                    last.then_inc(y_ps, 1)
            for i in range(8):
                pe.wait_ge(yq_ready, i + 1)
                for q in range(4):
                    last = tr(bank[i][:, P * q:P * q + P], yq[:, 512 * i + P * q:512 * i + P * q + P], ident[:])
                last.then_inc(yq_ps, 1)

            pe.wait_ge(rms_in, 48)
            pe.wait_ge(y_ready, 4)
            pe.wait_ge(y_dve, 4)
            tr(bank[0][:, 0:EA], rmsn[:], ident[0:EA, 0:EA]).then_inc(rms_ps, 1)

            def turn_y(c):
                if c >= 2:
                    pe.wait_ge(yT_ready, c - 1)
                if c == 0:
                    pe.wait_ge(w1_ready, 1)
                for q in range(4):
                    last = tr(bank[c % 2][:, P * q:P * q + P], y_sb[:, 4 * c + q, :], ident[:])
                last.then_inc(yT_ps, 1)

            def glu_products(c):
                pe.wait_ge(yT_ready, c + 1)
                pe.wait_ge(aT_ready, c) if c else None
                mm(bank[2][:], wT[:, 1, :], yT[:, c % 2], start=True, stop=True)
                mm(bank[3][:], wT[:, 2, :], yT[:, c % 2], start=True, stop=True).then_inc(ag_ps, 1)

            def project_out(c):
                pe.wait_ge(aT_ready, c + 1)
                if c:
                    pe.wait_ge(x2_ready, c)
                for q in range(4):
                    last = mm(bank[4][:, P * q:P * q + P], aT[:, c % 2, P * q:P * q + P], wT[:, 3, :], start=True, stop=True)
                last.then_inc(o_ps, 1)

            def turn_h0(c):
                pe.wait_ge(h0_ready, c + 1)
                if c:
                    pe.wait_ge(hT_ready, c)
                for q in range(4):
                    last = tr(bank[5][:, P * q:P * q + P], hx[:, 4 * c + q, 0, 0:D], ident[:])
                last.then_inc(hT_ps, 1)

            def route(c):
                pe.wait_ge(hT_ready, c + 1)
                for i in range(4 * c, 4 * c + 4):
                    last = mm(bank[6][:, E * i:E * i + E], h0T[:, P * i:P * i + P], rw[:], start=True, stop=True)
                if c == CH - 1:
                    last.then_inc(r_ps, 1)

            turn_y(0)
            for i in range(CH + 4):
                if i < CH:
                    glu_products(i)
                if i + 1 < CH:
                    turn_y(i + 1)
                if 0 <= i - 1 < CH:
                    project_out(i - 1)
                if 0 <= i - 3 < CH:
                    turn_h0(i - 3)
                if 0 <= i - 4 < CH:
                    route(i - 4)

            def shared_in(c):
                for e in range(ES * HC):
                    if c:
                        pe.wait_ge(sh_ready, 4 * c - 4 + e + 1)
                    mm(bank[e][:], w1_sb[:, E + e // HC, P * (e % HC):P * (e % HC) + P], h0T[:, 512 * c:512 * c + 512],
                       start=True, stop=True).then_inc(sh_ps, 1)

            def shared_out(c):
                pe.wait_ge(sh_ready, 4 * c + 4)
                if c == 0:
                    pe.wait_ge(ew2_in, 16 * 2 * HC)
                    pe.wait_ge(x2_ready, CH)
                if c >= 2:
                    pe.wait_ge(so_added, c - 1)
                for q in range(4):
                    for e in range(ES * HC):
                        last = mm(bank[4 + c % 2][:, P * q:P * q + P], ysh[:, c % 2, e, P * q:P * q + P],
                                  w2_sb[:, E + e // HC, e % HC, :], start=(e == 0), stop=(e == ES * HC - 1))
                last.then_inc(so_ps, 1)

            shared_in(0)
            shared_in(1)
            shared_out(0)
            pe.wait_ge(m_ready, 1)
            mm(bank[6][:, 0:448], ones[:], rt[5], start=True, stop=True)
            mm(bank[7][:, 0:448], upper[:], rt[5], start=True, stop=True).then_inc(rank_ps, 1)
            for c in range(1, CH):
                if c + 1 < CH:
                    shared_in(c + 1)
                shared_out(c)

            pe.nop().then_inc(hid_ps, 3)
            pe.nop().then_inc(yb_ps, 3)
            pe.wait_ge(sh_ready, 4 * CH)
            pe.wait_ge(so_added, CH)

            def turn_rows(n, loads, z):
                pe.wait_ge(xs_in[z % UNROLL], loads)
                pe.wait_ge(xt_ready, n + 1)
                tr(bank[z % 2][:, 0:P], xs[:, z % UNROLL, 0:D], ident[:]).then_inc(xt_ps, 1)

            def first_matrix(n, z):
                pe.wait_ge(xt_ready, n + 3)
                pe.wait_ge(wc_ready, n + 1)
                pe.wait_ge(act_ready, n + 1)
                for c in range(HC):
                    last = mm(bank[2 + z % 2][:, P * c:P * c + P], wc[:, z % STEP, 1, P * c:P * c + P], xsT[:, z % 3],
                              start=True, stop=True)
                last.then_inc(hid_ps, 1)

            def second_matrix(n, z):
                pe.wait_ge(act_ready, n + 3)
                pe.wait_ge(yb_ready, n + 1)
                for c in range(HC):
                    last = mm(bank[4 + z % 2][:, 0:D], act_sb[:, z % 3, P * c:P * c + P], wc[:, z % STEP, 0, P * c:P * c + P],
                              start=(c == 0), stop=(c == HC - 1))
                last.then_inc(yb_ps, 1)

            turn_rows(0, 16, 0)
            turn_rows(1, 16, 1)
            turn_rows(2, 16, 2)
            first_matrix(0, 0)
            first_matrix(1, 1)
            for z in range(STEP):
                turn_rows(z + 3, 16, z + 3)
                first_matrix(z + 2, z + 2)
                second_matrix(z, z)
            with pe.Fori(0, LOOPS) as it:
                for z in range(UNROLL):
                    turn_rows(it * UNROLL + (STEP + z + 3), it * 16 + 16 * (1 + (STEP + z + 3) // UNROLL), STEP + z + 3)
                    first_matrix(it * UNROLL + (STEP + z + 2), z + 2)
                    second_matrix(it * UNROLL + (STEP + z), z)


_INS = ['L0_attn_x', 'L0_attn_in_W', 'L0_attn_in_b', 'L0_attn_log_dt', 'L0_attn_C', 'L0_attn_log_A_real',
        'L0_attn_A_imag', 'L0_attn_D_skip', 'L0_attn_glu_W', 'L0_attn_glu_b', 'L0_attn_out_W', 'L0_attn_out_b',
        'L0_ffn_router_w', 'L0_ffn_rms_w', 'L0_ffn_w1', 'L0_ffn_w2', 'L0_ffn_rms_w_s', 'L0_ffn_w1_s', 'L0_ffn_w2_s']


def kernel(**inputs):
    import concourse.bacc as bacc
    from concourse.bass_utils import run_bass_kernel_spmd

    nc = bacc.Bacc("TRN2", target_bir_lowering=False, num_devices=1)
    arrays, args = {}, []
    for name in _INS:
        a = np.ascontiguousarray(inputs[name])
        arrays[f"in_{name}"] = a
        args.append(nc.dram_tensor(f"in_{name}", a.shape, mybir.dt.from_np(a.dtype), kind="ExternalInput").ap())
    out = nc.dram_tensor("out_x", (2, 2048, 128), F32, kind="ExternalOutput").ap()
    build_kernel(nc, *args, out)
    r = run_bass_kernel_spmd(nc, [arrays], core_ids=[0])
    return r.results[0]["out_x"]
```

```python
from contextlib import ExitStack

import numpy as np

import concourse.bass as bass
from concourse import mybir

F32 = mybir.dt.float32
U32 = mybir.dt.uint32
ALU = mybir.AluOpType
ACT = mybir.ActivationFunctionType
AX = mybir.AxisListType

P = 128
LN_EPS = 1e-5
RMS_EPS = 1.1920929e-07
PI = float(np.pi)
MAGIC = 12582912.0
LOG2E = float(np.log2(np.e))
LN2_HI = 0.693359375
LN2_LO = float(np.log(2.0) - 0.693359375)
TWO_PI = 6.2831850
FACT = [1.0, 1.0, 2.0, 6.0, 24.0, 120.0, 720.0, 5040.0, 40320.0, 362880.0]


def build_kernel(nc, x, in_w, in_b, log_dt, c_par, log_a, a_imag, d_skip, glu_w, glu_b,
                 out_w, out_b, router_w, rms_w, w1, w2, rms_ws, w1s, w2s, out):
    B, L, D = x.shape
    N = a_imag.shape[1]
    NT = B * L // P
    NC = L // P
    NPAIR = D // 2
    NG, HG = 4, D // 4
    PG = HG // 2
    NX = D // 4
    E, ES, HID = w1.shape[0], w1s.shape[0], w1.shape[2]
    EA, HC = E + ES, HID // P
    TOKENS = B * L
    ROUTES = 2 * TOKENS
    STEP = 6
    NBLK = -(-(ROUTES // P + E - 1) // STEP) * STEP
    UNROLL = 2 * STEP
    LOOPS = (NBLK - STEP) // UNROLL
    LOADS = NBLK - STEP + UNROLL
    RB = TOKENS // P + 1
    NULL = E * RB
    NROW = (NULL + 1) * P
    ROW = D + 2
    NOWHERE = 1 << 20
    CH = NT // 4
    EARLY = 1
    BATCH = [(0, 3 * CH // 8), (3 * CH // 8, CH)]
    RANKS = 4 * E * BATCH[0][1]
    T0_ORDER = (0, 1, 3, 2)
    HALF = NC // 2
    assert (NBLK - STEP) % UNROLL == 0 and (B, L, D, N) == (2, 2048, 128, 32) and (E, ES, HID) == (14, 2, 256)

    ctx = ExitStack()
    with ctx:
        def sb(name, shape, dt=F32):
            return ctx.enter_context(nc.sbuf_tensor(name, shape, dt))

        def sem(name):
            return ctx.enter_context(nc.semaphore(name))

        bank = [ctx.enter_context(nc.psum_tensor(f"bank{i}", [P, 512], F32)) for i in range(8)]

        x_sb = sb("x_sb", [P, NT, D])
        xn = sb("xn", [P, NT, D])
        xnT = sb("xnT", [P, 2, 512])
        u = sb("u", [P, D, NT])
        v1 = sb("v1", [P, D, 2, N])
        v2 = sb("v2", [P, NPAIR, P])
        area = sb("area", [P, 13312])
        v2_flat = v2[:].rearrange("p q s -> p (q s)")
        abb = [a_.rearrange("p (h c) -> p h c", h=HG) for a_ in
               (area[:, 0:2048], area[:, 2048:4096], v2_flat[:, 3584:5632], v2_flat[:, 5632:7680])]
        mag = area[:, 4096:8192].rearrange("p (g m) -> p g m", g=NG)
        trig = area[:, 8192:12288].rearrange("p (z r m) -> p z r m", z=2, r=2)
        rnd = area[:, 12288:13312]
        s_bd = area[:, 8192:12288].rearrange("p (q e c) -> p q e c", q=NPAIR, e=2)
        st = sb("st", [P, 2, NX, NT])
        v1_flat = v1[:].rearrange("p h r n -> p (h r n)")
        xn_flat = xn[:].rearrange("p i d -> p (i d)")
        hank = [h_.rearrange("p (h t) -> p h t", h=HG)
                for h_ in (area[:, 0:4096], area[:, 4096:8192], v1_flat[:, 4096:8192], xn_flat)]
        yq = area[:, 0:4096]
        mul1 = v1_flat[:, 0:2048].rearrange("p (r x t) -> p r x t", r=2, x=NX)
        mul2 = v1_flat[:, 2048:4096].rearrange("p (r x t) -> p r x t", r=2, x=NX)
        y_sb = xn
        w1_sb = v1_flat[:, 4096:8192].rearrange("p (e m) -> p e m", e=EA)
        w2_sb = v1_flat[:, 0:4096].rearrange("p (e c d) -> p e c d", e=EA, c=HC)
        h0T = v2_flat[:, 0:4096]
        yT = v2_flat[:, 4096:5120].rearrange("p (z m) -> p z m", z=2)
        aT = v2_flat[:, 5120:6144].rearrange("p (z m) -> p z m", z=2)
        sg = v2_flat[:, 6144:7168].rearrange("p (z m) -> p z m", z=2)
        hx = area[:, 0:NT * 2 * ROW].rearrange("p (i k c) -> p i k c", i=NT, k=2)
        ysh = xn[:].rearrange("p i d -> p (i d)").rearrange("p (z e m) -> p z e m", z=2, e=ES * HC)
        u_flat = u[:].rearrange("p h c -> p (h c)")
        rt = [u_flat[:, 448 * i:448 * i + 448] for i in range(9)]
        xs = area[:, NT * 2 * ROW:NT * 2 * ROW + UNROLL * ROW].rearrange("p (z c) -> p z c", z=UNROLL)
        xsT = v2_flat[:, 0:384].rearrange("p (z c) -> p z c", z=3)
        act_sb = v2_flat[:, 384:1152].rearrange("p (z c) -> p z c", z=3)
        yb = v2_flat[:, 1152:1152 + STEP * D].rearrange("p (z c) -> p z c", z=STEP)
        wc = v2_flat[:, 5120:8192].rearrange("p (z w c) -> p z w c", z=STEP, w=2)
        yl = area[:, 0:8192].rearrange("p (i m) -> p i m", i=NT)

        ident = sb("ident", [P, P])
        exch = sb("exch", [P, P])
        srow = sb("srow", [P, 1])
        halfpi = sb("halfpi", [P, 1])
        mhalf = sb("mhalf", [P, NT])
        inb_bc = sb("inb_bc", [P, D])
        outb_bc = sb("outb_bc", [P, D])
        glub = sb("glub", [P, 2])
        dskip = sb("dskip", [HG, NG])
        wnat = v2[:, NPAIR - 4:NPAIR, :]
        wT = sb("wT", [P, 4, P])

        p33 = sb("p33", [P, N + 1])
        z33 = sb("z33", [P, N + 1])
        r33 = sb("r33", [P, N + 1])
        q33 = sb("q33", [P, N + 1])
        e33 = sb("e33", [P, N + 1])
        aim = sb("aim", [P, N])
        cpar = sb("cpar", [P, N, 2])
        ab = sb("ab", [P, 2, N])
        fr = sb("fr", [P, 2, N])
        frq = sb("frq", [P, 2, N])
        sn = sb("sn", [P, 2, N])
        cs128 = sb("cs128", [P, N])
        sh = sb("sh", [P, N])
        mag128 = sb("mag128", [P, N])
        em = sb("em", [P, N])
        ey = sb("ey", [P, N])
        inv = sb("inv", [P, N])
        den = sb("den", [P, N])
        t = [sb(f"t{i}", [P, N]) for i in range(8)]
        q1 = sb("q1", [P, 4, N])
        q2 = sb("q2", [P, 2, N])
        lw = sb("lw", [P, 6, NX])
        cbig = st[:].rearrange("p r x c -> p (r x c)").rearrange("p (g m) -> p g m", g=NG)
        ksb = sb("ksb", [HG, NG, 256])
        stats = sb("stats", [P, NT, 6])
        mv = sb("mv", [P, NT, 2])
        ve = sb("ve", [P, NT])
        vars2 = sb("vars2", [P, CH, 2, 4])
        root0 = sb("root0", [P, CH, 2, 4])
        roott = sb("roott", [P, CH, 2, 4])
        roots = sb("roots", [P, CH, 2, 4])
        rs0 = sb("rs0", [P, NT])
        rs1 = sb("rs1", [P, NT])
        rstd = sb("rstd", [P, NT])
        nmr = sb("nmr", [P, NT])

        upper = sb("upper", [P, P])
        ones = sb("ones", [P, P])
        rank_w = sb("rank_w", [P, 448])
        first = sb("first", [P, NT * E])
        region = sb("region", [P, E])
        blk = sb("blk", [P, LOADS])
        xinit = sb("xinit", [P, ROW])
        rw = sb("rw", [P, E])
        rmsn = sb("rmsn", [EA, P])
        rmsT = sb("rmsT", [P, EA])
        ybi = sb("ybi", [P, STEP])
        col = [sb(f"col{i}", [P, NT]) for i in range(8)]
        e14 = [sb(f"e14_{i}", [P, E]) for i in range(4)]
        m12 = sb("m12", [P, NT, 2])
        pos = sb("pos", [P, 2, NT], U32)
        etab = sb("etab", [P, NBLK + STEP], U32)
        btab = sb("btab", [P, LOADS], U32)
        ptab = sb("ptab", [P, E], U32)

        xs_dram = nc.dram_tensor("xs_dram", [NROW, ROW], F32, kind="Internal")
        y_dram = nc.dram_tensor("y_dram", [ROUTES, D], F32, kind="Internal")
        ab_dram = nc.dram_tensor("ab_dram", [D, 2 * N], F32, kind="Internal")
        kp_dram = nc.dram_tensor("kp_dram", [D, 256], F32, kind="Internal")

        par_in = sem("par_in")
        x_in = [sem(f"x_in{g}") for g in range(4)]
        w_in = sem("w_in")
        b_in = sem("b_in")
        const_ready = sem("const_ready")
        pool_step = sem("pool_step")
        dve_step = sem("dve_step")
        act_step = sem("act_step")
        ab_ready = sem("ab_ready")
        ab_out = sem("ab_out")
        abb_in = [sem(f"abb_in{g}") for g in range(NG)]
        abb_used = sem("abb_used")
        turns_ready = sem("turns_ready")
        psin_ready = sem("psin_ready")
        inv_ready = sem("inv_ready")
        var_ready = sem("var_ready")
        rs_ready = sem("rs_ready")
        btab_ready = sem("btab_ready")
        m12_zero = sem("m12_zero")
        pads_out = sem("pads_out")
        xn_ready = sem("xn_ready")
        scaled = sem("scaled")
        xn_act = sem("xn_act")
        wT_ps = sem("wT_ps")
        wT_ready = sem("wT_ready")
        xnT_ps = sem("xnT_ps")
        xnT_ready = sem("xnT_ready")
        u_ps = sem("u_ps")
        u_ready = sem("u_ready")
        r0_ready = sem("r0_ready")
        mag_ready = sem("mag_ready")
        arg_ready = sem("arg_ready")
        trig_ready = sem("trig_ready")
        v1_dve = sem("v1_dve")
        v1_pool = sem("v1_pool")
        v2_ps = sem("v2_ps")
        v2_act = sem("v2_act")
        q_ready = sem("q_ready")
        q_ps = sem("q_ps")
        lw_act = sem("lw_act")
        cbig_ready = sem("cbig_ready")
        cbig_zero = sem("cbig_zero")
        k_ps = sem("k_ps")
        k_ready = sem("k_ready")
        kp_out = [sem(f"kp_out{g}") for g in range(NG)]
        hank_in = [sem(f"hank_in{g}") for g in range(NG)]
        t0_ps = sem("t0_ps")
        b_ps = sem("b_ps")
        b_act = sem("b_act")
        b_dve = sem("b_dve")
        sbd_zero = sem("sbd_zero")
        scan_half = sem("scan_half")
        mul_pool = sem("mul_pool")
        mul_ready = sem("mul_ready")
        sbd_act = sem("sbd_act")
        sbd_dve = sem("sbd_dve")
        y_ps = sem("y_ps")
        yq_ready = sem("yq_ready")
        yq_ps = sem("yq_ps")
        y_dve = sem("y_dve")
        y_ready = sem("y_ready")
        xinit_ready = sem("xinit_ready")
        ew_in = sem("ew_in")
        ew2_in = sem("ew2_in")
        rms_in = sem("rms_in")
        rms_ready = sem("rms_ready")
        w1_ready = sem("w1_ready")
        yT_ps = sem("yT_ps")
        yT_ready = sem("yT_ready")
        ag_ps = sem("ag_ps")
        sg_ready = sem("sg_ready")
        aT_ready = sem("aT_ready")
        o_ps = sem("o_ps")
        x2_ready = sem("x2_ready")
        q2_ready = sem("q2_ready")
        scale_ready = sem("scale_ready")
        h0_ready = sem("h0_ready")
        ids_ready = sem("ids_ready")
        hx_ready = sem("hx_ready")
        hT_ps = sem("hT_ps")
        hT_ready = sem("hT_ready")
        r_ps = sem("r_ps")
        rstd_ready = sem("rstd_ready")
        lg_ready = sem("lg_ready")
        ex_ready = sem("ex_ready")
        m_ready = sem("m_ready")
        rank_ps = sem("rank_ps")
        pos_ready = sem("pos_ready")
        sh_ps = sem("sh_ps")
        sh_ready = sem("sh_ready")
        so_ps = sem("so_ps")
        so_added = sem("so_added")
        rows_out = sem("rows_out")
        xs_in = [sem(f"xs_in{z}") for z in range(UNROLL)]
        pool_turn = sem("pool_turn")
        xt_ps = sem("xt_ps")
        xt_ready = sem("xt_ready")
        wc_ready = sem("wc_ready")
        hid_ps = sem("hid_ps")
        act_ready = sem("act_ready")
        yb_ps = sem("yb_ps")
        yb_ready = sem("yb_ready")
        yb_out = [sem(f"yb_out{z}") for z in range(STEP)]
        y_in = [sem(f"y_in{c}") for c in range(CH)]
        sum_ready = sem("sum_ready")
        out_done = sem("out_done")

        x_tok = x.rearrange("b (c p) d -> p (b c) d", p=P)

        def table_product(engine, g, r):
            return engine.tensor_tensor(v1[:, g * HG:(g + 1) * HG, r], mag[:, g].rearrange("p (h n) -> p h n", h=HG),
                                        trig[:, g % 2, r].rearrange("p (h n) -> p h n", h=HG), ALU.mult)

        def weigh_states(engine, link, b, lo, hi):
            c = slice(NC * b + lo, NC * b + hi)
            shape = [P, 2, NX, hi - lo]
            engine.tensor_tensor(mul1[:, :, :, c], lw[:, 1:3, :].unsqueeze(3).broadcast_to(shape), st[:, :, :, c], ALU.mult)
            link(engine.tensor_tensor(mul2[:, :, :, c], lw[:, 5, :].unsqueeze(1).unsqueeze(3).broadcast_to(shape),
                                      st[:, ::-1, :, c], ALU.mult))
            return engine.tensor_tensor(mul1[:, :, :, c], mul1[:, :, :, c], mul2[:, :, :, c], ALU.add)

        def state_copy(k, r, b, lo, hi):
            m, e = k // 2, k % 2
            return (s_bd[64 * e + 32 * r:64 * e + 32 * r + 32, m::2, e, NC * b + lo + 1:NC * b + hi + 1],
                    mul1[32 * k:32 * k + 32, r, :, NC * b + lo:NC * b + hi])

        def y_tiles(i):
            return y_sb[:, :, 16 * i:16 * i + 16].rearrange("p c (x k) -> p c x k", k=4)

        block = ctx.enter_context(nc.Block())

        @block.sync
        def _(sp):
            sp.dma_start(p33[:, 0:1], log_dt.rearrange("(h o) -> h o", o=1)).then_inc(par_in, 16)
            sp.dma_start(p33[:, 1:N + 1], log_a).then_inc(par_in, 16)
            sp.dma_start(aim[:], a_imag).then_inc(par_in, 16)
            sp.dma_start(cpar[:], c_par).then_inc(par_in, 16)
            def load_x(g):
                sp.dma_start(x_sb[:, 8 * g:8 * g + 8, :], x_tok[:, 8 * g:8 * g + 8, :]).then_inc(x_in[g], 16)

            load_x(0)
            load_x(1)
            sp.wait_ge(ab_ready, 1)
            sp.dma_start(ab_dram.ap(), ab[:].rearrange("p a n -> p (a n)")).then_inc(ab_out, 16)
            sp.wait_ge(ab_out, 16)
            for g in range(NG):
                src = bass.AP(ab_dram, g * HG * 2 * N, [[0, P], [1, HG * 2 * N]])
                sp.dma_start(abb[g].rearrange("p h c -> p (h c)"), src).then_inc(abb_in[g], 16)
                if g >= 2:
                    load_x(g)
            for g in T0_ORDER:
                sp.wait_ge(k_ready, g + 1)
                sp.dma_start(kp_dram.ap()[g * HG:(g + 1) * HG, :], ksb[:, g, :]).then_inc(kp_out[g], 16)
                sp.wait_ge(kp_out[g], 16)
                if g < 2:
                    sp.wait_ge(mag_ready, NG)
                    sp.wait_ge(abb_used, NG)
                    sp.wait_ge(v1_dve, NG)
                    sp.wait_ge(v1_pool, NG)
                if g == 2:
                    sp.wait_ge(b_ps, 8)
                if g == 3:
                    sp.wait_ge(r0_ready, 4)
                    sp.wait_ge(xnT_ps, 8)
                src = bass.AP(kp_dram, g * HG * 256, [[1, P], [256, HG], [1, P]])
                sp.dma_start(hank[g], src).then_inc(hank_in[g], 16)
            sp.wait_ge(xinit_ready, 1)
            sp.dma_start(xs_dram.ap()[NULL * P:NROW, :], xinit[:]).then_inc(pads_out, 16)
            sp.wait_ge(btab_ready, 1)
            for e in range(E):
                r = sp.value_load(ptab[0:1, e:e + 1], min_val=0, max_val=(NULL - 1) * P)
                sp.dma_start(xs_dram.ap()[bass.ds(r, P), :], xinit[:]).then_inc(pads_out, 16)
            sp.wait_ge(pads_out, 16 * (E + 1))
            xs_rows = xs_dram.ap().rearrange("(b p) c -> p b c", p=P)

            def load_rows(n, z0, routed=None):
                _, places = nc.values_load_multi_w_load_instructions(
                    btab[0:1, bass.ds(n, 4)], engines=[mybir.EngineType.SP], min_val=0, max_val=NULL)
                if routed is not None:
                    sp.wait_ge(rows_out, routed)
                for z, r in enumerate(places, z0):
                    sp.dma_start(xs[:, z, :], xs_rows[:, bass.ds(r, 1), :]
                                 .rearrange("p b c -> p (b c)")).then_inc(xs_in[z], 16)

            for z in range(0, UNROLL, 4):
                load_rows(z, z, 16 * 2 * NT if z == 0 else None)
            with sp.Fori(0, LOOPS) as it:
                for z in range(0, UNROLL, 4):
                    sp.wait_ge(yb_ready, it * UNROLL + (z + 4 + 2))
                    load_rows(it * UNROLL + (UNROLL + z), z)
            y_tok = y_dram.ap().rearrange("(i p k) d -> p i (k d)", p=P, k=2)
            for z in range(STEP):
                sp.wait_ge(yb_out[z], 16 * (NBLK // STEP))
            for c in range(CH):
                rows = slice(4 * c, 4 * c + 4)
                sp.dma_start(yl[:, rows], y_tok[:, rows]).then_inc(y_in[c], 16)
            out_tok = out.rearrange("b (c p) d -> p (b c) d", p=P)
            for c in range(CH):
                rows = slice(4 * c, 4 * c + 4)
                sp.wait_ge(sum_ready, c + 1)
                sp.dma_start(out_tok[:, rows], x_sb[:, rows]).then_inc(out_done, 16)
            for z in range(UNROLL):
                sp.wait_ge(xs_in[z], 16 * (LOADS // UNROLL))
            sp.wait_ge(out_done, 16 * CH)

        @block.gpsimd
        def _(pool):
            g_ = nc.gpsimd
            steps = [0]

            def link(ins):
                steps[0] += 1
                ins.then_inc(pool_step, 1)
                pool.wait_ge(pool_step, steps[0])

            link(g_.memset(ident[:], 0.0))
            link(g_.affine_select(out=ident[:], in_=ident[:], compare_op=ALU.not_equal, fill=1.0,
                                  base=0, pattern=[[-1, P]], channel_multiplier=1))
            link(g_.memset(exch[:], 0.0))
            link(g_.affine_select(out=exch[:], in_=exch[:], compare_op=ALU.not_equal, fill=1.0,
                                  base=-(P - 1), pattern=[[1, P]], channel_multiplier=1))
            link(g_.iota(srow[:], pattern=[[0, 1]], base=0, channel_multiplier=1,
                         allow_small_or_imprecise_dtypes=True))
            g_.memset(halfpi[:], PI / 2)
            link(g_.memset(mhalf[:], -0.5))
            link(g_.memset(xinit[:], 0.0))
            g_.memset(xinit[:, D:D + 1].bitcast(U32), NOWHERE).then_inc(xinit_ready, 1)
            g_.memset(cbig[:], 0.0).then_inc(cbig_zero, 1)
            g_.memset(ksb[:], 0.0).then_inc(const_ready, 1)

            def power(g):
                pool.wait_ge(var_ready, g + 1)
                g_.tensor_tensor(rs0[:, 8 * g:8 * g + 8], ve[:, 8 * g:8 * g + 8], mhalf[:, 8 * g:8 * g + 8],
                                 ALU.pow).then_inc(rs_ready, 1)

            def imaginary_half(g):
                pool.wait_ge(mag_ready, g + 1)
                pool.wait_ge(trig_ready, g + 1)
                table_product(g_, g, 1).then_inc(v1_pool, 1)

            tt, ts = g_.tensor_tensor, g_.tensor_scalar
            pool.wait_ge(ab_ready, 1)
            link(ts(ey[:], ab[:, 0, :], -24.0, 1.0 / 32, ALU.max, ALU.mult))
            link(ts(em[:], ey[:], 1.0 / FACT[9], None, ALU.mult))
            for k in (8, 7, 6, 5, 4, 3, 2, 1):
                link(ts(em[:], em[:], 1.0 / FACT[k], None, ALU.add))
                link(tt(em[:], em[:], ey[:], ALU.mult))
            for _ in range(5):
                link(ts(ey[:], em[:], 2.0, None, ALU.add))
                link(tt(em[:], em[:], ey[:], ALU.mult))
            power(0)
            pool.wait_ge(inv_ready, 1)
            pool.wait_ge(psin_ready, 1)
            tS, cb, lr, li, er, gr, gi, tmp = t
            ar, ai = e33[:, 1:N + 1], aim[:]
            cr, ci = cpar[:, :, 0], cpar[:, :, 1]
            link(tt(sh[:], sh[:], sh[:], ALU.mult))
            ts(cb[:], sh[:], -2.0, 1.0, ALU.mult, ALU.add)
            link(ts(tS[:], sh[:], 2.0, None, ALU.mult))
            tt(er[:], em[:], cb[:], ALU.mult)
            tt(li[:], em[:], sn[:, 0, :], ALU.mult)
            link(tt(lr[:], em[:], cb[:], ALU.mult))
            tt(er[:], er[:], tS[:], ALU.subtract)
            tt(lr[:], lr[:], cb[:], ALU.add)
            link(tt(li[:], li[:], sn[:, 0, :], ALU.add))
            imaginary_half(0)
            imaginary_half(1)
            tt(gr[:], li[:], ai, ALU.mult)
            link(tt(tmp[:], er[:], ar, ALU.mult))
            link(tt(gr[:], gr[:], tmp[:], ALU.subtract))
            tt(gi[:], li[:], ar, ALU.mult)
            link(tt(tmp[:], er[:], ai, ALU.mult))
            link(tt(gi[:], gi[:], tmp[:], ALU.add))
            tt(gr[:], gr[:], inv[:], ALU.mult)
            link(tt(gi[:], gi[:], inv[:], ALU.mult))
            tt(er[:], gr[:], cr, ALU.mult)
            tt(tS[:], gi[:], ci, ALU.mult)
            tt(cb[:], gr[:], ci, ALU.mult)
            link(tt(tmp[:], gi[:], cr, ALU.mult))
            tt(er[:], er[:], tS[:], ALU.add)
            link(tt(cb[:], cb[:], tmp[:], ALU.subtract))
            ts(q2[:, 0, :], er[:], 2.0, None, ALU.mult)
            link(ts(q2[:, 1, :], cb[:], -2.0, None, ALU.mult))
            tt(er[:], q2[:, 0, :], lr[:], ALU.mult)
            tt(tS[:], q2[:, 1, :], li[:], ALU.mult)
            tt(cb[:], q2[:, 0, :], li[:], ALU.mult)
            link(tt(tmp[:], q2[:, 1, :], lr[:], ALU.mult))
            tt(q1[:, 2, :], er[:], tS[:], ALU.add)
            tt(q1[:, 3, :], cb[:], tmp[:], ALU.subtract)
            tt(q1[:, 0, :], mag128[:], cs128[:], ALU.mult)
            link(tt(q1[:, 1, :], mag128[:], sn[:, 1, :], ALU.mult))
            g_.engine_nop().then_inc(q_ready, 1)
            imaginary_half(2)
            power(1)
            imaginary_half(3)
            power(2)
            power(3)
            link(g_.memset(ones[:], 1.0))
            link(g_.affine_select(out=upper[:], in_=ones[:], compare_op=ALU.is_gt, fill=0.0,
                                  base=0, pattern=[[1, P]], channel_multiplier=-1))
            g_.iota(rank_w[:], pattern=[[0, NT], [-1, E]], base=E, channel_multiplier=0,
                    allow_small_or_imprecise_dtypes=True)
            g_.iota(region[:], pattern=[[RB * P, E]], base=0, channel_multiplier=0,
                    allow_small_or_imprecise_dtypes=True)
            g_.iota(blk[:], pattern=[[1, LOADS]], base=0, channel_multiplier=0,
                    allow_small_or_imprecise_dtypes=True)
            g_.memset(m12[:], 0.0).then_inc(m12_zero, 1)
            link(g_.memset(first[:], 1.0))
            for lo, hi in BATCH:
                link(g_.memset(first[:, 4 * E * lo:4 * E * hi].rearrange("p (e i) -> p e i", e=E)[:, :, 0:1], 0.0))
            for g in range(4):
                rows = slice(8 * g, 8 * g + 8)
                pool.wait_ge(*((xn_ready, g + 1) if g < 3 else (xn_act, 1)))
                link(g_.tensor_tensor(x_sb[:, rows], x_sb[:, rows], xn[:, rows], ALU.add))
                g_.tensor_tensor(x_sb[:, rows], x_sb[:, rows], outb_bc[:].unsqueeze(1).broadcast_to([P, 8, D]),
                                 ALU.add).then_inc(r0_ready, 1)
            pool.wait_ge(v1_dve, NG)
            pool.wait_ge(v1_pool, NG)
            g_.memset(area[:, 8192:12288], 0.0).then_inc(sbd_zero, 1)

            pool.wait_ge(scan_half, 1)
            for b in range(B):
                weigh_states(g_, link, b, 0, HALF).then_inc(mul_pool, 1)
            pool.wait_ge(yq_ps, 8)
            ids = hx[:, :, :, D:D + 1].bitcast(U32).rearrange("p i k o -> p i (k o)")
            g_.iota(ids, pattern=[[2 * P, NT], [1, 2]], base=0, channel_multiplier=2).then_inc(ids_ready, 1)

            def send_rows(lo, hi):
                for i in range(lo, hi):
                    for k in range(2):
                        pool.indirect_dma_start(out=xs_dram.ap(), out_offset=bass.IndirectOffsetOnAxis(ap=pos[:, k, i:i + 1], axis=0),
                                                in_=hx[:, i, k, :], in_offset=None, bounds_check=NROW - 1,
                                                oob_is_err=False).then_inc(rows_out, 16)

            for c in range(CH):
                if c == CH - 1:
                    pool.wait_ge(ids_ready, 1)
                    pool.wait_ge(hx_ready, BATCH[0][1])
                    pool.wait_ge(pos_ready, 1)
                    send_rows(0, EARLY)
                pool.wait_ge(q2_ready, c + 1)
                src, r0, tmp = vars2[:, c], root0[:, c], roott[:, c]
                link(tt(r0, src, mhalf[:, 0:8].rearrange("p (a i) -> p a i", a=2), ALU.pow))
                link(tt(tmp, r0, r0, ALU.mult))
                link(tt(tmp, tmp, src, ALU.mult))
                link(ts(tmp, tmp, -0.5, 1.5, ALU.mult, ALU.add))
                link(tt(roots[:, c], r0, tmp, ALU.mult))
                g_.engine_nop().then_inc(scale_ready, 1)
                k = slice(4 * c, 4 * c + 4)
                link(tt(rstd[:, k], roots[:, c, 0], roots[:, c, 1], ALU.mult))
                tt(rstd[:, k], rstd[:, k], vars2[:, c, 0], ALU.mult).then_inc(rstd_ready, 1)

            send_rows(EARLY, 4 * BATCH[0][1])
            pool.wait_ge(hx_ready, CH)
            pool.wait_ge(pos_ready, 2)
            send_rows(4 * BATCH[1][0], NT)
            last_row = pool.to_reg(ROUTES - 1)
            def send_block(z):
                pool.indirect_dma_start(out=y_dram.ap(), out_offset=bass.IndirectOffsetOnAxis(ap=ybi[:, z:z + 1].bitcast(U32), axis=0),
                                        in_=yb[:, z, :], in_offset=None, bounds_check=last_row,
                                        oob_is_err=False).then_inc(yb_out[z], 16)

            for z in range(STEP):
                pool.wait_ge(yb_ready, z + 1 + 2)
                send_block(z)
            with pool.Fori(0, LOOPS) as it:
                for z in range(UNROLL):
                    pool.wait_ge(yb_ready, it * UNROLL + (STEP + z + 1 + 2))
                    g_.sem_inc(pool_turn, 1)
                    send_block(z % STEP)

        @block.vector
        def _(dve):
            v = nc.vector
            steps = [0]

            def link(ins):
                steps[0] += 1
                ins.then_inc(dve_step, 1)
                dve.wait_ge(dve_step, steps[0])

            dve.wait_ge(par_in, 64)
            link(v.tensor_scalar(p33[:], p33[:], -87.0, 88.0, ALU.max, ALU.min))
            link(v.tensor_scalar(z33[:], p33[:], LOG2E, MAGIC + 127.0, ALU.mult, ALU.add))
            link(v.tensor_scalar(q33[:], z33[:], -(MAGIC + 127.0), None, ALU.add))
            link(v.scalar_tensor_tensor(out=r33[:], in0=q33[:], scalar=-LN2_HI, in1=p33[:], op0=ALU.mult, op1=ALU.add))
            link(v.scalar_tensor_tensor(out=r33[:], in0=q33[:], scalar=-LN2_LO, in1=r33[:], op0=ALU.mult, op1=ALU.add))
            link(v.tensor_scalar(q33[:], r33[:], 1.0 / FACT[7], None, ALU.mult))
            for k in (6, 5, 4, 3, 2, 1):
                link(v.scalar_tensor_tensor(out=q33[:], in0=q33[:], scalar=1.0 / FACT[k], in1=r33[:],
                                            op0=ALU.add, op1=ALU.mult))
            link(v.tensor_scalar(z33[:].bitcast(U32), z33[:].bitcast(U32), 23, None, ALU.logical_shift_left))
            link(v.scalar_tensor_tensor(out=e33[:], in0=q33[:], scalar=1.0, in1=z33[:], op0=ALU.add, op1=ALU.mult))
            v.tensor_scalar(ab[:, 0, :], e33[:, 1:N + 1], e33[:, 0:1], -1.0, ALU.mult, ALU.mult)
            link(v.tensor_scalar(ab[:, 1, :], aim[:], e33[:, 0:1], 1.0 / (2 * PI), ALU.mult, ALU.mult))
            v.engine_nop().then_inc(ab_ready, 1)
            v.tensor_copy(fr[:, 0, :], ab[:, 1, :])
            link(v.tensor_scalar(fr[:, 1, :], ab[:, 1, :], float(P), None, ALU.mult))
            link(v.tensor_scalar(frq[:], fr[:], MAGIC, None, ALU.add))
            link(v.tensor_scalar(frq[:], frq[:], -MAGIC, None, ALU.add))
            link(v.tensor_tensor(fr[:], fr[:], frq[:], ALU.subtract))
            v.tensor_scalar(frq[:].bitcast(U32), fr[:].bitcast(U32), 0x7FFFFFFF, None, ALU.bitwise_and).then_inc(turns_ready, 1)
            v.tensor_tensor(den[:], e33[:, 1:N + 1], e33[:, 1:N + 1], ALU.mult)
            link(v.tensor_tensor(inv[:], aim[:], aim[:], ALU.mult))
            link(v.tensor_tensor(den[:], den[:], inv[:], ALU.add))
            v.reciprocal(inv[:], den[:]).then_inc(inv_ready, 1)

            def ln_stats(g):
                dve.wait_ge(x_in[g], 16)
                for i in range(8 * g, 8 * g + 8):
                    last = v.bn_stats(stats[:, i, :], x_sb[:, i, :])
                link(last)
                for i in range(8 * g, 8 * g + 8):
                    last = v.bn_aggr(mv[:, i, :], stats[:, i, :])
                link(last)
                v.tensor_scalar(ve[:, 8 * g:8 * g + 8], mv[:, 8 * g:8 * g + 8, 1], LN_EPS, None,
                                ALU.add).then_inc(var_ready, 1)

            def ln_scale(g):
                c = slice(8 * g, 8 * g + 8)
                dve.wait_ge(rs_ready, g + 1)
                link(v.tensor_tensor(rs1[:, c], rs0[:, c], rs0[:, c], ALU.mult))
                link(v.tensor_tensor(rs1[:, c], rs1[:, c], ve[:, c], ALU.mult))
                link(v.tensor_scalar(rs1[:, c], rs1[:, c], -0.5, 1.5, ALU.mult, ALU.add))
                link(v.tensor_tensor(rstd[:, c], rs1[:, c], rs0[:, c], ALU.mult))
                if g == 3:
                    v.scalar_tensor_tensor(out=nmr[:, c], in0=mv[:, c, 0], scalar=-1.0, in1=rstd[:, c],
                                           op0=ALU.mult, op1=ALU.mult).then_inc(scaled, 1)

            def ln_norm(g):
                ln_scale(g)
                for i in range(8 * g, 8 * g + 8):
                    last = v.tensor_scalar(xn[:, i, :], x_sb[:, i, :], mv[:, i, 0:1], rstd[:, i:i + 1],
                                           ALU.subtract, ALU.mult)
                last.then_inc(xn_ready, 1)

            def table_args(g):
                dve.wait_ge(abb_in[g], 16)
                if g >= 2:
                    dve.wait_ge(v1_pool, g - 1)
                    dve.wait_ge(v1_dve, g - 1)
                f = abb[g][:, :, N:2 * N]
                rv = rnd.rearrange("p (h n) -> p h n", h=HG)
                arg = trig[:, g % 2, 1].rearrange("p (h n) -> p h n", h=HG)
                link(v.tensor_scalar(rv, f, srow[:, 0:1], MAGIC, ALU.mult, ALU.add))
                link(v.tensor_scalar(rnd, rnd, -MAGIC, None, ALU.add))
                ins = v.scalar_tensor_tensor(out=arg, in0=f, scalar=srow[:, 0:1], in1=rv,
                                             op0=ALU.mult, op1=ALU.subtract)
                link(ins)
                v.tensor_scalar(trig[:, g % 2, 0].bitcast(U32), trig[:, g % 2, 1].bitcast(U32), 0x7FFFFFFF, None,
                                ALU.bitwise_and).then_inc(arg_ready, 1)
                v.engine_nop().then_inc(abb_used, 1)

            def evict_u(i):
                dve.wait_ge(u_ps, i + 1)
                src = bank[2 + i % 2][:].rearrange("p (c h) -> p h c", c=4)
                v.tensor_tensor(u[:, :, 4 * i:4 * i + 4], src, inb_bc[:].unsqueeze(2).broadcast_to([P, D, 4]),
                                ALU.add).then_inc(u_ready, 1)

            def real_half(g):
                dve.wait_ge(mag_ready, g + 1)
                dve.wait_ge(trig_ready, g + 1)
                table_product(v, g, 0).then_inc(v1_dve, 1)

            def evict_k(g):
                dve.wait_ge(k_ps, g + 1)
                link(v.tensor_copy(ksb[:, g, 127:255], bank[7][HG * g:HG * g + HG, 0:P]))
                v.tensor_tensor(ksb[:, g, 127:128], ksb[:, g, 127:128], dskip[:, g:g + 1], ALU.add).then_inc(k_ready, 1)

            dve.wait_ge(const_ready, 1)
            ln_stats(0)
            ln_stats(1)
            table_args(0)
            table_args(1)
            real_half(0)
            ln_norm(0)
            table_args(2)
            real_half(1)
            table_args(3)
            dve.wait_ge(b_in, 64)
            evict_u(0)
            evict_u(1)
            dve.wait_ge(q_ps, 1)
            dve.wait_ge(cbig_zero, 1)
            for e in range(2):
                dst = cbig[64 * e:64 * e + 64].rearrange("p g m -> p (g m)")
                for g in range(NG):
                    lo = 512 * g + e
                    last = v.tensor_copy(dst[:, lo:lo + 34 * 15 + 1:34], bank[3][0:64, HG * g + e:HG * (g + 1):2])
            last.then_inc(cbig_ready, 1)
            real_half(2)
            real_half(3)
            dve.wait_ge(lw_act, 1)
            v.tensor_scalar(lw[:, 2, :], lw[:, 1, :], -1.0, None, ALU.mult)
            v.tensor_scalar(lw[:, 3, :], lw[:, 4, :], -1.0, None, ALU.mult)
            link(v.tensor_scalar(lw[:, 5, :], lw[:, 5, :], -1.0, None, ALU.mult))
            ln_stats(2)
            ln_norm(1)
            evict_k(0)
            ln_stats(3)
            evict_k(1)
            ln_norm(2)
            evict_u(2)
            evict_u(3)
            ln_scale(3)
            evict_k(2)
            evict_k(3)
            for i in range(4, 8):
                evict_u(i)

            for i in range(8):
                dve.wait_ge(b_ps, i + 1)
                for m in range(2):
                    k = 2 * m + 1
                    for r in range(2):
                        src = bank[i][64 + 32 * r:96 + 32 * r].rearrange(
                            "p (j m e c) -> p j m e c", j=4, m=2, e=2)[:, :, m, 1, :]
                        last = v.tensor_copy(st[32 * k:32 * k + 32, r, 4 * i:4 * i + 4, :], src)
                last.then_inc(b_dve, 1)
            link(v.engine_nop())
            dve.wait_ge(b_act, 8)
            sv = st[:].rearrange("p r x (b j) -> p r x b j", b=B)
            m1, m2 = [rnd[:, 128 * i:128 * i + 128].rearrange("p (r x b) -> p r x b", r=2, x=NX) for i in range(2)]
            lr_b = lw[:, 0, :].unsqueeze(1).unsqueeze(3).broadcast_to([P, 2, NX, B])
            li_b = lw[:, 3:5, :].unsqueeze(3).broadcast_to([P, 2, NX, B])
            dve.wait_ge(v2_ps, 16)
            for j in range(1, NC - 1):
                v.tensor_tensor(m1, lr_b, sv[:, :, :, :, j - 1], ALU.mult).then_inc(dve_step, 1)
                v.tensor_tensor(m2, li_b, sv[:, ::-1, :, :, j - 1], ALU.mult).then_inc(dve_step, 1)
                dve.wait_ge(dve_step, steps[0] + 1)
                steps[0] += 2
                link(v.tensor_tensor(sv[:, :, :, :, j], sv[:, :, :, :, j], m1, ALU.add))
                link(v.tensor_tensor(sv[:, :, :, :, j], sv[:, :, :, :, j], m2, ALU.add))
                if j == HALF - 1:
                    v.engine_nop().then_inc(scan_half, 1)
            for b in range(B):
                link(weigh_states(v, link, b, HALF, NC - 1))
                v.engine_nop().then_inc(mul_ready, 1)
            dve.wait_ge(sbd_zero, 1)
            for b in range(B):
                for k in (1, 3):
                    for r in range(2):
                        dst, src = state_copy(k, r, b, HALF, NC - 1)
                        last = v.tensor_copy(dst, src)
            last.then_inc(sbd_dve, 1)

            for i in range(1, 8, 2):
                dve.wait_ge(yq_ps, i + 1)
                v.tensor_copy(y_tiles(i), bank[i][:].rearrange("p (x k c) -> p c x k", x=4, k=4)).then_inc(y_dve, 1)

            def glu(c):
                dve.wait_ge(sg_ready, c + 1)
                if c >= 2:
                    dve.wait_ge(o_ps, c - 1)
                v.scalar_tensor_tensor(out=aT[:, c % 2], in0=bank[2][:], scalar=glub[:, 0:1], in1=sg[:, c % 2],
                                       op0=ALU.add, op1=ALU.mult).then_inc(aT_ready, 1)

            def residual(c):
                rows = x_sb[:, 4 * c:4 * c + 4]
                dve.wait_ge(o_ps, c + 1)
                ins = v.tensor_tensor(rows, bank[4][:].rearrange("p (i d) -> p i d", i=4), rows, ALU.add)
                link(ins)
                v.engine_nop().then_inc(x2_ready, 1)
                for i in range(4 * c, 4 * c + 4):
                    last = v.bn_stats(stats[:, i, :], x_sb[:, i, :])
                link(last)
                for i in range(4 * c, 4 * c + 4):
                    last = v.bn_aggr(mv[:, i, :], stats[:, i, :])
                link(last)
                v.tensor_scalar(vars2[:, c, 1], mv[:, 4 * c:4 * c + 4, 1], LN_EPS, None, ALU.add)
                link(v.tensor_scalar(vars2[:, c, 0], mv[:, 4 * c:4 * c + 4, 1], 1.0 + RMS_EPS, RMS_EPS * LN_EPS,
                                     ALU.mult, ALU.add))
                v.engine_nop().then_inc(q2_ready, 1)

            def normalise(c):
                dve.wait_ge(scale_ready, c + 1)
                for i in range(4 * c, 4 * c + 4):
                    last = v.tensor_scalar(hx[:, i, 0, 0:D], x_sb[:, i, :], mv[:, i, 0:1], roots[:, c, 0, i - 4 * c:i - 4 * c + 1],
                                           ALU.subtract, ALU.mult)
                last.then_inc(h0_ready, 1)

            def te(a):
                return a.rearrange("p (i e) -> p i e", e=E)

            def tb(a):
                return a.unsqueeze(2).broadcast_to([P, a.shape[1], E])

            ei = "p (e i) -> p e i"
            after, nb, cnb, wgt = [x_[:] for x_ in e14]

            def batch(b):
                bt = slice(4 * BATCH[b][0], 4 * BATCH[b][1])
                return bt, [a_[:, E * bt.start:E * bt.stop] for a_ in rt], [c_[:, bt] for c_ in col]

            def choose_experts(b):
                bt, (lg, gt, oh1, oh2, sc, p2, _, _, _), (mx, _, _, m2_, r1, _, _, _) = batch(b)
                rank = rank_w[:, 0:E * (bt.stop - bt.start)]
                dve.wait_ge(m12_zero, 1)
                dve.wait_ge(r_ps, b + 1)
                dve.wait_ge(rstd_ready, BATCH[b][1])
                link(v.tensor_tensor(te(lg), te(bank[6 + b][:, 0:E * (bt.stop - bt.start)]), tb(rstd[:, bt]), ALU.mult))
                link(v.tensor_reduce(mx, te(lg), AX.X, ALU.max))

                def choose(best, values, out_):
                    link(v.tensor_tensor(te(sc), te(values), tb(best), ALU.is_equal))
                    link(v.tensor_tensor(sc, sc, rank, ALU.mult))
                    link(v.tensor_reduce(r1, te(sc), AX.X, ALU.max))
                    return v.tensor_tensor(te(out_), te(sc), tb(r1), ALU.is_equal)

                link(choose(mx, lg, oh1))
                link(v.scalar_tensor_tensor(out=p2, in0=oh1, scalar=-3e38, in1=lg, op0=ALU.mult, op1=ALU.add))
                link(v.tensor_reduce(m2_, te(p2), AX.X, ALU.max))
                link(choose(m2_, p2, oh2))
                v.tensor_tensor(p2, oh1, oh2, ALU.add).then_inc(m_ready, 1)
                v.tensor_tensor(te(lg), te(lg), tb(mx), ALU.subtract)
                v.tensor_tensor(m12[:, bt, 1], m2_, mx, ALU.subtract).then_inc(lg_ready, 1)

            def place_routes(b):
                bt, (_, gt, oh1, oh2, _, _, cntT, incl, slot), (mx, z1, m1_, _, _, gs, _, _) = batch(b)
                n = E * (bt.stop - bt.start)
                dve.wait_ge(rank_ps, b + 1)
                link(v.tensor_copy(cntT.rearrange(ei, e=E), te(bank[6 + b][:, 0:n]).rearrange("p i e -> p e i")))
                link(v.tensor_tensor_scan(incl, first[:, E * bt.start:E * bt.stop], cntT, 0.0, ALU.mult, ALU.add))
                before = region[:] if b == 0 else after
                link(v.tensor_tensor(cntT, incl, cntT, ALU.subtract))
                link(v.tensor_tensor(cntT.rearrange(ei, e=E), cntT.rearrange(ei, e=E), before.unsqueeze(2).broadcast_to([P, E, n // E]), ALU.add))
                v.tensor_tensor(after, before, incl.rearrange(ei, e=E)[:, :, n // E - 1], ALU.add)
                link(v.tensor_tensor(te(slot), te(bank[6][:, RANKS:RANKS + n]), cntT.rearrange(ei, e=E).rearrange("p e i -> p i e"), ALU.add))
                link(v.tensor_tensor(oh1, oh1, slot, ALU.mult))
                link(v.tensor_tensor(oh2, oh2, slot, ALU.mult))
                v.tensor_reduce(mx, te(oh1), AX.X, ALU.add)
                link(v.tensor_reduce(z1, te(oh2), AX.X, ALU.add))
                v.tensor_copy(pos[:, 0, bt], mx)
                link(v.tensor_copy(pos[:, 1, bt], z1))
                dve.wait_ge(ex_ready, b + 1)
                v.tensor_tensor(m1_, m12[:, bt, 0], m12[:, bt, 1], ALU.add)
                link(v.tensor_reduce(z1, te(gt), AX.X, ALU.add))
                link(v.scalar_tensor_tensor(out=gs, in0=z1, scalar=1e-9, in1=m1_, op0=ALU.mult, op1=ALU.add))
                link(v.reciprocal(gs, gs))
                for k in range(2):
                    last = v.tensor_tensor(hx[:, bt, k, D + 1], m12[:, bt, k], gs, ALU.mult)
                last.then_inc(pos_ready, 1)

            dve.wait_ge(yq_ps, 8)
            for i in range(CH + 2):
                if i < CH:
                    glu(i)
                if 0 <= i - 1 < CH:
                    residual(i - 1)
                if 0 <= i - 2 < CH:
                    normalise(i - 2)
                if i == CH - 2:
                    choose_experts(0)
                if i == CH - 1:
                    place_routes(0)

            def add_shared(c):
                dve.wait_ge(so_ps, c + 1)
                rows = x_sb[:, 4 * c:4 * c + 4]
                v.tensor_tensor(rows, bank[4 + c % 2][:].rearrange("p (i d) -> p i d", i=4), rows,
                                ALU.add).then_inc(so_added, 1)

            choose_experts(1)
            place_routes(1)
            v.tensor_copy(ptab[0:1], after[0:1])
            link(v.tensor_tensor(nb[0:1], after[0:1], region[0:1], ALU.subtract))
            link(v.tensor_scalar(nb[0:1], nb[0:1], 1.0 / P, (P - 1) / P - 0.5 + 1.0 / (2 * P), ALU.mult, ALU.add))
            link(v.tensor_scalar(nb[0:1], nb[0:1], MAGIC, None, ALU.add))
            link(v.tensor_scalar(nb[0:1], nb[0:1], -MAGIC, None, ALU.add))
            link(v.tensor_tensor_scan(cnb[0:1], ones[0:1, 0:E], nb[0:1], 0.0, ALU.mult, ALU.add))
            link(v.tensor_scalar(wgt[0:1], nb[0:1], -1.0, float(RB), ALU.mult, ALU.add))
            link(v.tensor_scalar(wgt[0:1, E - 1:E], nb[0:1, E - 1:E], 0.0, float(2 * NULL), ALU.mult, ALU.add))
            ended = v2_flat[0:1, 5120:5120 + LOADS * E].rearrange("p (b e) -> p b e", e=E)
            esum, bsum = rt[4][0:1, 0:LOADS], rt[5][0:1, 0:LOADS]
            link(v.tensor_tensor(ended, cnb[0:1].unsqueeze(1).broadcast_to([1, LOADS, E]),
                                 blk[0:1, :].unsqueeze(2).broadcast_to([1, LOADS, E]), ALU.is_le))
            link(v.tensor_reduce(esum, ended[:, :, 0:E - 1], AX.X, ALU.add))
            link(v.tensor_scalar(etab[0:1, :], esum[:, 0:NBLK + STEP], float(HID), None, ALU.mult))
            link(v.tensor_tensor(ended, ended, wgt[0:1].unsqueeze(1).broadcast_to([1, LOADS, E]), ALU.mult))
            link(v.tensor_reduce(bsum, ended, AX.X, ALU.add))
            link(v.tensor_tensor(bsum, bsum, blk[0:1, :], ALU.add))
            v.tensor_scalar(btab[0:1, :], bsum, float(NULL), None, ALU.min).then_inc(btab_ready, 1)

            dve.wait_ge(o_ps, CH)
            v.engine_nop().then_inc(yb_ready, 2)

            def fetch_weights(at, z):
                r = dve.value_load(etab[0:1, bass.ds(at, 1)], min_val=0, max_val=(E - 1) * HID)
                v.tensor_copy(wc[:, z % STEP], v1_flat.rearrange("p (w m) -> p w m", w=2)[:, :, bass.ds(r, HID)]).then_inc(wc_ready, 1)

            dve.wait_ge(w1_ready, CH)
            dve.wait_ge(ew2_in, 16 * 2 * HC)
            for z in range(STEP - 1):
                fetch_weights(z, z)
            for c in range(CH):
                add_shared(c)

            def finish_block(n, z):
                row = z % UNROLL
                z = z % STEP
                dve.wait_ge(yb_ps, n + 4)
                v.tensor_copy(ybi[:, z:z + 1].bitcast(U32), xs[:, row, D:D + 1].bitcast(U32))
                v.tensor_scalar(yb[:, z], bank[4 + z % 2][:, 0:D], xs[:, row, D + 1:D + 2], None,
                                ALU.mult).then_inc(yb_ready, 1)
                fetch_weights(n + STEP - 1, z + STEP - 1)

            for z in range(STEP):
                finish_block(z, z)
            with dve.Fori(0, LOOPS) as it:
                for z in range(UNROLL):
                    dve.wait_ge(yb_out[z % STEP], it * (16 * UNROLL // STEP) + 16 * (1 + z // STEP))
                    finish_block(it * UNROLL + (STEP + z), STEP + z)
            for c in range(CH):
                rows = slice(4 * c, 4 * c + 4)
                dve.wait_ge(y_in[c], 16)
                link(v.tensor_tensor(x_sb[:, rows], x_sb[:, rows], yl[:, rows, 0:D], ALU.add))
                v.tensor_tensor(x_sb[:, rows], x_sb[:, rows], yl[:, rows, D:2 * D], ALU.add).then_inc(sum_ready, 1)

        @block.scalar
        def _(act):
            a = nc.scalar
            steps = [0]

            def link(ins):
                steps[0] += 1
                ins.then_inc(act_step, 1)
                act.wait_ge(act_step, steps[0])

            act.dma_start(wnat[:, 0, :], in_w).then_inc(w_in, 16)
            act.dma_start(wnat[:, 1:3, :], glu_w.rearrange("(c p) h -> p c h", p=P)).then_inc(w_in, 16)
            act.dma_start(wnat[:, 3, :], out_w).then_inc(w_in, 16)
            act.dma_start(inb_bc[:], in_b.partition_broadcast(P)).then_inc(b_in, 16)
            act.dma_start(outb_bc[:], out_b.partition_broadcast(P)).then_inc(b_in, 16)
            act.dma_start(glub[:], glu_b.rearrange("(c p) -> p c", p=P), allow_slow_non_contiguous=True).then_inc(b_in, 16)
            act.dma_start(rmsn[0:E, :], rms_w).then_inc(rms_in, 16)
            act.dma_start(rmsn[E:EA, :], rms_ws).then_inc(rms_in, 16)
            act.dma_start(rw[:], router_w).then_inc(rms_in, 16)
            act.dma_start(dskip[:], d_skip.rearrange("(g p) -> p g", p=HG), allow_slow_non_contiguous=True).then_inc(b_in, 16)

            def evict_xnT(i):
                act.wait_ge(xnT_ps, i + 1)
                if i >= 2:
                    act.wait_ge(u_ps, i - 1)
                a.copy(xnT[:, i % 2, :], bank[i % 2][:]).then_inc(xnT_ready, 1)

            act.wait_ge(const_ready, 1)
            act.wait_ge(ab_ready, 1)
            a.activation(mag128[:], ab[:, 0, :], ACT.Exp, scale=float(P))
            act.wait_ge(wT_ps, 1)
            a.copy(wT[:].rearrange("p c m -> p (c m)"), bank[4][:]).then_inc(wT_ready, 1)
            a.copy(rmsT[:], bank[5][:, 0:EA]).then_inc(rms_ready, 1)

            def magnitude(g):
                act.wait_ge(abb_in[g], 16)
                a.activation(mag[:, g].rearrange("p (h n) -> p h n", h=HG), abb[g][:, :, 0:N], ACT.Exp,
                             scale=srow[:, 0:1]).then_inc(mag_ready, 1)

            def sines(g):
                act.wait_ge(arg_ready, g + 1)
                a.activation(trig[:, g % 2, 1], trig[:, g % 2, 1], ACT.Sin, scale=TWO_PI)
                a.activation(trig[:, g % 2, 0], trig[:, g % 2, 0], ACT.Sin, scale=-TWO_PI,
                             bias=halfpi[:]).then_inc(trig_ready, 1)

            act.wait_ge(turns_ready, 1)
            a.activation(sn[:], fr[:], ACT.Sin, scale=TWO_PI)
            a.activation(cs128[:], frq[:, 1, :], ACT.Sin, scale=-TWO_PI, bias=halfpi[:])
            a.activation(sh[:], fr[:, 0, :], ACT.Sin, scale=TWO_PI / 2).then_inc(psin_ready, 1)
            magnitude(0)
            magnitude(1)
            sines(0)
            sines(1)
            def evict_v2(g):
                for i in range(4 * g, 4 * g + 4):
                    act.wait_ge(v2_ps, i + 1)
                    a.copy(v2[:, 4 * i:4 * i + 4, :], bank[4 + i % 3][:]
                           .rearrange("p (q s) -> p q s", q=4)).then_inc(v2_act, 1)

            def normalise_x(g):
                act.wait_ge(scaled, 1)
                for i in range(8 * g, 8 * g + 8):
                    last = a.activation(xn[:, i, :], x_sb[:, i, :], ACT.Identity, bias=nmr[:, i:i + 1],
                                        scale=rstd[:, i:i + 1])
                last.then_inc(xn_act, 1)

            magnitude(2)
            magnitude(3)
            evict_v2(0)
            evict_xnT(0)
            evict_xnT(1)
            sines(2)
            sines(3)
            act.wait_ge(q_ps, 1)
            for k in range(4):
                for q, to in enumerate((0, 4, 1, 5)):
                    last = a.copy(lw[32 * k:32 * k + 32, to, :], bank[0][32 * q:32 * q + 32, k:P:4])
            last.then_inc(lw_act, 1)
            act.wait_ge(abb_used, NG)
            evict_v2(1)
            evict_v2(2)
            evict_xnT(2)
            evict_xnT(3)
            evict_v2(3)
            evict_xnT(4)
            evict_xnT(5)
            normalise_x(3)
            evict_xnT(6)
            evict_xnT(7)
            for i in range(8):
                act.wait_ge(b_ps, i + 1)
                for m in range(2):
                    k = 2 * m
                    for r in range(2):
                        src = bank[i][32 * r:32 + 32 * r].rearrange(
                            "p (j m e c) -> p j m e c", j=4, m=2, e=2)[:, :, m, 0, :]
                        last = a.copy(st[32 * k:32 * k + 32, r, 4 * i:4 * i + 4, :], src)
                last.then_inc(b_act, 1)
            act.wait_ge(sbd_zero, 1)
            for b in range(B):
                act.wait_ge(mul_pool, b + 1)
                for k in range(4):
                    for r in range(2):
                        dst, src = state_copy(k, r, b, 0, HALF)
                        a.copy(dst, src)
            for b in range(B):
                act.wait_ge(mul_ready, b + 1)
                for k in (0, 2):
                    for r in range(2):
                        dst, src = state_copy(k, r, b, HALF, NC - 1)
                        last = a.copy(dst, src)
            last.then_inc(sbd_act, 1)
            act.wait_ge(t0_ps, NG)
            act.dma_start(w1_sb[:, 0:E], w1.rearrange("e p m -> p e m")).then_inc(ew_in, 16)
            act.dma_start(w1_sb[:, E:EA], w1s.rearrange("e p m -> p e m")).then_inc(ew_in, 16)
            act.wait_ge(sbd_dve, 1)
            act.wait_ge(sbd_act, 1)
            for c in range(HC):
                act.dma_start(w2_sb[:, 0:E, c], w2.rearrange("e (c p) d -> c p e d", c=HC)[c]).then_inc(ew2_in, 16)
                act.dma_start(w2_sb[:, E:EA, c], w2s.rearrange("e (c p) d -> c p e d", c=HC)[c]).then_inc(ew2_in, 16)
            act.wait_ge(t0_ps, 4)
            for i in range(8):
                act.wait_ge(y_ps, i + 1)
                a.activation(yq[:, 512 * i:512 * i + 512], bank[i][:], ACT.Gelu).then_inc(yq_ready, 1)
            for i in range(0, 8, 2):
                act.wait_ge(yq_ps, i + 1)
                a.copy(y_tiles(i), bank[i][:].rearrange("p (x k c) -> p c x k", x=4, k=4)).then_inc(y_ready, 1)


            def copy_yT(c):
                act.wait_ge(yT_ps, c + 1)
                if c >= 2:
                    act.wait_ge(ag_ps, c - 1)
                a.copy(yT[:, c % 2], bank[c % 2][:]).then_inc(yT_ready, 1)

            def gate_glu(c):
                act.wait_ge(ag_ps, c + 1)
                if c >= 2:
                    act.wait_ge(aT_ready, c - 1)
                a.activation(sg[:, c % 2], bank[3][:], ACT.Sigmoid, bias=glub[:, 1:2]).then_inc(sg_ready, 1)

            def exp_logits(b):
                act.wait_ge(m12_zero, 1)
                act.wait_ge(lg_ready, b + 1)
                lo, hi = 4 * BATCH[b][0], 4 * BATCH[b][1]
                chosen = m12[:, lo:hi].rearrange("p i k -> p (i k)")
                a.activation(chosen, chosen, ACT.Exp)
                a.activation(rt[1][:, E * lo:E * hi], rt[0][:, E * lo:E * hi], ACT.Exp).then_inc(ex_ready, 1)

            copy_yT(0)
            for i in range(CH + 3):
                if i < CH:
                    gate_glu(i)
                if i + 1 < CH:
                    copy_yT(i + 1)
                if 0 <= i - 3 < CH:
                    c = i - 3
                    k = slice(4 * c, 4 * c + 4)
                    act.wait_ge(h0_ready, c + 1)
                    a.copy(hx[:, k, 1, 0:D], hx[:, k, 0, 0:D]).then_inc(hx_ready, 1)
                    act.wait_ge(hT_ps, c + 1)
                    a.copy(h0T[:, 512 * c:512 * c + 512], bank[5][:]).then_inc(hT_ready, 1)
                if i == CH - 1:
                    exp_logits(0)
                if i < CH:
                    if i == 0:
                        act.wait_ge(ew_in, 32)
                    for e in range(EA // CH * i, EA // CH * (i + 1)):
                        last = a.activation(w1_sb[:, e, :], w1_sb[:, e, :], ACT.Copy, scale=rmsT[:, e:e + 1])
                    last.then_inc(w1_ready, 1)
            exp_logits(1)
            for c in range(CH):
                for e in range(ES * HC):
                    act.wait_ge(sh_ps, 4 * c + e + 1)
                    if c >= 2 and e == 0:
                        act.wait_ge(so_ps, c - 1)
                    a.activation(ysh[:, c % 2, e], bank[e][:], ACT.Silu).then_inc(sh_ready, 1)
            a.nop().then_inc(xt_ready, 2)
            a.nop().then_inc(act_ready, 2)

            def copy_xsT(n, z):
                act.wait_ge(xt_ps, n + 1)
                act.wait_ge(hid_ps, n + 1)
                a.copy(xsT[:, z % 3], bank[z % 2][:, 0:P]).then_inc(xt_ready, 1)

            def silu(n, z):
                act.wait_ge(hid_ps, n + 4)
                act.wait_ge(yb_ps, n + 1)
                a.activation(act_sb[:, z % 3], bank[2 + z % 2][:, 0:HID], ACT.Silu).then_inc(act_ready, 1)

            copy_xsT(0, 0)
            copy_xsT(1, 1)
            copy_xsT(2, 2)
            silu(0, 0)
            silu(1, 1)
            for z in range(STEP):
                copy_xsT(z + 3, z + 3)
                silu(z + 2, z + 2)
            with act.Fori(0, LOOPS) as it:
                for z in range(UNROLL):
                    copy_xsT(it * UNROLL + (STEP + z + 3), z + 3)
                    silu(it * UNROLL + (STEP + z + 2), z + 2)

        @block.tensor
        def _(pe):
            mm, tr = nc.tensor.matmul, nc.tensor.transpose
            pe.wait_ge(const_ready, 1)
            pe.wait_ge(w_in, 48)
            for c in range(4):
                last = tr(bank[4][:, P * c:P * c + P], wnat[:, c, :], ident[:])
            pe.wait_ge(rms_in, 48)
            tr(bank[5][:, 0:EA], rmsn[:], ident[0:EA, 0:EA]).then_inc(wT_ps, 1)

            def turn_xn(i):
                if i % 2 == 0:
                    pe.wait_ge(*((xn_ready, i // 2 + 1) if i < 6 else (xn_act, 1)))
                if i >= 2:
                    pe.wait_ge(xnT_ready, i - 1)
                for c in range(4):
                    last = mm(bank[i % 2][:, P * c:P * c + P], xn[:, 4 * i + c, :], exch[:], start=True, stop=True)
                last.then_inc(xnT_ps, 1)

            def project_in(i):
                pe.wait_ge(xnT_ready, i + 1)
                if i == 0:
                    pe.wait_ge(wT_ready, 1)
                if i >= 2:
                    pe.wait_ge(u_ready, i - 1)
                for c in range(4):
                    last = mm(bank[2 + i % 2][:, P * c:P * c + P], xnT[:, i % 2, P * c:P * c + P], wT[:, 0, :],
                              start=True, stop=True)
                last.then_inc(u_ps, 1)

            def turn_tables(g):
                pe.wait_ge(v1_dve, g + 1)
                pe.wait_ge(v1_pool, g + 1)
                for i in range(4 * g, 4 * g + 4):
                    if i >= 3:
                        pe.wait_ge(v2_act, i - 2)
                    else:
                        pe.wait_ge(rms_ready, 1)
                    for q in range(4):
                        p = 4 * i + q
                        last = tr(bank[4 + i % 3][:, P * q:P * q + P], v1[:, 2 * p:2 * p + 2].rearrange("p h r n -> p (h r n)"), ident[:])
                    last.then_inc(v2_ps, 1)

            def impulse(g):
                if g == 0:
                    pe.wait_ge(cbig_ready, 1)
                pe.wait_ge(v2_act, 4 * g + 4)
                for j in range(PG):
                    last = mm(bank[7][HG * g:HG * g + HG, 0:P], cbig[:, g, 32 * j:32 * j + 32], v2[:, PG * g + j, :],
                              start=(j == 0), stop=(j == PG - 1))
                last.then_inc(k_ps, 1)

            turn_tables(0)
            turn_xn(0)
            turn_xn(1)
            project_in(0)
            project_in(1)
            pe.wait_ge(q_ready, 1)
            pe.wait_ge(xnT_ready, 2)
            pe.wait_ge(u_ready, 2)
            tr(bank[0][:, 0:P], q1[:].rearrange("p q n -> p (q n)"), ident[:])
            tr(bank[3][0:64, 0:P], q2[:].rearrange("p q n -> p (q n)"), ident[:]).then_inc(q_ps, 1)
            turn_tables(1)
            impulse(0)
            turn_tables(2)
            impulse(1)
            pe.wait_ge(lw_act, 1)
            turn_xn(2)
            turn_xn(3)
            project_in(2)
            project_in(3)
            turn_tables(3)
            impulse(2)
            impulse(3)
            turn_xn(4)
            for i in range(4, 8):
                if i < 7:
                    turn_xn(i + 1)
                project_in(i)

            pe.wait_ge(u_ready, 8)
            pe.wait_ge(lw_act, 1)
            pe.wait_ge(k_ready, NG)
            for i in range(8):
                for q in range(8):
                    p = 8 * i + q
                    last = mm(bank[i][:, 64 * q:64 * q + 64], v1[:, 2 * p:2 * p + 2].rearrange("p h r n -> p (h r n)"),
                              u[:, 2 * p:2 * p + 2, :].rearrange("p h c -> p (h c)"), start=True, stop=True)
                last.then_inc(b_ps, 1)

            for g in T0_ORDER:
                pe.wait_ge(hank_in[g], 16)
                for q in range(HG):
                    h = HG * g + q
                    if h % 16 == 0:
                        pe.wait_ge(b_act, h // 16 + 1)
                        pe.wait_ge(b_dve, h // 16 + 1)
                    k, x_ = h % 4, h // 4
                    last = mm(bank[x_ // 4][32 * k:32 * k + 32, P * (x_ % 4):P * (x_ % 4) + P], u[:, h, :], hank[g][:, q, :],
                              start=(x_ % 4 == 0), stop=False, skip_group_check=True)
                last.then_inc(t0_ps, 1)
            pe.wait_ge(sbd_act, 1)
            pe.wait_ge(sbd_dve, 1)
            for p in range(NPAIR):
                m, x_ = p % 2, p // 2
                last = mm(bank[x_ // 4][64 * m:64 * m + 64, P * (x_ % 4):P * (x_ % 4) + P],
                          s_bd[:, p].rearrange("p e c -> p (e c)"), v2[:, p, :],
                          start=False, stop=(x_ % 4 == 3), skip_group_check=True)
                if p % 8 == 7:
                    last.then_inc(y_ps, 1)
            for i in range(8):
                pe.wait_ge(yq_ready, i + 1)
                for q in range(4):
                    last = tr(bank[i][:, P * q:P * q + P], yq[:, 512 * i + P * q:512 * i + P * q + P], ident[:])
                last.then_inc(yq_ps, 1)

            pe.wait_ge(y_ready, 4)
            pe.wait_ge(y_dve, 4)

            def turn_y(c):
                if c >= 2:
                    pe.wait_ge(yT_ready, c - 1)
                for q in range(4):
                    last = tr(bank[c % 2][:, P * q:P * q + P], y_sb[:, 4 * c + q, :], ident[:])
                last.then_inc(yT_ps, 1)

            def glu_products(c):
                pe.wait_ge(yT_ready, c + 1)
                if c:
                    pe.wait_ge(aT_ready, c)
                mm(bank[2][:], wT[:, 1, :], yT[:, c % 2], start=True, stop=True)
                mm(bank[3][:], wT[:, 2, :], yT[:, c % 2], start=True, stop=True).then_inc(ag_ps, 1)

            def project_out(c):
                pe.wait_ge(aT_ready, c + 1)
                if c:
                    pe.wait_ge(x2_ready, c)
                for q in range(4):
                    last = mm(bank[4][:, P * q:P * q + P], aT[:, c % 2, P * q:P * q + P], wT[:, 3, :], start=True, stop=True)
                last.then_inc(o_ps, 1)

            def turn_h0(c):
                pe.wait_ge(h0_ready, c + 1)
                if c:
                    pe.wait_ge(hT_ready, c)
                for q in range(4):
                    last = tr(bank[5][:, P * q:P * q + P], hx[:, 4 * c + q, 0, 0:D], ident[:])
                last.then_inc(hT_ps, 1)

            def route(c):
                pe.wait_ge(hT_ready, c + 1)
                b = int(c >= BATCH[0][1])
                for i in range(4 * c, 4 * c + 4):
                    at = E * (i - 4 * BATCH[b][0])
                    last = mm(bank[6 + b][:, at:at + E], h0T[:, P * i:P * i + P], rw[:], start=True, stop=True)
                if c + 1 == BATCH[b][1]:
                    last.then_inc(r_ps, 1)

            def count_routes(b):
                lo, hi = 4 * E * BATCH[b][0], 4 * E * BATCH[b][1]
                pe.wait_ge(m_ready, b + 1)
                if b:
                    pe.wait_ge(pos_ready, b)
                mm(bank[6 + b][:, 0:hi - lo], ones[:], rt[5][:, lo:hi], start=True, stop=True)
                mm(bank[6][:, RANKS:RANKS + hi - lo], upper[:], rt[5][:, lo:hi], start=True, stop=True).then_inc(rank_ps, 1)

            turn_y(0)
            for i in range(CH + 4):
                if i < CH:
                    glu_products(i)
                if i + 1 < CH:
                    turn_y(i + 1)
                if 0 <= i - 1 < CH:
                    project_out(i - 1)
                if i == CH - 1:
                    count_routes(0)
                if 0 <= i - 3 < CH:
                    turn_h0(i - 3)
                if 0 <= i - 4 < CH:
                    route(i - 4)

            def shared_in(c):
                for e in range(ES * HC):
                    if c:
                        pe.wait_ge(sh_ready, 4 * c - 4 + e + 1)
                    mm(bank[e][:], w1_sb[:, E + e // HC, P * (e % HC):P * (e % HC) + P], h0T[:, 512 * c:512 * c + 512],
                       start=True, stop=True).then_inc(sh_ps, 1)

            def shared_out(c):
                pe.wait_ge(sh_ready, 4 * c + 4)
                if c == 0:
                    pe.wait_ge(ew2_in, 16 * 2 * HC)
                    pe.wait_ge(x2_ready, CH)
                if c >= 2:
                    pe.wait_ge(so_added, c - 1)
                for q in range(4):
                    for e in range(ES * HC):
                        last = mm(bank[4 + c % 2][:, P * q:P * q + P], ysh[:, c % 2, e, P * q:P * q + P],
                                  w2_sb[:, E + e // HC, e % HC, :], start=(e == 0), stop=(e == ES * HC - 1))
                last.then_inc(so_ps, 1)

            pe.wait_ge(w1_ready, CH)
            shared_in(0)
            count_routes(1)
            shared_in(1)
            shared_out(0)
            for c in range(1, CH):
                if c + 1 < CH:
                    shared_in(c + 1)
                shared_out(c)

            pe.nop().then_inc(hid_ps, 3)
            pe.nop().then_inc(yb_ps, 3)
            pe.wait_ge(sh_ready, 4 * CH)
            pe.wait_ge(so_added, CH)

            def turn_rows(n, loads, z):
                pe.wait_ge(xs_in[z % UNROLL], loads)
                pe.wait_ge(xt_ready, n + 1)
                tr(bank[z % 2][:, 0:P], xs[:, z % UNROLL, 0:D], ident[:]).then_inc(xt_ps, 1)

            def first_matrix(n, z):
                pe.wait_ge(xt_ready, n + 3)
                pe.wait_ge(wc_ready, n + 1)
                pe.wait_ge(act_ready, n + 1)
                for c in range(HC):
                    last = mm(bank[2 + z % 2][:, P * c:P * c + P], wc[:, z % STEP, 1, P * c:P * c + P], xsT[:, z % 3],
                              start=True, stop=True)
                last.then_inc(hid_ps, 1)

            def second_matrix(n, z):
                pe.wait_ge(act_ready, n + 3)
                pe.wait_ge(yb_ready, n + 1)
                for c in range(HC):
                    last = mm(bank[4 + z % 2][:, 0:D], act_sb[:, z % 3, P * c:P * c + P], wc[:, z % STEP, 0, P * c:P * c + P],
                              start=(c == 0), stop=(c == HC - 1))
                last.then_inc(yb_ps, 1)

            turn_rows(0, 16, 0)
            turn_rows(1, 16, 1)
            turn_rows(2, 16, 2)
            first_matrix(0, 0)
            first_matrix(1, 1)
            for z in range(STEP):
                turn_rows(z + 3, 16, z + 3)
                first_matrix(z + 2, z + 2)
                second_matrix(z, z)
            with pe.Fori(0, LOOPS) as it:
                for z in range(UNROLL):
                    turn_rows(it * UNROLL + (STEP + z + 3), it * 16 + 16 * (1 + (STEP + z + 3) // UNROLL), STEP + z + 3)
                    first_matrix(it * UNROLL + (STEP + z + 2), z + 2)
                    second_matrix(it * UNROLL + (STEP + z), z)


_INS = ['L0_attn_x', 'L0_attn_in_W', 'L0_attn_in_b', 'L0_attn_log_dt', 'L0_attn_C', 'L0_attn_log_A_real',
        'L0_attn_A_imag', 'L0_attn_D_skip', 'L0_attn_glu_W', 'L0_attn_glu_b', 'L0_attn_out_W', 'L0_attn_out_b',
        'L0_ffn_router_w', 'L0_ffn_rms_w', 'L0_ffn_w1', 'L0_ffn_w2', 'L0_ffn_rms_w_s', 'L0_ffn_w1_s', 'L0_ffn_w2_s']


def kernel(**inputs):
    import concourse.bacc as bacc
    from concourse.bass_utils import run_bass_kernel_spmd

    nc = bacc.Bacc("TRN2", target_bir_lowering=False, num_devices=1)
    arrays, args = {}, []
    for name in _INS:
        a = np.ascontiguousarray(inputs[name])
        arrays[f"in_{name}"] = a
        args.append(nc.dram_tensor(f"in_{name}", a.shape, mybir.dt.from_np(a.dtype), kind="ExternalInput").ap())
    out = nc.dram_tensor("out_x", (2, 2048, 128), F32, kind="ExternalOutput").ap()
    build_kernel(nc, *args, out)
    r = run_bass_kernel_spmd(nc, [arrays], core_ids=[0])
    return r.results[0]["out_x"]
```
